# Optimizing a Trainium2 kernel written in Bass

```python
import numpy as np
import jax
import jax.numpy as jnp

def _softmax(x, axis=-1):
    return jax.nn.softmax(x, axis=axis)

def _gelu(x):
    return jax.nn.gelu(x, approximate=True)

def _silu(x):
    return jax.nn.silu(x)

def _sigmoid(x):
    return jax.nn.sigmoid(x)

def _layernorm(x, axis=-1, eps=1e-05):
    m = jnp.mean(x, axis=axis, keepdims=True)
    v = jnp.var(x, axis=axis, keepdims=True)
    return (x - m) / jnp.sqrt(v + eps)

def _scatter_add(tgt, idx, src, axis=0):
    return tgt.at[idx].add(src)

def _segment_sum(src, seg, n):
    return jax.ops.segment_sum(src, seg, n)
kernel_name = 'mk_prb_d2_jaxref_r8_c9457d'

def setup_inputs(seed: int=0):
    np.random.seed(seed)
    _w = jnp.asarray

    def _L0_attn_setup():
        import jax, jax.numpy as jnp
        import numpy as np
        D_MODEL = 128
        N_HEADS = 16
        D_HEAD = 64
        BATCH = 4
        SEQ = 256
        NEG = -1000000000.0
        key = jax.random.key(seed)
        k1, k2, k3, k4, k5 = jax.random.split(key, 5)
        x = jax.random.normal(k1, (BATCH, SEQ, D_MODEL), dtype=jnp.float32)
        std = 0.02
        wq = jax.random.normal(k2, (N_HEADS, D_HEAD, D_MODEL), dtype=jnp.float32) * std
        wk = jax.random.normal(k3, (N_HEADS, D_HEAD, D_MODEL), dtype=jnp.float32) * std
        wv = jax.random.normal(k4, (N_HEADS, D_HEAD, D_MODEL), dtype=jnp.float32) * std
        wo = jax.random.normal(k5, (D_MODEL, N_HEADS * D_HEAD), dtype=jnp.float32) * std
        return {'x': x, 'wq': wq, 'wk': wk, 'wv': wv, 'wo': wo}
    _L0_attn_in = _L0_attn_setup()

    def _L0_ffn_setup():
        import jax, jax.numpy as jnp
        import numpy as np
        DIM = 128
        DEPTH = 6
        HEADS = 16
        DIM_HEAD = 64
        WINDOW = 32
        INNER = HEADS * DIM_HEAD
        DIM_INNER = int(DIM * 4 * 2 / 3)
        QK_SCALE = 8.0

        def shift_tokens(t):
            a, s = jnp.split(t, 2, -1)
            s = jnp.pad(s, ((0, 0), (1, 0), (0, 0)))[:, :-1]
            return jnp.concatenate([a, s], -1)

        def l2norm(t):
            return t / jnp.maximum(jnp.linalg.norm(t, axis=-1, keepdims=True), 1e-12)

        def rotate_half(x):
            x1, x2 = jnp.split(x, 2, -1)
            return jnp.concatenate([-x2, x1], -1)

        def rotary_tables(n):
            half = jnp.arange(0, DIM_HEAD, 2, dtype=jnp.float32)
            inv_freq = 1.0 / 10000.0 ** (half / DIM_HEAD)
            t = jnp.arange(n, dtype=jnp.float32)
            freqs = t[:, None] * inv_freq[None, :]
            freqs = jnp.concatenate([freqs, freqs], -1)
            base_scale = (half + 0.4 * DIM_HEAD) / (1.4 * DIM_HEAD)
            power = (t - n // 2) / (WINDOW // 2)
            scale = base_scale[None, :] ** power[:, None]
            scale = jnp.concatenate([scale, scale], -1)
            return (freqs, scale)

        def local_attention(q, k, v):
            b, h, n, d = q.shape
            w = WINDOW
            nw = n // w
            bq = q.reshape(b, h, nw, w, d)
            bk = k.reshape(b, h, nw, w, d)
            bv = v.reshape(b, h, nw, w, d)

            def look(t):
                p = jnp.pad(t, ((0, 0), (0, 0), (1, 0), (0, 0), (0, 0)))
                return jnp.concatenate([p[:, :, :nw], p[:, :, 1:]], axis=3)
            bk2, bv2 = (look(bk), look(bv))
            seq = jnp.arange(n).reshape(nw, w)
            seq_p = jnp.pad(seq, ((1, 0), (0, 0)), constant_values=-1)
            jt = jnp.concatenate([seq_p[:nw], seq_p[1:]], axis=1)
            it = seq[:, :, None]
            jb = jt[:, None, :]
            mask = (it < jb) | (it > jb + w) | (jb == -1)
            sim = jnp.einsum('bhwie,bhwje->bhwij', bq, bk2) * QK_SCALE
            sim = jnp.where(mask, -jnp.finfo(sim.dtype).max, sim)
            attn = jax.nn.softmax(sim, -1)
            out = jnp.einsum('bhwij,bhwje->bhwie', attn, bv2)
            return out.reshape(b, h, n, d)

        def attn_layer(x, Wqkv, qs, ksc, Wo):
            b, n, _ = x.shape
            qkv = x @ Wqkv
            q, k, v = jnp.split(qkv, 3, -1)
            sh = lambda t: t.reshape(b, n, HEADS, DIM_HEAD).transpose(0, 2, 1, 3)
            q, k, v = (sh(q), sh(k), sh(v))
            q = l2norm(q) * qs
            k = l2norm(k) * ksc
            freqs, scale = rotary_tables(n)
            cos, sin = (jnp.cos(freqs), jnp.sin(freqs))
            q = q * cos * scale + rotate_half(q) * sin * scale
            inv = 1.0 / scale
            k = k * cos * inv + rotate_half(k) * sin * inv
            out = local_attention(q, k, v)
            out = out.transpose(0, 2, 1, 3).reshape(b, n, INNER)
            return out @ Wo

        def ffn_layer(x, g, bln, W1, b1, W2, b2):
            mu = x.mean(-1, keepdims=True)
            var = ((x - mu) ** 2).mean(-1, keepdims=True)
            xn = (x - mu) / jnp.sqrt(var + 1e-05) * g + bln
            hg = xn @ W1 + b1
            a, gate = jnp.split(hg, 2, -1)
            return a * jax.nn.gelu(gate, approximate=False) @ W2 + b2
        key = jax.random.key(seed)
        ks = jax.random.split(key, 8)
        B, N = (2, 256)
        init = lambda k, shape: jax.random.normal(k, shape, jnp.float32) * 0.02
        return {'x': jax.random.normal(ks[0], (B, N, DIM), jnp.float32), 'Wqkv': init(ks[1], (DEPTH, DIM, 3 * INNER)), 'q_scale': jnp.ones((DEPTH, DIM_HEAD), jnp.float32), 'k_scale': jnp.ones((DEPTH, DIM_HEAD), jnp.float32), 'Wo': init(ks[2], (DEPTH, INNER, DIM)), 'ln_g': jnp.ones((DEPTH, DIM), jnp.float32), 'ln_b': jnp.zeros((DEPTH, DIM), jnp.float32), 'W1': init(ks[3], (DEPTH, DIM, 2 * DIM_INNER)), 'b1': jnp.zeros((DEPTH, 2 * DIM_INNER), jnp.float32), 'W2': init(ks[4], (DEPTH, DIM_INNER, DIM)), 'b2': jnp.zeros((DEPTH, DIM), jnp.float32)}
    _L0_ffn_in = _L0_ffn_setup()

    def _L1_attn_setup():
        import jax, jax.numpy as jnp
        import numpy as np
        DIM = 128
        HEADS = 16
        DIM_HEAD = 64
        SOFTCLAMP = 50.0

        def _rmsnorm(x, w):
            eps = jnp.finfo(x.dtype).eps
            var = jnp.mean(jnp.square(x), axis=-1, keepdims=True)
            return x * jax.lax.rsqrt(var + eps) * w

        def _head_rmsnorm(x, gamma):
            norm = jnp.linalg.norm(x, axis=-1, keepdims=True)
            normed = x / jnp.maximum(norm, 1e-12)
            scale = (gamma + 1.0) * DIM_HEAD ** 0.5
            return normed * scale[None, :, None, :]
        key = jax.random.key(seed)
        ks = jax.random.split(key, 7)
        b, n = (4, 256)
        di = HEADS * DIM_HEAD
        s = 0.02
        return {'tokens': jax.random.normal(ks[0], (b, n, DIM), dtype=jnp.float32), 'norm_w': jnp.ones((DIM,), dtype=jnp.float32), 'Wq': jax.random.normal(ks[1], (DIM, di), dtype=jnp.float32) * s, 'Wkv': jax.random.normal(ks[2], (DIM, 2 * di), dtype=jnp.float32) * s, 'Wo': jax.random.normal(ks[3], (di, DIM), dtype=jnp.float32) * s, 'q_gamma': jnp.zeros((HEADS, DIM_HEAD), dtype=jnp.float32), 'k_gamma': jnp.zeros((HEADS, DIM_HEAD), dtype=jnp.float32)}
    _L1_attn_in = _L1_attn_setup()

    def _L1_ffn_setup():
        import jax, jax.numpy as jnp
        import numpy as np
        B, S, D = (1, 256, 128)
        E, F = (16, 128)
        NG, TKG, K = (4, 2, 4)
        NSH = 2
        SCALE = 2.5
        STD = 0.02
        EPG = E // NG

        def _route(x_flat, router_w, bias):
            logits = x_flat.astype(jnp.float32) @ router_w.T
            scores = jax.nn.sigmoid(logits)
            s = scores + bias[None, :]
            sg = s.reshape(-1, NG, EPG)
            group_score = jax.lax.top_k(sg, 2)[0].sum(-1)
            gidx = jax.lax.top_k(group_score, TKG)[1]
            gmask = jnp.sum(jax.nn.one_hot(gidx, NG, dtype=jnp.float32), axis=1) > 0
            emask = jnp.repeat(gmask, EPG, axis=1)
            masked = jnp.where(emask, s, -1.0)
            topk_idx = jax.lax.top_k(masked, K)[1]
            tw = jnp.take_along_axis(scores, topk_idx, axis=1)
            tw = tw / (tw.sum(-1, keepdims=True) + 1e-20)
            tw = tw * SCALE
            return (topk_idx, tw)
        key = jax.random.key(seed)
        ks = jax.random.split(key, 8)
        return {'hidden_states': jax.random.normal(ks[0], (B, S, D), jnp.float32), 'router_w': jax.random.normal(ks[1], (E, D), jnp.float32) * STD, 'bias': jnp.zeros((E,), jnp.float32), 'gate_w': jax.random.normal(ks[2], (E, D, F), jnp.float32) * STD, 'up_w': jax.random.normal(ks[3], (E, D, F), jnp.float32) * STD, 'down_w': jax.random.normal(ks[4], (E, F, D), jnp.float32) * STD, 'sh_gate_w': jax.random.normal(ks[5], (D, NSH * F), jnp.float32) * STD, 'sh_up_w': jax.random.normal(ks[6], (D, NSH * F), jnp.float32) * STD, 'sh_down_w': jax.random.normal(ks[7], (NSH * F, D), jnp.float32) * STD}
    _L1_ffn_in = _L1_ffn_setup()
    _d = {'L0_attn_x': _L0_attn_in['x'], 'L0_attn_wq': _L0_attn_in['wq'], 'L0_attn_wk': _L0_attn_in['wk'], 'L0_attn_wv': _L0_attn_in['wv'], 'L0_attn_wo': _L0_attn_in['wo'], 'L0_ffn_Wqkv': _L0_ffn_in['Wqkv'], 'L0_ffn_q_scale': _L0_ffn_in['q_scale'], 'L0_ffn_k_scale': _L0_ffn_in['k_scale'], 'L0_ffn_Wo': _L0_ffn_in['Wo'], 'L0_ffn_ln_g': _L0_ffn_in['ln_g'], 'L0_ffn_ln_b': _L0_ffn_in['ln_b'], 'L0_ffn_W1': _L0_ffn_in['W1'], 'L0_ffn_b1': _L0_ffn_in['b1'], 'L0_ffn_W2': _L0_ffn_in['W2'], 'L0_ffn_b2': _L0_ffn_in['b2'], 'L1_attn_norm_w': _L1_attn_in['norm_w'], 'L1_attn_Wq': _L1_attn_in['Wq'], 'L1_attn_Wkv': _L1_attn_in['Wkv'], 'L1_attn_Wo': _L1_attn_in['Wo'], 'L1_attn_q_gamma': _L1_attn_in['q_gamma'], 'L1_attn_k_gamma': _L1_attn_in['k_gamma'], 'L1_ffn_router_w': _L1_ffn_in['router_w'], 'L1_ffn_bias': _L1_ffn_in['bias'], 'L1_ffn_gate_w': _L1_ffn_in['gate_w'], 'L1_ffn_up_w': _L1_ffn_in['up_w'], 'L1_ffn_down_w': _L1_ffn_in['down_w'], 'L1_ffn_sh_gate_w': _L1_ffn_in['sh_gate_w'], 'L1_ffn_sh_up_w': _L1_ffn_in['sh_up_w'], 'L1_ffn_sh_down_w': _L1_ffn_in['sh_down_w']}
    _x0 = _d['L0_attn_x']
    _d['L0_attn_x'] = jax.random.normal(jax.random.fold_in(jax.random.key(seed), 1), (2, 1024, 128), dtype=_x0.dtype)
    del _x0
    return _d

def reference(L0_attn_x, L0_attn_wq, L0_attn_wk, L0_attn_wv, L0_attn_wo, L0_ffn_Wqkv, L0_ffn_q_scale, L0_ffn_k_scale, L0_ffn_Wo, L0_ffn_ln_g, L0_ffn_ln_b, L0_ffn_W1, L0_ffn_b1, L0_ffn_W2, L0_ffn_b2, L1_attn_norm_w, L1_attn_Wq, L1_attn_Wkv, L1_attn_Wo, L1_attn_q_gamma, L1_attn_k_gamma, L1_ffn_router_w, L1_ffn_bias, L1_ffn_gate_w, L1_ffn_up_w, L1_ffn_down_w, L1_ffn_sh_gate_w, L1_ffn_sh_up_w, L1_ffn_sh_down_w):

    def _L0_attn_ref(x, wq, wk, wv, wo):
        import jax, jax.numpy as jnp
        import numpy as np
        D_MODEL = 128
        N_HEADS = 16
        D_HEAD = 64
        BATCH = 4
        SEQ = 256
        NEG = -1000000000.0
        b, s, _ = x.shape
        scale = jnp.sqrt(jnp.asarray(D_HEAD, x.dtype))
        q = jnp.einsum('bsd,hed->bhse', x, wq)
        k = jnp.einsum('bsd,hed->bhse', x, wk)
        v = jnp.einsum('bsd,hed->bhse', x, wv)
        scores = jnp.einsum('bhse,bhte->bhst', q, k) / scale
        causal_mask = jnp.triu(jnp.ones((s, s), dtype=bool), k=1)
        scores = jnp.where(causal_mask, jnp.asarray(NEG, scores.dtype), scores)
        weights = jax.nn.softmax(scores, axis=-1)
        heads = jnp.einsum('bhst,bhte->bhse', weights, v)
        concat = heads.transpose(0, 2, 1, 3).reshape(b, s, N_HEADS * D_HEAD)
        return concat @ wo.T

    def _L0_ffn_ref(x, Wqkv, q_scale, k_scale, Wo, ln_g, ln_b, W1, b1, W2, b2):
        import jax, jax.numpy as jnp
        import numpy as np
        DIM = 128
        DEPTH = 6
        HEADS = 16
        DIM_HEAD = 64
        WINDOW = 32
        INNER = HEADS * DIM_HEAD
        DIM_INNER = int(DIM * 4 * 2 / 3)
        QK_SCALE = 8.0

        def shift_tokens(t):
            a, s = jnp.split(t, 2, -1)
            s = jnp.pad(s, ((0, 0), (1, 0), (0, 0)))[:, :-1]
            return jnp.concatenate([a, s], -1)

        def l2norm(t):
            return t / jnp.maximum(jnp.linalg.norm(t, axis=-1, keepdims=True), 1e-12)

        def rotate_half(x):
            x1, x2 = jnp.split(x, 2, -1)
            return jnp.concatenate([-x2, x1], -1)

        def rotary_tables(n):
            half = jnp.arange(0, DIM_HEAD, 2, dtype=jnp.float32)
            inv_freq = 1.0 / 10000.0 ** (half / DIM_HEAD)
            t = jnp.arange(n, dtype=jnp.float32)
            freqs = t[:, None] * inv_freq[None, :]
            freqs = jnp.concatenate([freqs, freqs], -1)
            base_scale = (half + 0.4 * DIM_HEAD) / (1.4 * DIM_HEAD)
            power = (t - n // 2) / (WINDOW // 2)
            scale = base_scale[None, :] ** power[:, None]
            scale = jnp.concatenate([scale, scale], -1)
            return (freqs, scale)

        def local_attention(q, k, v):
            b, h, n, d = q.shape
            w = WINDOW
            nw = n // w
            bq = q.reshape(b, h, nw, w, d)
            bk = k.reshape(b, h, nw, w, d)
            bv = v.reshape(b, h, nw, w, d)

            def look(t):
                p = jnp.pad(t, ((0, 0), (0, 0), (1, 0), (0, 0), (0, 0)))
                return jnp.concatenate([p[:, :, :nw], p[:, :, 1:]], axis=3)
            bk2, bv2 = (look(bk), look(bv))
            seq = jnp.arange(n).reshape(nw, w)
            seq_p = jnp.pad(seq, ((1, 0), (0, 0)), constant_values=-1)
            jt = jnp.concatenate([seq_p[:nw], seq_p[1:]], axis=1)
            it = seq[:, :, None]
            jb = jt[:, None, :]
            mask = (it < jb) | (it > jb + w) | (jb == -1)
            sim = jnp.einsum('bhwie,bhwje->bhwij', bq, bk2) * QK_SCALE
            sim = jnp.where(mask, -jnp.finfo(sim.dtype).max, sim)
            attn = jax.nn.softmax(sim, -1)
            out = jnp.einsum('bhwij,bhwje->bhwie', attn, bv2)
            return out.reshape(b, h, n, d)

        def attn_layer(x, Wqkv, qs, ksc, Wo):
            b, n, _ = x.shape
            qkv = x @ Wqkv
            q, k, v = jnp.split(qkv, 3, -1)
            sh = lambda t: t.reshape(b, n, HEADS, DIM_HEAD).transpose(0, 2, 1, 3)
            q, k, v = (sh(q), sh(k), sh(v))
            q = l2norm(q) * qs
            k = l2norm(k) * ksc
            freqs, scale = rotary_tables(n)
            cos, sin = (jnp.cos(freqs), jnp.sin(freqs))
            q = q * cos * scale + rotate_half(q) * sin * scale
            inv = 1.0 / scale
            k = k * cos * inv + rotate_half(k) * sin * inv
            out = local_attention(q, k, v)
            out = out.transpose(0, 2, 1, 3).reshape(b, n, INNER)
            return out @ Wo

        def ffn_layer(x, g, bln, W1, b1, W2, b2):
            mu = x.mean(-1, keepdims=True)
            var = ((x - mu) ** 2).mean(-1, keepdims=True)
            xn = (x - mu) / jnp.sqrt(var + 1e-05) * g + bln
            hg = xn @ W1 + b1
            a, gate = jnp.split(hg, 2, -1)
            return a * jax.nn.gelu(gate, approximate=False) @ W2 + b2
        for i in range(DEPTH):
            x = attn_layer(shift_tokens(x), Wqkv[i], q_scale[i], k_scale[i], Wo[i]) + x
            x = ffn_layer(shift_tokens(x), ln_g[i], ln_b[i], W1[i], b1[i], W2[i], b2[i]) + x
        return x

    def _L1_attn_ref(tokens, norm_w, Wq, Wkv, Wo, q_gamma, k_gamma):
        import jax, jax.numpy as jnp
        import numpy as np
        DIM = 128
        HEADS = 16
        DIM_HEAD = 64
        SOFTCLAMP = 50.0

        def _rmsnorm(x, w):
            eps = jnp.finfo(x.dtype).eps
            var = jnp.mean(jnp.square(x), axis=-1, keepdims=True)
            return x * jax.lax.rsqrt(var + eps) * w

        def _head_rmsnorm(x, gamma):
            norm = jnp.linalg.norm(x, axis=-1, keepdims=True)
            normed = x / jnp.maximum(norm, 1e-12)
            scale = (gamma + 1.0) * DIM_HEAD ** 0.5
            return normed * scale[None, :, None, :]
        b, n, _ = tokens.shape
        x = _rmsnorm(tokens, norm_w)
        q = x @ Wq
        kv = x @ Wkv
        k, v = jnp.split(kv, 2, axis=-1)
        split = lambda t: t.reshape(b, n, HEADS, DIM_HEAD).transpose(0, 2, 1, 3)
        q, k, v = (split(q), split(k), split(v))
        q = _head_rmsnorm(q, q_gamma)
        k = _head_rmsnorm(k, k_gamma)
        sim = jnp.einsum('bhid,bhjd->bhij', q, k)
        sim = jnp.tanh(sim / SOFTCLAMP) * SOFTCLAMP
        sim = sim * DIM_HEAD ** (-0.5)
        attn = jax.nn.softmax(sim, axis=-1)
        out = jnp.einsum('bhij,bhjd->bhid', attn, v)
        out = out.transpose(0, 2, 1, 3).reshape(b, n, HEADS * DIM_HEAD)
        return out @ Wo

    def _L1_ffn_ref(hidden_states, router_w, bias, gate_w, up_w, down_w, sh_gate_w, sh_up_w, sh_down_w):
        import jax, jax.numpy as jnp
        import numpy as np
        B, S, D = (1, 256, 128)
        E, F = (16, 128)
        NG, TKG, K = (4, 2, 4)
        NSH = 2
        SCALE = 2.5
        STD = 0.02
        EPG = E // NG

        def _route(x_flat, router_w, bias):
            logits = x_flat.astype(jnp.float32) @ router_w.T
            scores = jax.nn.sigmoid(logits)
            s = scores + bias[None, :]
            sg = s.reshape(-1, NG, EPG)
            group_score = jax.lax.top_k(sg, 2)[0].sum(-1)
            gidx = jax.lax.top_k(group_score, TKG)[1]
            gmask = jnp.sum(jax.nn.one_hot(gidx, NG, dtype=jnp.float32), axis=1) > 0
            emask = jnp.repeat(gmask, EPG, axis=1)
            masked = jnp.where(emask, s, -1.0)
            topk_idx = jax.lax.top_k(masked, K)[1]
            tw = jnp.take_along_axis(scores, topk_idx, axis=1)
            tw = tw / (tw.sum(-1, keepdims=True) + 1e-20)
            tw = tw * SCALE
            return (topk_idx, tw)
        x = hidden_states.reshape(-1, D)
        topk_idx, tw = _route(x, router_w, bias)
        combine = (jax.nn.one_hot(topk_idx, E, dtype=tw.dtype) * tw[..., None]).sum(1)
        h = jnp.einsum('td,edf->etf', x, gate_w)
        u = jnp.einsum('td,edf->etf', x, up_w)
        y = jnp.einsum('etf,efd->etd', jax.nn.silu(h) * u, down_w)
        routed = jnp.einsum('etd,te->td', y, combine)
        sh = jax.nn.silu(x @ sh_gate_w) * (x @ sh_up_w) @ sh_down_w
        return (routed + sh).reshape(hidden_states.shape)
    x = L0_attn_x
    xn = _layernorm(x, axis=-1)
    x = x + _L0_attn_ref(xn, L0_attn_wq, L0_attn_wk, L0_attn_wv, L0_attn_wo) + _L0_ffn_ref(xn, L0_ffn_Wqkv, L0_ffn_q_scale, L0_ffn_k_scale, L0_ffn_Wo, L0_ffn_ln_g, L0_ffn_ln_b, L0_ffn_W1, L0_ffn_b1, L0_ffn_W2, L0_ffn_b2)
    xn = _layernorm(x, axis=-1)
    x = x + _L1_attn_ref(xn, L1_attn_norm_w, L1_attn_Wq, L1_attn_Wkv, L1_attn_Wo, L1_attn_q_gamma, L1_attn_k_gamma) + _L1_ffn_ref(xn, L1_ffn_router_w, L1_ffn_bias, L1_ffn_gate_w, L1_ffn_up_w, L1_ffn_down_w, L1_ffn_sh_gate_w, L1_ffn_sh_up_w, L1_ffn_sh_down_w)
    return x

_drawn_inputs = setup_inputs


def setup_inputs(seed=0):
    import zlib

    import numpy as np

    out = dict(_drawn_inputs(seed))
    spreads = {'L0_ffn_q_scale': (1.0, 0.6),
     'L0_ffn_k_scale': (1.0, 0.6),
     'L0_ffn_ln_g': (1.0, 0.6),
     'L0_ffn_ln_b': (0.0, 0.8),
     'L0_ffn_b1': (0.0, 0.8),
     'L0_ffn_b2': (0.0, 0.1),
     'L1_attn_norm_w': (1.0, 0.6),
     'L1_attn_q_gamma': (0.0, 0.8),
     'L1_attn_k_gamma': (0.0, 0.8),
     'L1_ffn_bias': (0.0, 0.8)}
    factors = {'L0_attn_wq': 8.0,
     'L0_attn_wk': 8.0,
     'L0_attn_wv': 8.0,
     'L0_attn_wo': 8.0,
     'L0_ffn_W1': 3.64,
     'L0_ffn_W2': 3.572,
     'L1_attn_Wq': 7.753,
     'L1_attn_Wkv': 4.904,
     'L1_attn_Wo': 4.968,
     'L1_ffn_router_w': 8.0,
     'L1_ffn_gate_w': 8.0,
     'L1_ffn_up_w': 8.0,
     'L1_ffn_down_w': 8.0,
     'L1_ffn_sh_gate_w': 8.0,
     'L1_ffn_sh_up_w': 8.0,
     'L1_ffn_sh_down_w': 8.0}
    for name, (base, spread) in spreads.items():
        noise = np.random.default_rng([zlib.crc32(name.encode()), seed]).standard_normal(out[name].shape)
        drawn = base * np.exp(spread * noise) if base else spread * noise
        out[name] = jnp.asarray(drawn.astype(out[name].dtype))
    for name, factor in factors.items():
        out[name] = (out[name] * factor).astype(out[name].dtype)
    return out
```

```python
from contextlib import ExitStack

import numpy as np
import concourse.bass as bass
from concourse import mybir
from concourse.alu_op_type import AluOpType as ALU

F32 = mybir.dt.float32
BF16 = mybir.dt.bfloat16
ACT = mybir.ActivationFunctionType
AX = mybir.AxisListType

P = 128
B, S, D = 2, 1024, 128
N = B * S
NT = N // P
H, DH = 16, 64
PAIRS = H // 2
LAYERS = 6
WIN = 32
FFN_IN = int(D * 4 * 2 / 3)
FFN_PARTS = [(i * P, min(P, FFN_IN - i * P)) for i in range(-(-FFN_IN // P))]
NF = len(FFN_PARTS)
CH = 512
NCH = N // CH
E, F = 16, 128
NE = E + 2
GROUPS, TOP_GROUPS, TOP_K, ROUTE_SCALE = 4, 2, 4, 2.5
LN_EPS = 1e-5
RMS_EPS = float(np.finfo(np.float32).eps)
NEG = -1e30
QK_SCALE = 8.0
SOFTCLAMP = 50.0
BANK = 512
START = 1


def spread(ap, axis, n):
    a = ap.unsqueeze(axis)
    shape = list(a.shape)
    shape[axis] = n
    return a.broadcast_to(shape)


class Chain:

    def __init__(self, engine, sem, start=0):
        self.engine, self.sem, self.start, self.count = engine, sem, start, 0

    def link(self, instruction):
        instruction.then_inc(self.sem, 1)
        self.count += 1
        self.engine.wait_ge(self.sem, self.start + self.count)


def start_semaphores(nc, m, sems):
    with nc.Block() as block:
        @block.gpsimd
        def _(pool):
            for i, sem in enumerate(sems):
                nc.gpsimd.memset(m.scratch[:, i:i + 1], 0.0).then_inc(sem, START)


class Memory:
    pass


def tensors(ctx, nc, prefix):
    def sb(name, shape, dt=F32):
        return ctx.enter_context(nc.sbuf_tensor(prefix + name, shape, dt))

    def ps(name, shape, dt=F32):
        return ctx.enter_context(nc.psum_tensor(prefix + name, shape, dt))

    def sem(name):
        return ctx.enter_context(nc.semaphore(prefix + name))

    return sb, ps, sem


def norm_statistics(nc, dve, link, x, stats, mv, count):
    for t in range(count):
        last = nc.vector.bn_stats(stats[:, t, :], x[:, t, :])
    link(last)
    for t in range(count):
        last = nc.vector.bn_aggr(mv[:, t, :], stats[:, t, :])
    link(last)


def load_and_norm(nc, m, d):
    with ExitStack() as ctx:
        sb, ps, sem = tensors(ctx, nc, "n0_")
        stats = sb("stats", [P, NT, 6])
        mv = sb("mv", [P, NT, 2])
        veps = sb("veps", [P, NT])
        rstd = sb("rstd", [P, NT])
        xn = sb("xn", [P, NT, D])
        causal = sb("causal", [P, P])
        band = sb("band", [P, NT, 2 * WIN])
        psT = ps("psT", [P, 4, BANK])
        x_in, const_in, pow_in, ready, dchain, rstd_ready, xn_ready, xnT_ps = map(sem, (
            "x_in", "const_in", "pow_in", "ready", "dchain", "rstd_ready", "xn_ready", "xnT_ps"))
        xT_ready, zeros = sem("xT_ready"), sem("zeros")
        block = ctx.enter_context(nc.Block())

        @block.sync
        def _(sp):
            sp.dma_start(m.x[:, :, :], d["x"].rearrange("(t p) d -> p t d", p=P)).then_inc(x_in, 16)
            sp.dma_start(m.ident[:, :], d["ident"]).then_inc(const_in, 16)
            sp.dma_start(causal[:, :], d["causal"]).then_inc(const_in, 16)
            sp.dma_start(band[:, :, :], d["band"]).then_inc(const_in, 16)
            sp.dma_start(m.keep[:, :], d["keep"].partition_broadcast(P)).then_inc(const_in, 16)
            sp.dma_start(m.rot_base[:, :, :, :], d["rot_base"]).then_inc(const_in, 16)
            sp.dma_start(m.rot_scale[:, :, :], d["rot_scale"][0].partition_broadcast(P)).then_inc(const_in, 16)
            sp.wait_ge(const_in, 6 * 16)
            sp.wait_ge(x_in, 16)

        @block.gpsimd
        def _(pool):
            nc.gpsimd.memset(m.minus_half[:, :], -0.5).then_inc(ready, 1)
            nc.gpsimd.memset(m.ones[:, :], 1.0)
            nc.gpsimd.memset(m.xa[:, 0:1], 0.0)
            nc.gpsimd.memset(m.xa[:, 1 + N:], 0.0)
            nc.gpsimd.memset(m.xb[:, 0:1], 0.0)
            nc.gpsimd.memset(m.branchT[:, :], 0.0).then_inc(zeros, 1)
            pool.wait_ge(const_in, 6 * 16)
            for b in range(B):
                nc.gpsimd.tensor_tensor(m.rot[:, b * 8:b * 8 + 8, :, :], m.rot_base[:, :, :, :],
                                        spread(m.rot_scale[:, :, :], 1, 8), ALU.mult).then_inc(zeros, 1)
            pool.wait_ge(dchain, 3)
            pool.wait_ge(ready, 1)
            nc.gpsimd.tensor_tensor(rstd[:, :], veps[:, :], m.minus_half[:, 0:NT], ALU.pow).then_inc(rstd_ready, 1)

        @block.vector
        def _(dve):
            chain = Chain(dve, dchain)
            dve.wait_ge(x_in, 16)
            norm_statistics(nc, dve, chain.link, m.x, stats, mv, NT)
            chain.link(nc.vector.tensor_scalar(veps[:, :], mv[:, :, 1], LN_EPS, None, ALU.add))
            dve.wait_ge(rstd_ready, 1)
            for t in range(NT):
                nc.vector.tensor_scalar(xn[:, t, :], m.x[:, t, :], mv[:, t, 0:1], rstd[:, t:t + 1],
                                        ALU.subtract, ALU.mult).then_inc(xn_ready, 1)

        @block.tensor
        def _(pe):
            pe.wait_ge(const_in, 6 * 16)
            for t in range(NT):
                pe.wait_ge(xn_ready, t + 1)
                nc.tensor.transpose(psT[:, t // 4, (t % 4) * P:(t % 4 + 1) * P], xn[:, t, :],
                                    m.ident[:, :]).then_inc(xnT_ps, 1)

        @block.scalar
        def _(act):
            act.wait_ge(const_in, 6 * 16)
            nc.scalar.activation(m.identb[:, :], m.ident[:, :], ACT.Copy).then_inc(xT_ready, 1)
            nc.scalar.activation(m.causal[:, :], causal[:, :], ACT.Copy).then_inc(xT_ready, 1)
            nc.scalar.activation(m.band[:, :, :], band[:, :, :], ACT.Copy).then_inc(xT_ready, 1)
            for c in range(NCH):
                act.wait_ge(xnT_ps, 4 * (c + 1))
                nc.scalar.activation(m.xa[:, 1 + c * CH:1 + (c + 1) * CH], psT[:, c, :], ACT.Copy)\
                    .then_inc(xT_ready, 1)
                nc.scalar.activation(m.xnT[:, c * CH:(c + 1) * CH], psT[:, c, :], ACT.Copy)\
                    .then_inc(xT_ready, 1)


def causal_attention(nc, m, d):
    TB = S // P
    STEPS = [(b, qi, e) for b in range(B) for qi in range(TB) for e in range(2)]
    NS = len(STEPS)
    PER_CHUNK = 8
    CHUNKS = NS // PER_CHUNK
    groups = []
    for s, (b, qi, e) in enumerate(STEPS):
        groups += [(s, k, min(4, qi + 1 - k)) for k in range(0, qi + 1, 4)]
    NG = len(groups)
    first_group = [next(r for r, g in enumerate(groups) if g[0] == s) for s in range(NS)] + [NG]

    with ExitStack() as ctx:
        sb, ps, sem = tensors(ctx, nc, "a0_")
        w = sb("w", [P, 3, P])
        wo = sb("wo", [P, D])
        QT = sb("QT", [P, N])
        KT = sb("KT", [P, N])
        V = sb("V", [P, NT, P])
        prob = sb("prob", [P, 4, S])
        probT = sb("probT", [P, 2, 2, TB, CH])
        OT = sb("OT", [P, CH])
        nmax = sb("nmax", [P, 4])
        rsum = sb("rsum", [P, 4])
        rinv = sb("rinv", [P, 4])
        psS = ps("psS", [P, 2, S])
        psT = ps("psT", [P, 2, BANK])
        psO = ps("psO", [P, BANK])
        psW = ps("psW", [P, BANK])
        names = ("w_in wo_in proj_ps q_ready k_ready v_ready s_ps max_done exp_done dchain norm_done t_ps "
                 "ev_act ev_dve pv_ps ot_ready wo_ps acc_done").split()
        (w_in, wo_in, proj_ps, q_ready, k_ready, v_ready, s_ps, max_done, exp_done, dchain, norm_done, t_ps,
         ev_act, ev_dve, pv_ps, ot_ready, wo_ps, acc_done) = sems = [sem(name) for name in names]
        start_semaphores(nc, m, sems)
        block = ctx.enter_context(nc.Block())

        def bank(n):
            return psS[:, (n % 4) // 2, ((n % 4) % 2) * BANK:((n % 4) % 2 + 1) * BANK]

        @block.sync
        def _(sp):
            with sp.Fori(0, PAIRS) as g:
                sp.wait_ge(proj_ps, START + g * 12)
                sp.dma_start(w[:, :, :], d["a_wqkv"][bass.ds(g, 1)].rearrange("g d x f -> (g d) x f")).then_inc(w_in, 16)
                sp.wait_ge(wo_ps, START + g * CHUNKS)
                sp.dma_start(wo[:, :], d["a_wo"][bass.ds(g, 1)].rearrange("g f d -> (g f) d")).then_inc(wo_in, 16)

        @block.tensor
        def _(pe):
            def scores(g, s):
                b, qi, e = STEPS[s]
                if s >= 2:
                    pe.wait_ge(exp_done, START + g * NS + s - 1)
                keys = (qi + 1) * P
                h = slice(64 * e, 64 * e + 64)
                for k in range(0, keys, BANK):
                    n = min(BANK, keys - k)
                    diagonal = k + n == keys
                    last = nc.tensor.matmul(psS[:, e, k:k + n], QT[h, b * S + qi * P:b * S + (qi + 1) * P],
                                            KT[h, b * S + k:b * S + k + n], start=True, stop=not diagonal)
                    if diagonal:
                        last = nc.tensor.matmul(psS[:, e, keys - P:keys], m.identb[:, :], m.causal[:, :],
                                                start=False, stop=True)
                last.then_inc(s_ps, 1)

            def transposes(g, s):
                pe.wait_ge(norm_done, START + g * NS + s + 1)
                for r in range(first_group[s], first_group[s + 1]):
                    _, k0, n = groups[r]
                    pe.wait_ge(ev_act if r % 2 == 0 else ev_dve, START + g * (NG // 2) + r // 2)
                    for j in range(n):
                        last = nc.tensor.transpose(psT[:, r % 2, j * P:(j + 1) * P],
                                                   prob[:, s % 4, (k0 + j) * P:(k0 + j + 1) * P], m.ident[:, :])
                    last.then_inc(t_ps, 1)

            def values(g, c):
                b, qc = c // 2, c % 2
                done = first_group[PER_CHUNK * (c + 1)]
                pe.wait_ge(ev_act, START + g * (NG // 2) + (done + 1) // 2)
                pe.wait_ge(ev_dve, START + g * (NG // 2) + done // 2)
                pe.wait_ge(ot_ready, START + g * CHUNKS + c)
                kts = 4 * (qc + 1)
                for kt in range(kts):
                    r0 = max(0, kt - 4 * qc) * P
                    for e in range(2):
                        last = nc.tensor.matmul(psO[64 * e:64 * e + 64, r0:CH], V[:, b * TB + kt, 64 * e:64 * e + 64],
                                                probT[:, c % 2, e, kt, r0:CH], start=kt == 0, stop=kt == kts - 1)
                last.then_inc(pv_ps, 1)

            def project(g, c):
                pe.wait_ge(ot_ready, START + g * CHUNKS + c + 1)
                pe.wait_ge(acc_done, START + g * CHUNKS + c)
                if c == 0:
                    pe.wait_ge(wo_in, START + (g + 1) * 16)
                nc.tensor.matmul(psW[:, :], wo[:, :], OT[:, :], start=True, stop=True).then_inc(wo_ps, 1)

            with pe.Fori(0, PAIRS) as g:
                pe.wait_ge(w_in, START + (g + 1) * 16)
                pe.wait_ge(exp_done, START + g * NS)
                for i in range(NCH):
                    for x in range(3):
                        n = 3 * i + x
                        if n >= 4:
                            who = (q_ready, k_ready, v_ready)[(n - 4) % 3]
                            pe.wait_ge(who, START + g * NCH + (n - 4) // 3 + 1)
                        if x < 2:
                            last = nc.tensor.matmul(bank(n), w[:, x, :], m.xnT[:, i * CH:(i + 1) * CH],
                                                    start=True, stop=True)
                        else:
                            for j in range(4):
                                last = nc.tensor.matmul(bank(n)[:, j * P:(j + 1) * P],
                                                        m.xnT[:, i * CH + j * P:i * CH + (j + 1) * P], w[:, 2, :],
                                                        start=True, stop=True)
                        last.then_inc(proj_ps, 1)
                for ready in (q_ready, k_ready, v_ready):
                    pe.wait_ge(ready, START + (g + 1) * NCH)
                scores(g, 0)
                scores(g, 1)
                for s in range(NS + 1):
                    if s + 2 < NS:
                        scores(g, s + 2)
                    if s >= 1:
                        transposes(g, s - 1)
                    if s % PER_CHUNK == 3 and s > PER_CHUNK:
                        values(g, s // PER_CHUNK - 1)
                    if s % PER_CHUNK == 5 and s > PER_CHUNK:
                        project(g, s // PER_CHUNK - 1)
                values(g, CHUNKS - 1)
                project(g, CHUNKS - 1)

        def copy_out(engine, g, r, copy, done):
            s, k0, n = groups[r]
            b, qi, e = STEPS[s]
            c = s // PER_CHUNK
            engine.wait_ge(t_ps, START + g * NG + r + 1)
            if c >= 2:
                engine.wait_ge(pv_ps, START + g * CHUNKS + c - 1)
            copy(probT[:, c % 2, e, k0:k0 + n, (qi % 4) * P:(qi % 4 + 1) * P],
                 psT[:, r % 2, 0:n * P].rearrange("p (k q) -> p k q", q=P)).then_inc(done, 1)

        @block.scalar
        def _(act):
            def copy(out, in_):
                return nc.scalar.activation(out, in_, ACT.Copy)

            def heads_out(g, c):
                act.wait_ge(pv_ps, START + g * CHUNKS + c + 1)
                act.wait_ge(wo_ps, START + g * CHUNKS + c)
                nc.scalar.activation(OT[:, :], psO[:, :], ACT.Copy).then_inc(ot_ready, 1)

            with act.Fori(0, PAIRS) as g:
                for i in range(NCH):
                    act.wait_ge(proj_ps, START + g * 12 + 3 * i + 1)
                    nc.scalar.activation(QT[:, i * CH:(i + 1) * CH], bank(3 * i), ACT.Copy, scale=DH ** -0.5)\
                        .then_inc(q_ready, 1)
                    act.wait_ge(proj_ps, START + g * 12 + 3 * i + 3)
                    nc.scalar.activation(V[:, 4 * i:4 * i + 4, :], bank(3 * i + 2).rearrange("p (t f) -> p t f", f=P),
                                         ACT.Copy).then_inc(v_ready, 1)
                for s in range(NS + 3):
                    if s % PER_CHUNK == 6 and s > PER_CHUNK:
                        heads_out(g, s // PER_CHUNK - 1)
                    if s >= 3:
                        for r in range(first_group[s - 3], first_group[s - 2]):
                            if r % 2 == 0:
                                copy_out(act, g, r, copy, ev_act)
                    if s < NS:
                        b, qi, e = STEPS[s]
                        keys = (qi + 1) * P
                        act.wait_ge(max_done, START + g * NS + s + 1)
                        nc.scalar.activation(prob[:, s % 4, 0:keys], psS[:, e, 0:keys], ACT.Exp,
                                             bias=nmax[:, s % 4:s % 4 + 1],
                                             accum_out=rsum[:, s % 4:s % 4 + 1]).then_inc(exp_done, 1)
                heads_out(g, CHUNKS - 1)

        @block.vector
        def _(dve):
            def add_out(g, c):
                b, qc = c // 2, c % 2
                dve.wait_ge(wo_ps, START + g * CHUNKS + c + 1)
                cols = slice(b * S + qc * CH, b * S + (qc + 1) * CH)
                nc.vector.tensor_tensor(m.branchT[:, cols], m.branchT[:, cols], psW[:, :], ALU.add)\
                    .then_inc(acc_done, 1)

            with dve.Fori(0, PAIRS) as g:
                for i in range(NCH):
                    dve.wait_ge(proj_ps, START + g * 12 + 3 * i + 2)
                    nc.vector.tensor_copy(KT[:, i * CH:(i + 1) * CH], bank(3 * i + 1)).then_inc(k_ready, 1)
                for s in range(NS + 3):
                    if s < NS:
                        b, qi, e = STEPS[s]
                        dve.wait_ge(s_ps, START + g * NS + s + 1)
                        nc.vector.tensor_reduce(nmax[:, s % 4:s % 4 + 1], psS[:, e, 0:(qi + 1) * P], AX.X, ALU.max,
                                                negate=True).then_inc(max_done, 1)
                    if s % PER_CHUNK == 0 and s > PER_CHUNK:
                        add_out(g, s // PER_CHUNK - 2)
                    if s >= 3:
                        for r in range(first_group[s - 3], first_group[s - 2]):
                            if r % 2 == 1:
                                copy_out(dve, g, r, nc.vector.tensor_copy, ev_dve)
                    if 1 <= s <= NS:
                        b, qi, e = STEPS[s - 1]
                        keys, q = (qi + 1) * P, (s - 1) % 4
                        dve.wait_ge(exp_done, START + g * NS + s)
                        nc.vector.reciprocal(rinv[:, q:q + 1], rsum[:, q:q + 1]).then_inc(dchain, 1)
                        dve.wait_ge(dchain, START + g * NS + s)
                        nc.vector.tensor_scalar(prob[:, q, 0:keys], prob[:, q, 0:keys], rinv[:, q:q + 1], None,
                                                ALU.mult).then_inc(norm_done, 1)
                add_out(g, CHUNKS - 1)


def windowed_layers(nc, m, d):
    with ExitStack() as ctx:
        sb, ps, sem = tensors(ctx, nc, "b_")
        k = Memory()
        k.w_qkv = sb("w_qkv", [P, 3 * H * DH])
        k.wo = sb("wo", [P, PAIRS, D])
        k.w1 = sb("w1", [P, 2 * FFN_IN])
        k.w2 = sb("w2", [P, NF, D])
        k.cols = sb("cols", [P, 3 + 2 * NF])
        k.KT = sb("KT", [P, 2, PAIRS, WIN + P])
        k.v = sb("v", [P, 2, 2, PAIRS * DH])
        k.attn_in = sem("attn_in")
        k.ffn_in = sem("ffn_in")
        attention = WindowAttention(ctx, nc, k)
        ffn = GatedFfn(ctx, nc, k)
        start_semaphores(nc, m, [k.attn_in, k.ffn_in] + attention.sems + ffn.sems)
        with nc.Block() as block:
            @block.sync
            def _(sp):
                sp.dma_start(k.w_qkv[:, :], d["b_wqkv"][0]).then_inc(k.attn_in, 16)
                sp.dma_start(k.wo[:, :, :], d["b_wo"][0]).then_inc(k.attn_in, 16)

            @block.vector
            def _(dve):
                nc.vector.memset(k.KT[:, :, :, :], 0.0).then_inc(attention.o_ps, 1)
                nc.vector.memset(k.v[:, :, :, :], 0.0).then_inc(attention.o_ps, 1)

        with nc.Fori(0, LAYERS) as layer:
            attention.emit(nc, m, d, k, layer)
            ffn.emit(nc, m, d, k, layer)
        with nc.Block() as block:
            @block.sync
            def _(sp):
                sp.wait_ge(k.attn_in, START + (LAYERS + 1) * 32)


class WindowAttention:
    NAMES = ("xs_ready v_ps k_ps q_ps sq_done rot_done ss_done khat_done v_ready win_even win_odd tr_ps tr_act s_ps "
             "sub_done exp_done sum_done o_ps norm_done res_done halo_done dchain pchain").split()
    FULL = ["p0", "p1", "k0", "k1", "q0", "q1", "o0", "o1", "w"]
    LAST = ["p0", "p1", "o0", "o1", "w"]

    def __init__(self, ctx, nc, k):
        sb, ps, sem = tensors(ctx, nc, "ba_")
        self.sems = [sem(name) for name in self.NAMES]
        (self.xs_ready, self.v_ps, self.k_ps, self.q_ps, self.sq_done, self.rot_done, self.ss_done, self.khat_done,
         self.v_ready, self.win_even, self.win_odd, self.tr_ps, self.tr_act, self.s_ps, self.sub_done, self.exp_done,
         self.sum_done, self.o_ps, self.norm_done, self.res_done, self.halo_done, self.dchain,
         self.pchain) = self.sems
        self.win_in = (self.win_even, self.win_odd)

    def emit(self, nc, m, d, k, layer):
        with ExitStack() as ctx:
            sb, ps, _ = tensors(ctx, nc, "bt_")
            W = H * DH
            xs = sb("xs", [P, 2, P])
            sq = sb("sq", [P, 2, W])
            t1 = sb("t1", [P, 2, W])
            t2 = sb("t2", [P, 2, W])
            ss = sb("ss", [P, 2, H])
            rn = sb("rn", [P, 2, H])
            hat = sb("hat", [P, 2, 2, W])
            QT = sb("QT", [P, PAIRS, P])
            win = sb("win", [P, 2, P // WIN, PAIRS * DH])
            sc = sb("sc", [P, W])
            prob = sb("prob", [P, PAIRS, 2, 2 * WIN])
            probT = sb("probT", [P, PAIRS, P])
            mx = sb("mx", [P, H])
            rs = sb("rs", [P, H])
            rr = sb("rr", [P, H])
            o = sb("o", [P, PAIRS, 2, DH])
            OT = sb("OT", [P, PAIRS, P])
            psA = ps("psA", [P, W])
            psB = ps("psB", [P, W])
            psC = ps("psC", [P, 2, BANK])
            psD = ps("psD", [P, W])
            s = self
            base = layer * NT
            Q, K = 0, 1
            NTURN = 4 + 9 * (NT - 1) + 5
            NACT = 4 + 8 * (NT - 1) + 4

            def turn(n, u, what, last):
                order = self.LAST if last else self.FULL
                i = order.index(what)
                number = layer * NTURN + 4 + 9 * n + i
                half = (u + i) % 2
                return number, half, i, order

            def act_count(n, i, order):
                return layer * NACT + 4 + 8 * n + i + 1

            block = ctx.enter_context(nc.Block())

            @block.sync
            def _(sp):
                sp.dma_start(k.w1[:, :], d["b_w1"][bass.ds(layer, 1)].rearrange("l d f -> (l d) f")).then_inc(k.ffn_in, 16)
                sp.dma_start(k.w2[:, :, :], d["b_w2"][bass.ds(layer, 1)].rearrange("l p c d -> (l p) c d")).then_inc(k.ffn_in, 16)
                sp.dma_start(k.cols[:, :], d["b_cols"][bass.ds(layer, 1)].rearrange("l p c -> (l p) c")).then_inc(k.ffn_in, 16)
                sp.dma_start(m.rot_scale[:, :, :], d["rot_scale"][bass.ds(layer + 1, 1)].rearrange("l a f -> (l a f)")
                             .partition_broadcast(P).rearrange("p (a f) -> p a f", f=DH)).then_inc(k.ffn_in, 16)

                def windows(n, u):
                    sp.wait_ge(s.v_ready, START + base + n + 1)
                    sp.wait_ge(s.o_ps, START + base + n + 1)
                    for e in range(2):
                        h = 64 * e
                        sp.dma_start(win[h:h + 32, u, 0, :], k.v[P - WIN:P, 1 - u, e, :]).then_inc(s.win_in[u], 16)
                        sp.dma_start(win[h + 32:h + 64, u, 0, :], k.v[0:WIN, u, e, :]).then_inc(s.win_in[u], 16)
                        for w in range(1, P // WIN):
                            sp.dma_start(win[h:h + 64, u, w, :], k.v[WIN * (w - 1):WIN * (w + 1), u, e, :])\
                                .then_inc(s.win_in[u], 16)

                for u in range(2):
                    windows(u, u)
                with sp.Fori(1, NT // 2) as tp:
                    for u in range(2):
                        windows(2 * tp + u, u)

            @block.tensor
            def _(pe):
                def project(n, u, what):
                    ps_, third, done = {"v": (psA, 2, s.v_ps), "k": (psB, 1, s.k_ps), "q": (psA, 0, s.q_ps)}[what]
                    if what == "v":
                        pe.wait_ge(s.xs_ready, START + layer * (NT + 1) + n + 1)
                        pe.wait_ge(s.sq_done, START + 2 * (base + n))
                        pe.wait_ge(s.rot_done, START + 2 * (base + n))
                    if what == "q":
                        pe.wait_ge(s.v_ready, START + base + n + 1)
                    for e in range(2):
                        last = nc.tensor.matmul(ps_[:, e * BANK:(e + 1) * BANK], xs[:, u, :],
                                                k.w_qkv[:, third * W + e * BANK:third * W + (e + 1) * BANK],
                                                start=True, stop=True)
                    last.then_inc(done, 1)

                def take_turn(n, u, what, last):
                    number, half, i, order = turn(n, u, what, last)
                    if i == 0:
                        pe.wait_ge(s.tr_act, START + act_count(n, -2, order) + 1)
                    elif i == 1:
                        pe.wait_ge(s.res_done, START + base + n)
                    else:
                        pe.wait_ge(s.tr_act, START + act_count(n, i - 2, order))
                    return psC[:, half, :]

                def transpose4(dst, src):
                    for j in range(4):
                        last = nc.tensor.transpose(dst[:, j * P:(j + 1) * P], src(j), m.ident[:, :])
                    last.then_inc(s.tr_ps, 1)

                def hat_turn(dst, u, x, g):
                    transpose4(dst, lambda j: hat[:, u, x, (4 * g + j) * P:(4 * g + j + 1) * P])

                def scores(n, u):
                    pe.wait_ge(s.tr_act, START + layer * NACT + (4 if isinstance(n, int) and n == 0 else 2 + 8 * n))
                    pe.wait_ge(s.halo_done, START + base + n)
                    pe.wait_ge(s.norm_done, START + base + n)
                    for e in range(2):
                        nc.tensor.matmul(psD[:, e * BANK:(e + 1) * BANK].rearrange("p (h j) -> p h j", j=2 * WIN),
                                         m.identb[:, :], band_of(n), start=True, stop=True)
                    for hp in range(PAIRS):
                        for e in range(2):
                            for w in range(P // WIN):
                                c = e * BANK + hp * 2 * WIN
                                last = nc.tensor.matmul(
                                    psD[WIN * w:WIN * (w + 1), c:c + 2 * WIN],
                                    QT[64 * e:64 * e + 64, hp, WIN * w:WIN * (w + 1)],
                                    k.KT[64 * e:64 * e + 64, u, hp, WIN * w:WIN * (w + 2)],
                                    start=False, stop=True, skip_group_check=True)
                    last.then_inc(s.s_ps, 1)

                def band_of(n):
                    b = m.band[:, bass.ds(n, 1), :] if not isinstance(n, int) else m.band[:, n:n + 1, :]
                    return b.broadcast_to([P, PAIRS, 2 * WIN])

                def values(n, u):
                    pe.wait_ge(s.win_in[u], START + (base + n - u) * 80 + 160)
                    pe.wait_ge(s.sub_done, START + base + n + 1)
                    nc.tensor.matmul(psD[:, 0:1], m.identb[:, :], m.identb[:, 0:1], start=True, stop=True)
                    for hp in range(PAIRS):
                        for e in range(2):
                            for w in range(P // WIN):
                                c = e * BANK + hp * DH
                                last = nc.tensor.matmul(
                                    psD[WIN * w:WIN * (w + 1), c:c + DH],
                                    probT[64 * e:64 * e + 64, hp, WIN * w:WIN * (w + 1)],
                                    win[64 * e:64 * e + 64, u, w, hp * DH:(hp + 1) * DH],
                                    start=True, stop=True)
                    last.then_inc(s.o_ps, 1)

                def iteration(n, u, projecting, last):
                    if projecting:
                        project(n + 2, u, "v")
                        project(n + 2, u, "k")
                    pe.wait_ge(s.exp_done, START + base + n + 1)
                    for g in range(2):
                        transpose4(take_turn(n, u, f"p{g}", last),
                                   lambda j: prob[:, 4 * g + j, :, :].rearrange("p e j -> p (e j)"))
                    if projecting:
                        project(n + 2, u, "q")
                    pe.wait_ge(s.tr_act, START + act_count(n, 1, None))
                    values(n, u)
                    if not last:
                        for what, x, count in (("k", K, 1), ("q", Q, 2)):
                            pe.wait_ge(s.khat_done, START + 2 * (base + n + 1) + count)
                            for g in range(2):
                                hat_turn(take_turn(n, u, f"{what}{g}", last), 1 - u, x, g)
                    pe.wait_ge(s.norm_done, START + base + n + 1)
                    for g in range(2):
                        transpose4(take_turn(n, u, f"o{g}", last),
                                   lambda j: o[:, 4 * g + j, :, :].rearrange("p e f -> p (e f)"))
                    if not last:
                        scores(n + 1, 1 - u)
                    dst = take_turn(n, u, "w", last)
                    pe.wait_ge(s.tr_act, START + act_count(n, 3 if last else 7, None))
                    for hp in range(PAIRS):
                        mm = nc.tensor.matmul(dst[:, 0:P], k.wo[:, hp, :], OT[:, hp, :],
                                              start=hp == 0, stop=hp == PAIRS - 1)
                    mm.then_inc(s.tr_ps, 1)

                pe.wait_ge(k.attn_in, START + (layer + 1) * 32)
                for n in range(2):
                    for what in "vkq":
                        project(n, n, what)
                for x, count in ((K, 1), (Q, 2)):
                    pe.wait_ge(s.khat_done, START + 2 * base + count)
                    for g in range(2):
                        if x == Q:
                            pe.wait_ge(s.tr_act, START + layer * NACT + g + 1)
                        hat_turn(psC[:, g, :], 0, x, g)
                scores(0, 0)
                with pe.Fori(0, NT // 2 - 1) as tp:
                    for u in range(2):
                        iteration(2 * tp + u, u, True, False)
                iteration(NT - 2, 0, False, False)
                iteration(NT - 1, 1, False, True)

            @block.scalar
            def _(act):
                def value_out(n, u):
                    act.wait_ge(s.v_ps, START + base + n + 1)
                    act.wait_ge(s.win_in[u], START + (base + n - u) * 80)
                    act.wait_ge(s.win_in[1 - u], START + (base + n + u) * 80)
                    nc.scalar.activation(k.v[:, u, :, :], psA[:, :].rearrange("p (e f) -> p e f", e=2), ACT.Copy)\
                        .then_inc(s.v_ready, 1)

                def square(n, what):
                    x = {"k": 0, "q": 1}[what]
                    act.wait_ge(s.k_ps if x == 0 else s.q_ps, START + base + n + 1)
                    if not isinstance(n, int):
                        act.wait_ge(s.ss_done, START + 2 * (base + n) + x - 1)
                    elif n == 1:
                        act.wait_ge(s.ss_done, START + 2 * base + x + 1)
                    nc.scalar.activation(sq[:, x, :], (psB if x == 0 else psA)[:, :], ACT.Square).then_inc(s.sq_done, 1)

                def copy_out(number, half, dst):
                    act.wait_ge(s.tr_ps, START + number + 1)
                    nc.scalar.activation(dst, psC[:, half, :].rearrange("p (h t) -> p h t", t=P), ACT.Copy)\
                        .then_inc(s.tr_act, 1)

                def turn_out(n, u, what, last, dst):
                    number, half, i, order = turn(n, u, what, last)
                    copy_out(number, half, dst)

                def exponential(n):
                    act.wait_ge(s.sub_done, START + base + n + 1)
                    act.wait_ge(s.sum_done, START + base + n)
                    nc.scalar.activation(prob[:, :, :, :].rearrange("p h e j -> p e h j"),
                                         sc[:, :].rearrange("p (e h j) -> p e h j", e=2, j=2 * WIN), ACT.Exp,
                                         scale=QK_SCALE)\
                        .then_inc(s.exp_done, 1)

                def iteration(n, u, projecting, last):
                    if projecting:
                        value_out(n + 2, u)
                        square(n + 2, "k")
                    for g in range(2):
                        turn_out(n, u, f"p{g}", last, probT[:, 4 * g:4 * g + 4, :])
                    if projecting:
                        square(n + 2, "q")
                    if not last:
                        for g in range(2):
                            turn_out(n, u, f"k{g}", last, k.KT[:, 1 - u, 4 * g:4 * g + 4, WIN:WIN + P])
                        for g in range(2):
                            turn_out(n, u, f"q{g}", last, QT[:, 4 * g:4 * g + 4, :])
                    for g in range(2):
                        turn_out(n, u, f"o{g}", last, OT[:, 4 * g:4 * g + 4, :])
                    if not last:
                        exponential(n + 1)

                for n in range(2):
                    value_out(n, n)
                    square(n, "k")
                    square(n, "q")
                for g in range(2):
                    copy_out(layer * NTURN + g, g, k.KT[:, 0, 4 * g:4 * g + 4, WIN:WIN + P])
                for g in range(2):
                    copy_out(layer * NTURN + 2 + g, g, QT[:, 4 * g:4 * g + 4, :])
                exponential(0)
                with act.Fori(0, NT // 2 - 1) as tp:
                    for u in range(2):
                        iteration(2 * tp + u, u, True, False)
                iteration(NT - 2, 0, False, False)
                iteration(NT - 1, 1, False, True)

            CPT = 4

            @block.vector
            def _(dve):
                def shift(n, u):
                    at = n * P
                    nc.vector.tensor_copy(xs[0:64, u, :], m.xa[0:64, bass.ds(at + 1, P)])
                    nc.vector.tensor_copy(xs[64:P, u, 1:P], m.xa[64:P, bass.ds(at + 1, P - 1)])
                    nc.vector.tensor_scalar(xs[64:P, u, 0:1], m.xa[64:P, bass.ds(at, 1)],
                                            m.keep[64:P, bass.ds(n, 1)], None, ALU.mult).then_inc(s.xs_ready, 1)

                def rotate(n, u, what):
                    x = {"k": 0, "q": 1}[what]
                    src = (psB if x == 0 else psA)[:, :].rearrange("p (h c f) -> p h c f", c=2, f=DH // 2)
                    dve.wait_ge(s.sq_done, START + 2 * (base + n) + x + 1)
                    dve.wait_ge(s.khat_done, START + 2 * base + (2 * (n - 1) + x + 1 if not isinstance(n, int) or n >= 1
                                                            else 0))
                    table = m.rot[:, bass.ds(n, 1), :, :].rearrange("p n a f -> p (n a) f")
                    a = 2 * (1 - x)
                    cos = spread(table[:, a, :], 1, H)
                    sin = spread(table[:, a + 1, :].rearrange("p (c f) -> p c f", c=2), 1, H)
                    nc.vector.tensor_tensor(t1[:, x, :].rearrange("p (h f) -> p h f", f=DH),
                                            src.rearrange("p h c f -> p h (c f)"), cos, ALU.mult)
                    nc.vector.tensor_tensor(t2[:, x, :].rearrange("p (h c f) -> p h c f", c=2, f=DH // 2),
                                            src[:, :, ::-1, :], sin, ALU.mult).then_inc(s.rot_done, 1)

                def norms(n, what, link):
                    x = {"k": 0, "q": 1}[what]
                    link(n, nc.vector.tensor_reduce(ss[:, x, :], sq[:, x, :].rearrange("p (h f) -> p h f", f=DH), AX.X, ALU.add))
                    nc.vector.tensor_scalar(ss[:, x, :], ss[:, x, :], 1e-24, None, ALU.max).then_inc(s.ss_done, 1)

                def halo(n, u):
                    dve.wait_ge(s.tr_act, START + layer * NACT + 4 + 8 * n - 12)
                    dve.wait_ge(s.s_ps, START + base + n - 1)
                    nc.vector.tensor_scalar(k.KT[:, u, :, 0:WIN], k.KT[:, 1 - u, :, P:P + WIN],
                                            m.keep[:, bass.ds(n, 1)], None, ALU.mult).then_inc(s.halo_done, 1)

                def subtract_maximum(n, link):
                    dve.wait_ge(s.s_ps, START + base + n + 1)
                    scores = psD[:, :].rearrange("p (h j) -> p h j", j=2 * WIN)
                    link(n, nc.vector.tensor_reduce(mx[:, :], scores, AX.X, ALU.max))
                    dve.wait_ge(s.exp_done, START + base + n)
                    nc.vector.tensor_tensor(sc[:, :].rearrange("p (h j) -> p h j", j=2 * WIN), scores,
                                            spread(mx[:, :], 2, 2 * WIN), ALU.subtract).then_inc(s.sub_done, 1)

                def iteration(n, u, projecting, last):
                    counts = [0]
                    before = 5 + CPT * n - (2 if last else 0)

                    def link(_, ins):
                        ins.then_inc(s.dchain, 1)
                        counts[0] += 1
                        dve.wait_ge(s.dchain, START + layer * (CPT * NT) + before + counts[0])

                    dve.wait_ge(s.exp_done, START + base + n + 1)
                    link(n, nc.vector.tensor_reduce(rs[:, :].rearrange("p (e h) -> p h e", e=2), prob[:, :, :, :],
                                                    AX.X, ALU.add))
                    nc.vector.reciprocal(rr[:, :], rs[:, :]).then_inc(s.sum_done, 1)
                    if projecting:
                        rotate(n + 2, u, "k")
                        norms(n + 2, "k", link)
                        shift(n + 3, 1 - u)
                    dve.wait_ge(s.sum_done, START + base + n + 1)
                    dve.wait_ge(s.o_ps, START + base + n + 3)
                    nc.vector.tensor_tensor(o[:, :, :, :].rearrange("p h e f -> p e h f"),
                                            psD[:, :].rearrange("p (e h f) -> p e h f", e=2, f=DH),
                                            spread(rr[:, :].rearrange("p (e h) -> p e h", e=2), 3, DH),
                                            ALU.mult).then_inc(s.norm_done, 1)
                    if projecting:
                        rotate(n + 2, u, "q")
                        norms(n + 2, "q", link)
                    if not last:
                        halo(n + 2, u)
                        subtract_maximum(n + 1, link)
                    number, half, _, _ = turn(n, u, "w", last)
                    dve.wait_ge(s.tr_ps, START + number + 1)
                    cols = bass.ds(n * P + 1, P)
                    nc.vector.tensor_tensor(m.xb[:, cols], m.xa[:, cols], psC[:, half, 0:P], ALU.add)\
                        .then_inc(s.res_done, 1)

                done = [0]

                def link0(n, ins):
                    ins.then_inc(s.dchain, 1)
                    done[0] += 1
                    dve.wait_ge(s.dchain, START + layer * (CPT * NT) + done[0])

                for n in range(2):
                    shift(n, n)
                for n in range(2):
                    for what in "kq":
                        rotate(n, n, what)
                        norms(n, what, link0)
                    if n == 0:
                        shift(2, 0)
                dve.wait_ge(s.tr_act, START + layer * NACT + 2)
                nc.vector.tensor_scalar(k.KT[:, 1, :, 0:WIN], k.KT[:, 0, :, P:P + WIN], m.keep[:, 1:2], None,
                                        ALU.mult).then_inc(s.halo_done, 1)
                subtract_maximum(0, link0)
                with dve.Fori(0, NT // 2 - 1) as tp:
                    for u in range(2):
                        iteration(2 * tp + u, u, True, False)
                iteration(NT - 2, 0, False, False)
                iteration(NT - 1, 1, False, True)

            @block.gpsimd
            def _(pool):
                def finish(n, u, what):
                    x = {"k": 0, "q": 1}[what]
                    count = 2 * (base + n) + x
                    pool.wait_ge(s.ss_done, START + count + 1)
                    nc.gpsimd.tensor_tensor(rn[:, x, :], ss[:, x, :], m.minus_half[:, 0:H], ALU.pow).then_inc(s.pchain, 1)
                    pool.wait_ge(s.rot_done, START + count + 1)
                    nc.gpsimd.tensor_tensor(t1[:, x, :], t1[:, x, :], t2[:, x, :], ALU.add).then_inc(s.pchain, 1)
                    pool.wait_ge(s.pchain, START + 2 * count + 2)
                    if not isinstance(n, int):
                        pool.wait_ge(s.tr_ps, START + layer * NTURN + 4 + 9 * (n - 2))
                    nc.gpsimd.tensor_tensor(hat[:, u, 1 - x, :].rearrange("p (hp e f) -> p e hp f", e=2, f=DH),
                                            t1[:, x, :].rearrange("p (e hp f) -> p e hp f", e=2, f=DH),
                                            spread(rn[:, x, :].rearrange("p (e hp) -> p e hp", e=2), 3, DH),
                                            ALU.mult).then_inc(s.khat_done, 1)

                for n in range(2):
                    for what in "kq":
                        finish(n, n, what)
                with pool.Fori(1, NT // 2) as tp:
                    for u in range(2):
                        for what in "kq":
                            finish(2 * tp + u, u, what)


class GatedFfn:
    NAMES = "xs_ready f_ps stat_done rstd_done xn_ready b_ps xnT_ready ga_ps gelu_done h_done y_ps y_done rot_done dchain".split()

    def __init__(self, ctx, nc, k):
        sb, ps, sem = tensors(ctx, nc, "bf_")
        self.sems = [sem(name) for name in self.NAMES]
        (self.xs_ready, self.f_ps, self.stat_done, self.rstd_done, self.xn_ready, self.b_ps, self.xnT_ready,
         self.ga_ps, self.gelu_done, self.h_done, self.y_ps, self.y_done, self.rot_done, self.dchain) = self.sems

    def emit(self, nc, m, d, k, layer):
        with ExitStack() as ctx:
            sb, ps, _ = tensors(ctx, nc, "bg_")
            xs = sb("xs", [P, 2, CH])
            stats = sb("stats", [P, 4, 6])
            mv = sb("mv", [P, 4, 2])
            veps = sb("veps", [P, 4])
            rstd = sb("rstd", [P, 4])
            xn = sb("xn", [P, 4, D])
            xnT = sb("xnT", [P, 2, CH])
            gel = sb("gel", [P, 2, CH])
            h = sb("h", [P, 2, NF, CH])
            psF = ps("psF", [P, BANK])
            psR = ps("psR", [P, BANK])
            psG = ps("psG", [P, 2, 2, BANK])
            psY = ps("psY", [P, 2, BANK])
            s = self
            T = CH // P
            c0 = layer * NCH
            g0 = layer * (NCH * NF)
            ln_g, ln_b, b2 = (k.cols[:, i:i + 1] for i in range(3))
            block = ctx.enter_context(nc.Block())

            @block.sync
            def _(sp):
                sp.dma_start(k.w_qkv[:, :], d["b_wqkv"][bass.ds(layer + 1, 1)].rearrange("l d f -> (l d) f"))\
                    .then_inc(k.attn_in, 16)
                sp.dma_start(k.wo[:, :, :], d["b_wo"][bass.ds(layer + 1, 1)].rearrange("l p h d -> (l p) h d"))\
                    .then_inc(k.attn_in, 16)
            @block.tensor
            def _(pe):
                def forward(c):
                    pe.wait_ge(s.xs_ready, START + c0 + c + 1)
                    pe.wait_ge(s.xn_ready, START + c0 + c)
                    for j in range(T):
                        last = nc.tensor.transpose(psF[:, j * P:(j + 1) * P], xs[:, c % 2, j * P:(j + 1) * P], m.ident[:, :])
                    last.then_inc(s.f_ps, 1)

                def back(c):
                    pe.wait_ge(s.xn_ready, START + c0 + c + 1)
                    pe.wait_ge(s.xnT_ready, START + c0 + c)
                    for j in range(T):
                        last = nc.tensor.transpose(psR[:, j * P:(j + 1) * P], xn[:, j, :], m.ident[:, :])
                    last.then_inc(s.b_ps, 1)

                pe.wait_ge(k.ffn_in, START + (layer + 1) * 64)
                forward(0)
                back(0)
                for c in range(NCH):
                    if c + 1 < NCH:
                        forward(c + 1)
                    pe.wait_ge(s.xnT_ready, START + c0 + c + 1)
                    for i, (f0, width) in enumerate(FFN_PARTS):
                        n = c * NF + i
                        if n >= 2:
                            pe.wait_ge(s.h_done, START + g0 + n - 1)
                        for gate in range(2):
                            last = nc.tensor.matmul(psG[0:width, n % 2, gate, :],
                                                    k.w1[:, gate * FFN_IN + f0:gate * FFN_IN + f0 + width],
                                                    xnT[:, c % 2, :], start=True, stop=True)
                        last.then_inc(s.ga_ps, 1)
                    if c + 1 < NCH:
                        back(c + 1)
                    pe.wait_ge(s.h_done, START + g0 + (c + 1) * NF)
                    if c >= 2:
                        pe.wait_ge(s.y_done, START + c0 + c - 1)
                    for i, (f0, width) in enumerate(FFN_PARTS):
                        last = nc.tensor.matmul(psY[:, c % 2, :], k.w2[0:width, i, :], h[0:width, c % 2, i, :],
                                                start=i == 0, stop=i == NF - 1)
                    last.then_inc(s.y_ps, 1)

            @block.scalar
            def _(act):
                def norm_out(c):
                    act.wait_ge(s.b_ps, START + c0 + c + 1)
                    nc.scalar.activation(xnT[:, c % 2, :], psR[:, :], ACT.Identity, scale=ln_g, bias=ln_b)\
                        .then_inc(s.xnT_ready, 1)

                act.wait_ge(k.ffn_in, START + (layer + 1) * 64)
                norm_out(0)
                for c in range(NCH):
                    for i, (f0, width) in enumerate(FFN_PARTS):
                        n = c * NF + i
                        act.wait_ge(s.ga_ps, START + g0 + n + 1)
                        if n >= 2:
                            act.wait_ge(s.h_done, START + g0 + n - 1)
                        nc.scalar.activation(gel[0:width, n % 2, :], psG[0:width, n % 2, 1, :], ACT.Gelu,
                                             bias=k.cols[0:width, 3 + NF + i:4 + NF + i]).then_inc(s.gelu_done, 1)
                    if c + 1 < NCH:
                        norm_out(c + 1)

            @block.vector
            def _(dve):
                def shift(c):
                    first = c * CH + 1
                    if c * CH % S == 0:
                        nc.vector.memset(xs[64:P, c % 2, 0:1], 0.0)
                    skip = 1 if c * CH % S == 0 else 0
                    nc.vector.tensor_copy(xs[64:P, c % 2, skip:CH], m.xb[64:P, first - 1 + skip:first + CH - 1])
                    nc.vector.tensor_copy(xs[0:64, c % 2, :], m.xb[0:64, first:first + CH]).then_inc(s.xs_ready, 1)

                def norm(c):
                    chain = Chain(dve, s.dchain, START + layer * (2 * NCH) + 2 * c)
                    dve.wait_ge(s.f_ps, START + c0 + c + 1)
                    psx = psF[:, :].rearrange("p (t f) -> p t f", f=D)
                    for t in range(T):
                        last = nc.vector.bn_stats(stats[:, t, :], psx[:, t, :])
                    chain.link(last)
                    nc.vector.memset(veps[:, :], LN_EPS)
                    for t in range(T):
                        last = nc.vector.bn_aggr(mv[:, t, :], stats[:, t, :])
                    chain.link(last)
                    nc.vector.tensor_tensor(veps[:, :], veps[:, :], mv[:, :, 1], ALU.add).then_inc(s.stat_done, 1)
                    if c >= 1:
                        dve.wait_ge(s.b_ps, START + c0 + c)
                    dve.wait_ge(s.rstd_done, START + c0 + c + 1)
                    for t in range(T):
                        last = nc.vector.tensor_scalar(xn[:, t, :], psx[:, t, :], mv[:, t, 0:1], rstd[:, t:t + 1],
                                                       ALU.subtract, ALU.mult)
                    last.then_inc(s.xn_ready, 1)

                dve.wait_ge(k.ffn_in, START + (layer + 1) * 64)
                shift(0)
                norm(0)
                shift(1)
                for c in range(NCH):
                    if c + 1 < NCH:
                        norm(c + 1)
                    if c + 2 < NCH:
                        shift(c + 2)
                    for i, (f0, width) in enumerate(FFN_PARTS):
                        n = c * NF + i
                        dve.wait_ge(s.gelu_done, START + g0 + n + 1)
                        nc.vector.scalar_tensor_tensor(out=h[0:width, c % 2, i, :], in0=psG[0:width, n % 2, 0, :],
                                                       scalar=k.cols[0:width, 3 + i:4 + i], in1=gel[0:width, n % 2, :],
                                                       op0=ALU.add, op1=ALU.mult).then_inc(s.h_done, 1)
                    dve.wait_ge(s.y_ps, START + c0 + c + 1)
                    cols = slice(1 + c * CH, 1 + (c + 1) * CH)
                    nc.vector.scalar_tensor_tensor(out=m.xa[:, cols], in0=psY[:, c % 2, :], scalar=b2,
                                                   in1=m.xb[:, cols], op0=ALU.add, op1=ALU.add).then_inc(s.y_done, 1)

            @block.gpsimd
            def _(pool):
                pool.wait_ge(k.ffn_in, START + (layer + 1) * 64)
                for b in range(B):
                    nc.gpsimd.tensor_tensor(m.rot[:, b * 8:b * 8 + 8, :, :], m.rot_base[:, :, :, :],
                                            spread(m.rot_scale[:, :, :], 1, 8), ALU.mult).then_inc(s.rot_done, 1)
                for c in range(NCH):
                    pool.wait_ge(s.stat_done, START + c0 + c + 1)
                    nc.gpsimd.tensor_tensor(rstd[:, :], veps[:, :], m.minus_half[:, 0:T], ALU.pow)\
                        .then_inc(s.rstd_done, 1)


def second_norm(nc, m, d):
    with ExitStack() as ctx:
        sb, ps, sem = tensors(ctx, nc, "n1_")
        stats = sb("stats", [P, NT, 6])
        mv = sb("mv", [P, NT, 2])
        eps_sum = sb("eps_sum", [P, NT])
        rstd = sb("rstd", [P, NT])
        ms = sb("ms", [P, NT])
        rrms = sb("rrms", [P, NT])
        xn = sb("xn", [P, NT, D])
        xr = sb("xr", [P, NT, D])
        router_w = sb("router_w", [D, E])
        bias = sb("bias", [P, E])
        norm_w = sb("norm_w", [D, 1])
        lower = sb("lower", [P, E, E])
        score = sb("score", [P, NT, E])
        s = sb("s", [P, NT, E])
        pair_max = sb("pair_max", [P, NT * GROUPS, 2])
        pair_min = sb("pair_min", [P, NT * GROUPS, 2])
        top = sb("top", [P, NT * GROUPS])
        second = sb("second", [P, NT * GROUPS])
        gscore = sb("gscore", [P, NT, GROUPS])
        above = sb("above", [P, NT * E * E])
        equal = sb("equal", [P, NT * E * E])
        rank = sb("rank", [P, NT * E])
        gsel = sb("gsel", [P, NT, GROUPS])
        gout = sb("gout", [P, NT, GROUPS])
        masked = sb("masked", [P, NT, E])
        wsum = sb("wsum", [P, NT])
        psX = ps("psX", [P, 4, BANK])
        psN = ps("psN", [P, 2, BANK])
        psL = ps("psL", [P, NT, E])
        names = "in_ dchain x_ps x_ready stat_done pow_done xn_ready n_ps n_ready logits_ps score_done".split()
        in_, dchain, x_ps, x_ready, stat_done, pow_done, xn_ready, n_ps, n_ready, logits_ps, score_done = map(sem, names)
        block = ctx.enter_context(nc.Block())
        T4 = CH // P

        @block.sync
        def _(sp):
            sp.dma_start(router_w[:, :], d["router_w"]).then_inc(in_, 16)
            sp.dma_start(bias[:, :], d["router_bias"].partition_broadcast(P)).then_inc(in_, 16)
            sp.dma_start(norm_w[:, :], d["c_norm_w"]).then_inc(in_, 16)
            sp.dma_start(lower[:, :, :].rearrange("p a b -> p (a b)"),
                         d["lower"].rearrange("a b -> (a b)").partition_broadcast(P)).then_inc(in_, 16)
            sp.wait_ge(in_, 64)

        @block.tensor
        def _(pe):
            pe.wait_ge(dchain, 1)
            for t in range(NT):
                nc.tensor.transpose(psX[:, t // 4, (t % 4) * P:(t % 4 + 1) * P],
                                    m.branchT[:, t * P:(t + 1) * P], m.ident[:, :]).then_inc(x_ps, 1)
            for i in range(2 * NCH):
                src = (xn, xr)[i // NCH]
                pe.wait_ge(xn_ready, i // NCH + 1)
                if i >= 2:
                    pe.wait_ge(n_ready, i - 1)
                for j in range(T4):
                    last = nc.tensor.transpose(psN[:, i % 2, j * P:(j + 1) * P], src[:, (i % NCH) * T4 + j, :],
                                               m.ident[:, :])
                last.then_inc(n_ps, 1)
            pe.wait_ge(n_ready, NCH)
            pe.wait_ge(in_, 64)
            for t in range(NT):
                last = nc.tensor.matmul(psL[:, t, :], m.xnT[:, t * P:(t + 1) * P], router_w[:, :], start=True, stop=True)
            last.then_inc(logits_ps, 1)

        @block.scalar
        def _(act):
            act.wait_ge(in_, 64)
            for i in range(2 * NCH):
                act.wait_ge(n_ps, i + 1)
                cols = slice((i % NCH) * CH, (i % NCH + 1) * CH)
                if i < NCH:
                    nc.scalar.activation(m.xnT[:, cols], psN[:, i % 2, :], ACT.Copy).then_inc(n_ready, 1)
                else:
                    nc.scalar.activation(m.xrT[:, cols], psN[:, i % 2, :], ACT.Copy, scale=norm_w[:, 0:1])\
                        .then_inc(n_ready, 1)
            act.wait_ge(logits_ps, 1)
            nc.scalar.activation(score[:, :, :], psL[:, :, :], ACT.Sigmoid).then_inc(score_done, 1)

        @block.gpsimd
        def _(pool):
            for i, out in enumerate((rstd, rrms)):
                pool.wait_ge(stat_done, i + 1)
                nc.gpsimd.tensor_tensor(out[:, :], eps_sum[:, :], m.minus_half[:, 0:NT], ALU.pow).then_inc(pow_done, 1)

        @block.vector
        def _(dve):
            chain = Chain(dve, dchain)
            v = nc.vector
            chain.link(v.tensor_tensor(m.branchT[:, :], m.branchT[:, :], m.xa[:, 1:1 + N], ALU.add))
            for c in range(NCH):
                dve.wait_ge(x_ps, T4 * (c + 1))
                tiles = slice(T4 * c, T4 * (c + 1))
                last = v.tensor_tensor(m.x[:, tiles, :], m.x[:, tiles, :],
                                       psX[:, c, :].rearrange("p (t f) -> p t f", f=D), ALU.add)
            chain.link(last)
            norm_statistics(nc, dve, chain.link, m.x, stats, mv, NT)
            v.tensor_scalar(eps_sum[:, :], mv[:, :, 1], LN_EPS, None, ALU.add).then_inc(stat_done, 1)
            dve.wait_ge(pow_done, 1)
            for t in range(NT):
                last = v.tensor_scalar(xn[:, t, :], m.x[:, t, :], mv[:, t, 0:1], rstd[:, t:t + 1],
                                       ALU.subtract, ALU.mult)
            last.then_inc(xn_ready, 1)
            dve.wait_ge(xn_ready, 1)
            chain.link(v.tensor_tensor(xr[:, :, :], xn[:, :, :], xn[:, :, :], ALU.mult))
            chain.link(v.tensor_reduce(ms[:, :], xr[:, :, :], AX.X, ALU.add))
            v.tensor_scalar(eps_sum[:, :], ms[:, :], 1.0 / D, RMS_EPS, ALU.mult, ALU.add).then_inc(stat_done, 1)
            dve.wait_ge(pow_done, 2)
            v.tensor_tensor(xr[:, :, :], xn[:, :, :], spread(rrms[:, :], 2, D), ALU.mult).then_inc(xn_ready, 1)

            def ranks(x, n):
                big = [P, NT, n, n]
                a = above[:, 0:NT * n * n].rearrange("p (t i j) -> p t i j", i=n, j=n)
                q = equal[:, 0:NT * n * n].rearrange("p (t i j) -> p t i j", i=n, j=n)
                mine, other = spread(x, 3, n), spread(x, 2, n)
                v.tensor_tensor(a, other, mine, ALU.is_gt)
                chain.link(v.tensor_tensor(q, other, mine, ALU.is_equal))
                chain.link(v.tensor_tensor(q, q, spread(lower[:, 0:n, 0:n], 1, NT), ALU.mult))
                chain.link(v.tensor_tensor(a, a, q, ALU.add))
                chain.link(v.tensor_reduce(rank[:, 0:NT * n].rearrange("p (t i) -> p t i", i=n), a, AX.X, ALU.add))

            dve.wait_ge(in_, 64)
            dve.wait_ge(score_done, 1)
            chain.link(v.tensor_tensor(s[:, :, :], score[:, :, :], spread(bias[:, :], 1, NT), ALU.add))
            by_pair = s[:, :, :].rearrange("p t (g c a) -> p (t g) c a", g=GROUPS, a=2)
            v.tensor_tensor(pair_max[:, :, :], by_pair[:, :, :, 0], by_pair[:, :, :, 1], ALU.max)
            chain.link(v.tensor_tensor(pair_min[:, :, :], by_pair[:, :, :, 0], by_pair[:, :, :, 1], ALU.min))
            v.tensor_tensor(top[:, :], pair_max[:, :, 0], pair_max[:, :, 1], ALU.max)
            v.tensor_tensor(second[:, :], pair_max[:, :, 0], pair_max[:, :, 1], ALU.min)
            chain.link(v.tensor_tensor(pair_min[:, :, 0], pair_min[:, :, 0], pair_min[:, :, 1], ALU.max))
            chain.link(v.tensor_tensor(second[:, :], second[:, :], pair_min[:, :, 0], ALU.max))
            chain.link(v.tensor_tensor(gscore[:, :, :].rearrange("p t g -> p (t g)"), top[:, :], second[:, :], ALU.add))
            ranks(gscore[:, :, :], GROUPS)
            rank_g = rank[:, 0:NT * GROUPS].rearrange("p (t i) -> p t i", i=GROUPS)
            chain.link(v.tensor_scalar(gsel[:, :, :], rank_g, float(TOP_GROUPS), None, ALU.is_lt))
            chain.link(v.tensor_scalar(gout[:, :, :], gsel[:, :, :], -1.0, None, ALU.add))
            by_group = masked[:, :, :].rearrange("p t (g c) -> p (t g) c", g=GROUPS)
            flat = gsel[:, :, :].rearrange("p t g -> p (t g)"), gout[:, :, :].rearrange("p t g -> p (t g)")
            chain.link(v.tensor_tensor(by_group, s[:, :, :].rearrange("p t (g c) -> p (t g) c", g=GROUPS),
                                       spread(flat[0], 2, E // GROUPS), ALU.mult))
            chain.link(v.tensor_tensor(by_group, by_group, spread(flat[1], 2, E // GROUPS), ALU.add))
            ranks(masked[:, :, :], E)
            chain.link(v.tensor_scalar(masked[:, :, :], rank[:, :].rearrange("p (t i) -> p t i", i=E), float(TOP_K),
                                       None, ALU.is_lt))
            chain.link(v.tensor_tensor(masked[:, :, :], masked[:, :, :], score[:, :, :], ALU.mult))
            chain.link(v.tensor_reduce(wsum[:, :], masked[:, :, :], AX.X, ALU.add))
            chain.link(v.tensor_scalar(wsum[:, :], wsum[:, :], 1e-20, None, ALU.add))
            chain.link(v.reciprocal(wsum[:, :], wsum[:, :]))
            chain.link(v.tensor_scalar(wsum[:, :], wsum[:, :], ROUTE_SCALE, None, ALU.mult))
            v.tensor_tensor(m.combine[:, 0:E, :].rearrange("p e t -> p t e"), masked[:, :, :],
                            spread(wsum[:, :], 2, E), ALU.mult)
            v.memset(m.combine[:, E:NE, :], 1.0)


def capped_attention(nc, m, d):
    TB = S // P
    NS = B * TB * 2
    NJ = NS // 2
    with ExitStack() as ctx:
        sb, ps, sem = tensors(ctx, nc, "c_")
        gamma = sb("gamma", [P, PAIRS, 2])
        factor = sb("factor", [P, PAIRS, 2])
        fac = sb("fac", [P, 2])
        w = sb("w", [P, 3 * P])
        wo = sb("wo", [P, D])
        raw = sb("raw", [P, NT, 3 * P])
        sq = sb("sq", [P, 4, 2 * P])
        ss = sb("ss", [P, NT, 4])
        rn = sb("rn", [P, NT, 4])
        QT = sb("QT", [P, N])
        KT = sb("KT", [P, N])
        th = sb("th", [P, 3, S])
        prob = sb("prob", [P, 4, S])
        acc = sb("acc", [P, 2, S])
        rec = sb("rec", [P, 2, BANK])
        OT = sb("OT", [P, S])
        psS = ps("psS", [P, 2, S])
        psO = ps("psO", [P, S])
        psL = ps("psL", [P, BANK])
        psW = ps("psW", [P, BANK])
        names = ("g_in w_in wo_in proj_ps raw_ready ss_done rn_done hat_done h_ps q_ready k_ready st_ps tanh_done "
                 "exp_done acc_done pv_ps sum_ps rec_done ot_ready wo_ps add_done dchain factor_done").split()
        (g_in, w_in, wo_in, proj_ps, raw_ready, ss_done, rn_done, hat_done, h_ps, q_ready, k_ready, st_ps, tanh_done,
         exp_done, acc_done, pv_ps, sum_ps, rec_done, ot_ready, wo_ps, add_done, dchain, factor_done) = sems = [sem(name) for name in names]
        start_semaphores(nc, m, sems)
        block = ctx.enter_context(nc.Block())

        def bank(n):
            return psS[:, n // 2, (n % 2) * BANK:(n % 2 + 1) * BANK]

        @block.sync
        def _(sp):
            sp.dma_start(gamma[:, :, :], d["c_gamma"].rearrange("a p x -> p a x")).then_inc(g_in, 16)
            with sp.Fori(0, PAIRS) as g:
                sp.wait_ge(proj_ps, START + g * NT)
                sp.dma_start(w[:, :], d["c_wqkv"][bass.ds(g, 1)].rearrange("g d x f -> (g d) (x f)")).then_inc(w_in, 16)
                sp.wait_ge(wo_ps, START + g * 2 * B)
                sp.dma_start(wo[:, :], d["c_wo"][bass.ds(g, 1)].rearrange("g f d -> (g f) d")).then_inc(wo_in, 16)
            sp.wait_ge(g_in, START + 16)
            sp.wait_ge(w_in, START + PAIRS * 16)
            sp.wait_ge(wo_in, START + PAIRS * 16)

        @block.tensor
        def _(pe):
            def scores(g, s):
                b, kt, e = s // (2 * TB), s // 2 % TB, s % 2
                if s >= 2:
                    pe.wait_ge(tanh_done, START + g * NS + s - 1)
                h = slice(64 * e, 64 * e + 64)
                for c in range(2):
                    last = nc.tensor.matmul(psS[:, e, c * BANK:(c + 1) * BANK],
                                            KT[h, b * S + kt * P:b * S + (kt + 1) * P],
                                            QT[h, b * S + c * BANK:b * S + (c + 1) * BANK], start=True, stop=True)
                last.then_inc(st_ps, 1)

            def values(g, j):
                b, kt = j // TB, j % TB
                pe.wait_ge(exp_done, START + g * NS + 2 * j + 2)
                if kt == 0:
                    pe.wait_ge(ot_ready, START + g * 2 * B + 2 * b)
                for c in range(2):
                    for e in range(2):
                        last = nc.tensor.matmul(psO[64 * e:64 * e + 64, c * BANK:(c + 1) * BANK],
                                                raw[:, b * TB + kt, 2 * P + 64 * e:2 * P + 64 * e + 64],
                                                prob[:, (2 * j + e) % 4, c * BANK:(c + 1) * BANK],
                                                start=kt == 0, stop=kt == TB - 1)
                last.then_inc(pv_ps, 1)

            def sums(g, b):
                pe.wait_ge(acc_done, START + g * NS + (b + 1) * 2 * TB)
                for c in range(2):
                    pe.wait_ge(rec_done, START + g * 2 * B + 2 * b + c)
                    if c == 0:
                        pe.wait_ge(add_done, START + g * 2 * B + 2 * b)
                    for e in range(2):
                        last = nc.tensor.matmul(psL[64 * e:64 * e + 64, :], m.ones[:, 0:64],
                                                acc[:, e, c * BANK:(c + 1) * BANK], start=True, stop=True)
                    last.then_inc(sum_ps, 1)

            def project(g, b):
                pe.wait_ge(ot_ready, START + g * 2 * B + 2 * b + 2)
                pe.wait_ge(add_done, START + g * 2 * B + 2 * b)
                if b == 0:
                    pe.wait_ge(wo_in, START + (g + 1) * 16)
                for c, out in enumerate((psW, psL)):
                    for t in range(4):
                        last = nc.tensor.matmul(out[:, t * P:(t + 1) * P], OT[:, (4 * c + t) * P:(4 * c + t + 1) * P],
                                                wo[:, :], start=True, stop=True)
                    last.then_inc(wo_ps, 1)

            def transposes(g, i):
                pe.wait_ge(hat_done, START + g * NCH + i + 1)
                if i >= 1:
                    pe.wait_ge(q_ready, START + g * NCH + i)
                    pe.wait_ge(k_ready, START + g * NCH + i)
                for x in range(2):
                    for t in range(4):
                        last = nc.tensor.transpose(bank(2 + x)[:, t * P:(t + 1) * P],
                                                   raw[:, 4 * i + t, x * P:(x + 1) * P], m.ident[:, :])
                    last.then_inc(h_ps, 1)

            with pe.Fori(0, PAIRS) as g:
                pe.wait_ge(w_in, START + (g + 1) * 16)
                pe.wait_ge(tanh_done, START + g * NS)
                for t in range(NT):
                    if t >= 2:
                        pe.wait_ge(raw_ready, START + g * NT + t - 1)
                    nc.tensor.matmul(bank(t % 2)[:, 0:3 * P], m.xrT[:, t * P:(t + 1) * P], w[:, :],
                                     start=True, stop=True).then_inc(proj_ps, 1)
                    if t >= 7 and t % 4 == 3:
                        transposes(g, t // 4 - 1)
                transposes(g, NCH - 1)
                pe.wait_ge(q_ready, START + (g + 1) * NCH)
                pe.wait_ge(k_ready, START + (g + 1) * NCH)
                scores(g, 0)
                scores(g, 1)
                for j in range(NJ):
                    if j + 1 < NJ:
                        scores(g, 2 * j + 2)
                        scores(g, 2 * j + 3)
                    values(g, j)
                    if j % TB == TB - 1:
                        sums(g, j // TB)
                    if j % TB == 0 and j > 0:
                        project(g, j // TB - 1)
                project(g, B - 1)

        @block.scalar
        def _(act):
            act.wait_ge(factor_done, START + 1)
            with act.Fori(0, PAIRS) as g:
                def q_out(i):
                    act.wait_ge(h_ps, START + g * 2 * NCH + 2 * i + 1)
                    if i == 0:
                        act.wait_ge(factor_done, START + g + 2)
                    nc.scalar.activation(QT[:, i * CH:(i + 1) * CH], bank(2), ACT.Copy, scale=fac[:, 0:1])\
                        .then_inc(q_ready, 1)

                for t in range(NT):
                    act.wait_ge(proj_ps, START + g * NT + t + 1)
                    nc.scalar.activation(raw[:, t, :], bank(t % 2)[:, 0:3 * P], ACT.Copy).then_inc(raw_ready, 1)
                    if t >= 9 and t % 4 == 1:
                        q_out(t // 4 - 2)
                q_out(NCH - 2)
                q_out(NCH - 1)
                for s in range(NS + 1):
                    if s < NS:
                        act.wait_ge(st_ps, START + g * NS + s + 1)
                        if s >= 3:
                            act.wait_ge(exp_done, START + g * NS + s - 2)
                        else:
                            act.wait_ge(exp_done, START + g * NS)
                        nc.scalar.activation(th[:, s % 3, :], psS[:, s % 2, :], ACT.Tanh, scale=1.0 / SOFTCLAMP)\
                            .then_inc(tanh_done, 1)
                    if s >= 1:
                        act.wait_ge(tanh_done, START + g * NS + s)
                        if s >= 5:
                            act.wait_ge(pv_ps, START + g * NJ + (s - 5) // 2 + 1)
                            act.wait_ge(acc_done, START + g * NS + s - 4)
                        nc.scalar.activation(prob[:, (s - 1) % 4, :], th[:, (s - 1) % 3, :], ACT.Exp,
                                             scale=SOFTCLAMP * DH ** -0.5).then_inc(exp_done, 1)

        @block.gpsimd
        def _(pool):
            with pool.Fori(0, PAIRS) as g:
                for i in range(NCH):
                    pool.wait_ge(ss_done, START + g * NCH + i + 1)
                    tiles = slice(4 * i, 4 * i + 4)
                    nc.gpsimd.tensor_tensor(rn[:, tiles, :], ss[:, tiles, :],
                                            m.minus_half[:, 0:16].rearrange("p (t h) -> p t h", h=4), ALU.pow)\
                        .then_inc(rn_done, 1)

        @block.vector
        def _(dve):
            v = nc.vector
            dve.wait_ge(g_in, START + 16)
            v.tensor_scalar(factor[:, :, :], gamma[:, :, :], 1.0, DH ** 0.5, ALU.add, ALU.mult).then_inc(factor_done, 1)
            dve.wait_ge(factor_done, START + 1)
            with dve.Fori(0, PAIRS) as g:
                chain = Chain(dve, dchain, START + g * (2 * NCH))

                def k_out(i):
                    dve.wait_ge(h_ps, START + g * 2 * NCH + 2 * i + 2)
                    if i == 0:
                        dve.wait_ge(factor_done, START + g + 2)
                    v.tensor_scalar(KT[:, i * CH:(i + 1) * CH], bank(3), fac[:, 1:2], None, ALU.mult)\
                        .then_inc(k_ready, 1)

                v.tensor_copy(fac[:, :], factor[:, bass.ds(g, 1), :].rearrange("p g x -> p (g x)"))\
                    .then_inc(factor_done, 1)
                for i in range(NCH):
                    tiles = slice(4 * i, 4 * i + 4)
                    dve.wait_ge(raw_ready, START + g * NT + 4 * i + 4)
                    qk = raw[:, tiles, 0:2 * P]
                    chain.link(v.tensor_tensor(sq[:, :, :], qk, qk, ALU.mult))
                    chain.link(v.tensor_reduce(ss[:, tiles, :], sq[:, :, :].rearrange("p t (h f) -> p t h f", f=DH),
                                               AX.X, ALU.add))
                    v.tensor_scalar(ss[:, tiles, :], ss[:, tiles, :], 1e-24, None, ALU.max).then_inc(ss_done, 1)
                    if i >= 2:
                        k_out(i - 2)
                    dve.wait_ge(rn_done, START + g * NCH + i + 1)
                    heads = qk.rearrange("p t (h f) -> p t h f", f=DH)
                    v.tensor_tensor(heads, heads, spread(rn[:, tiles, :], 3, DH), ALU.mult).then_inc(hat_done, 1)
                k_out(NCH - 2)
                k_out(NCH - 1)

                def add_out(b):
                    for c, out in enumerate((psW, psL)):
                        dve.wait_ge(wo_ps, START + g * 2 * B + 2 * b + c + 1)
                        tiles = slice(b * TB + 4 * c, b * TB + 4 * c + 4)
                        v.tensor_tensor(m.x[:, tiles, :], m.x[:, tiles, :],
                                        out[:, :].rearrange("p (t f) -> p t f", f=D), ALU.add).then_inc(add_done, 1)

                for s in range(NS):
                    b, kt, e = s // (2 * TB), s // 2 % TB, s % 2
                    dve.wait_ge(exp_done, START + g * NS + s + 1)
                    if kt == 0:
                        dve.wait_ge(sum_ps, START + g * 2 * B + 2 * b)
                        v.tensor_copy(acc[:, e, :], prob[:, s % 4, :]).then_inc(acc_done, 1)
                    else:
                        dve.wait_ge(acc_done, START + g * NS + s - 1)
                        v.tensor_tensor(acc[:, e, :], acc[:, e, :], prob[:, s % 4, :], ALU.add).then_inc(acc_done, 1)
                    if s % (2 * TB) == 2 * TB - 1:
                        for c in range(2):
                            dve.wait_ge(sum_ps, START + g * 2 * B + 2 * b + c + 1)
                            v.reciprocal(rec[:, c, :], psL[:, :]).then_inc(rec_done, 1)
                            dve.wait_ge(rec_done, START + g * 2 * B + 2 * b + c + 1)
                            if c == 0:
                                dve.wait_ge(wo_ps, START + g * 2 * B + 2 * b)
                                dve.wait_ge(pv_ps, START + g * NJ + (b + 1) * TB)
                            v.tensor_tensor(OT[:, c * BANK:(c + 1) * BANK], psO[:, c * BANK:(c + 1) * BANK],
                                            rec[:, c, :], ALU.mult).then_inc(ot_ready, 1)
                    if s % (2 * TB) == 1 and s > 2 * TB:
                        add_out(b - 1)
                add_out(B - 1)


def experts(nc, m, d, out):
    with ExitStack() as ctx:
        sb, ps, sem = tensors(ctx, nc, "e_")
        w_gu = sb("w_gu", [D, 2, 2, F])
        w_down = sb("w_down", [F, 2, D])
        weight = sb("weight", [P, 2, NT])
        sg = sb("sg", [F, 2, CH])
        hT = sb("hT", [F, 2, CH])
        psG = ps("psG", [P, 2, BANK])
        psU = ps("psU", [P, 2, BANK])
        psY = ps("psY", [P, 2, BANK])
        names = "w_in_even w_in_odd gu_ps silu_done h_done y_ps y_done weight_done out_done".split()
        w_in_even, w_in_odd, gu_ps, silu_done, h_done, y_ps, y_done, weight_done, out_done = sems = [sem(name) for name in names]
        start_semaphores(nc, m, sems)
        w_in = (w_in_even, w_in_odd)
        block = ctx.enter_context(nc.Block())
        PER = 2 * NCH

        @block.sync
        def _(sp):
            def load(i, u):
                e = 2 * i + u
                sp.dma_start(w_gu[:, u, :, :], d["e_gate_up"][bass.ds(e, 1)].rearrange("e d x f -> (e d) x f"))\
                    .then_inc(w_in[u], 16)
                sp.dma_start(w_down[:, u, :], d["e_down"][bass.ds(e, 1)].rearrange("e f d -> (e f) d"))\
                    .then_inc(w_in[u], 16)
            load(0, 0)
            load(0, 1)
            with sp.Fori(1, NE // 2) as i:
                for u in range(2):
                    sp.wait_ge(y_ps, START + PER * i + NCH * (u - 1))
                    load(i, u)
            rows = out.rearrange("(t p) d -> p t d", p=P)
            for c in range(NCH):
                sp.wait_ge(y_done, START + (NE - 1) * NCH + c + 1)
                sp.dma_start(rows[:, 4 * c:4 * c + 4, :], m.x[:, 4 * c:4 * c + 4, :]).then_inc(out_done, 16)
            sp.wait_ge(out_done, START + NCH * 16)

        @block.tensor
        def _(pe):
            def gate_up(i, c):
                u = c // NCH
                if c % NCH == 0:
                    pe.wait_ge(w_in[u], START + (i + 1) * 32)
                if c >= 2:
                    pe.wait_ge(h_done, START + PER * i + c - 1)
                for x, dst in enumerate((psG, psU)):
                    last = nc.tensor.matmul(dst[:, c % 2, :], w_gu[:, u, x, :],
                                            m.xnT[:, (c % NCH) * CH:(c % NCH + 1) * CH], start=True, stop=True)
                last.then_inc(gu_ps, 1)

            def down(i, c):
                pe.wait_ge(h_done, START + PER * i + c + 1)
                pe.wait_ge(y_done, START + PER * i + max(0, c - 1))
                for t in range(4):
                    last = nc.tensor.matmul(psY[:, c % 2, t * P:(t + 1) * P], hT[:, c % 2, t * P:(t + 1) * P],
                                            w_down[:, c // NCH, :], start=True, stop=True)
                last.then_inc(y_ps, 1)

            with pe.Fori(0, NE // 2) as i:
                for c in range(PER):
                    gate_up(i, c)
                    if c >= 1:
                        down(i, c - 1)
                down(i, PER - 1)

        @block.scalar
        def _(act):
            with act.Fori(0, NE // 2) as i:
                for c in range(PER):
                    act.wait_ge(gu_ps, START + PER * i + c + 1)
                    nc.scalar.activation(sg[:, c % 2, :], psG[:, c % 2, :], ACT.Silu).then_inc(silu_done, 1)

        @block.vector
        def _(dve):
            v = nc.vector

            def add(i, c):
                dve.wait_ge(y_ps, START + PER * i + c + 1)
                for t in range(4):
                    tile = (c % NCH) * 4 + t
                    last = v.scalar_tensor_tensor(out=m.x[:, tile, :], in0=psY[:, c % 2, t * P:(t + 1) * P],
                                                  scalar=weight[:, c // NCH, tile:tile + 1], in1=m.x[:, tile, :],
                                                  op0=ALU.mult, op1=ALU.add)
                last.then_inc(y_done, 1)

            with dve.Fori(0, NE // 2) as i:
                dve.wait_ge(y_done, START + PER * i)
                for u in range(2):
                    v.tensor_copy(weight[:, u, :], m.combine[:, bass.ds(2 * i + u, 1), :].rearrange("p e t -> p (e t)"))\
                        .then_inc(weight_done, 1)
                dve.wait_ge(weight_done, START + 2 * i + 2)
                for c in range(PER):
                    dve.wait_ge(silu_done, START + PER * i + c + 1)
                    if c >= 2:
                        dve.wait_ge(y_ps, START + PER * i + c - 1)
                    v.tensor_tensor(hT[:, c % 2, :], psU[:, c % 2, :], sg[:, c % 2, :], ALU.mult).then_inc(h_done, 1)
                    if c >= 1:
                        add(i, c - 1)
                add(i, PER - 1)


def persistent(ctx, nc):
    sb, _, _ = tensors(ctx, nc, "")
    m = Memory()
    m.x = sb("x", [P, NT, D])
    m.xnT = sb("xnT", [P, N])
    m.xa = sb("xaT", [P, 1 + N + P])
    m.xb = sb("xbT", [P, 1 + N])
    m.branchT = sb("branchT", [P, N])
    m.ident = sb("ident", [P, P])
    m.identb = sb("identb", [P, P], BF16)
    m.causal = sb("causal", [P, P], BF16)
    m.band = sb("band", [P, NT, 2 * WIN], BF16)
    m.keep = sb("keep", [P, NT + 1])
    m.ones = sb("ones", [P, P])
    m.minus_half = sb("minus_half", [P, 4 * NT])
    m.rot_base = sb("rot_base", [P, S // P, 4, DH])
    m.rot_scale = sb("rot_scale", [P, 4, DH])
    m.rot = sb("rot", [P, NT, 4, DH])
    m.xrT = m.xb[:, 1:]
    m.scratch = sb("scratch", [P, 64])
    m.combine = sb("combine", [P, NE, NT])
    return m


def shape_constants():
    i, j = np.arange(P)[:, None], np.arange(P)[None, :]
    c = {"ident": np.eye(P, dtype=np.float32), 
         "causal": np.where(j > i, NEG, 0.0).astype(np.float32)}
    q, k = np.arange(P)[:, None] % WIN, np.arange(2 * WIN)[None, :]
    band = np.where((k >= q) & (k <= q + WIN), 0.0, NEG)
    band = np.repeat(band[:, None, :], NT, axis=1)
    for t in range(0, NT, S // P):
        band[0:WIN, t, 0:WIN] = NEG
    c["band"] = band.astype(np.float32)
    keep = np.ones((NT + 1,), np.float32)
    keep[::S // P] = 0.0
    c["keep"] = keep
    half = np.arange(0, DH, 2, dtype=np.float32)
    inv_freq = (1.0 / np.float32(10000.0) ** (half / np.float32(DH))).astype(np.float32)
    t = np.arange(S, dtype=np.float32)
    freqs = (t[:, None] * inv_freq[None, :]).astype(np.float32).astype(np.float64)
    base = ((half + np.float32(0.4 * DH)) / np.float32(1.4 * DH)).astype(np.float32)
    power = ((t - S // 2) / np.float32(WIN // 2)).astype(np.float32)
    scale = base[None, :].astype(np.float64) ** power[:, None]
    cos, sin = np.cos(freqs), np.sin(freqs)
    sign = np.array([-1.0, 1.0])[None, :, None]

    def both(a):
        return np.repeat(a[:, None, :], 2, axis=1)

    tabs = [both(cos * scale), both(sin * scale) * sign, both(cos / scale), both(sin / scale) * sign]
    tabs = np.stack([a.reshape(S, DH) for a in tabs], axis=1).astype(np.float32)
    c["rot_base"] = np.ascontiguousarray(tabs.reshape(S // P, P, 4, DH).transpose(1, 0, 2, 3))
    c["lower"] = (np.arange(E)[None, :] < np.arange(E)[:, None]).astype(np.float32)
    return c


def laid_out(i):
    f = {k: np.asarray(v) for k, v in i.items()}

    def pairs(w):
        return w.reshape(D, PAIRS, P).transpose(1, 0, 2)

    a = {"x": f["L0_attn_x"].reshape(N, D)}
    qkv = [f[f"L0_attn_w{n}"].reshape(PAIRS, P, D).transpose(0, 2, 1) for n in "qkv"]
    a["a_wqkv"] = np.stack(qkv, axis=2)
    a["a_wo"] = f["L0_attn_wo"].reshape(D, PAIRS, P).transpose(1, 2, 0)

    def again(w):
        return np.concatenate([w, w[:1]])

    def swapped(s):
        return np.concatenate([s[:, DH // 2:], s[:, :DH // 2]], axis=1)

    qs, ks = f["L0_ffn_q_scale"], f["L0_ffn_k_scale"]
    a["rot_scale"] = again(np.stack([qs, swapped(qs), ks, swapped(ks)], axis=1))
    w = f["L0_ffn_Wqkv"].reshape(LAYERS, D, 3, PAIRS, 2, DH).transpose(0, 1, 2, 4, 3, 5)
    a["b_wqkv"] = again(w.reshape(LAYERS, D, 3 * H * DH))
    a["b_wo"] = again(f["L0_ffn_Wo"].reshape(LAYERS, PAIRS, P, D).transpose(0, 2, 1, 3))
    a["b_w1"] = f["L0_ffn_W1"]
    pad = NF * P - FFN_IN
    a["b_w2"] = np.pad(f["L0_ffn_W2"], ((0, 0), (0, pad), (0, 0))).reshape(LAYERS, NF, P, D).transpose(0, 2, 1, 3)
    b1 = np.pad(f["L0_ffn_b1"].reshape(LAYERS, 2, FFN_IN), ((0, 0), (0, 0), (0, pad))).reshape(LAYERS, 2 * NF, P)
    a["b_cols"] = np.concatenate([f["L0_ffn_ln_g"][:, None], f["L0_ffn_ln_b"][:, None], f["L0_ffn_b2"][:, None], b1],
                                 axis=1).transpose(0, 2, 1)
    q, (k, v) = f["L1_attn_Wq"], np.split(f["L1_attn_Wkv"], 2, axis=1)
    a["c_wqkv"] = np.stack([pairs(q), pairs(k), pairs(v)], axis=2)
    a["c_wo"] = f["L1_attn_Wo"].reshape(PAIRS, P, D)
    a["c_norm_w"] = f["L1_attn_norm_w"].reshape(D, 1)
    a["c_gamma"] = np.stack([f["L1_attn_q_gamma"].reshape(PAIRS, P), f["L1_attn_k_gamma"].reshape(PAIRS, P)], axis=2)
    a["router_w"] = f["L1_ffn_router_w"].T
    a["router_bias"] = f["L1_ffn_bias"]

    def halves(w):
        return w.reshape(D, 2, F).transpose(1, 0, 2)

    a["e_gate_up"] = np.stack([np.concatenate([f["L1_ffn_gate_w"], halves(f["L1_ffn_sh_gate_w"])]),
                               np.concatenate([f["L1_ffn_up_w"], halves(f["L1_ffn_sh_up_w"])])], axis=2)
    a["e_down"] = np.concatenate([f["L1_ffn_down_w"], f["L1_ffn_sh_down_w"].reshape(2, F, D)])
    a.update(shape_constants())
    return {k: np.ascontiguousarray(v) for k, v in a.items()}


def build(nc, d, out):
    with ExitStack() as ctx:
        m = persistent(ctx, nc)
        load_and_norm(nc, m, d)
        causal_attention(nc, m, d)
        windowed_layers(nc, m, d)
        second_norm(nc, m, d)
        capped_attention(nc, m, d)
        experts(nc, m, d, out)


def kernel(**inputs):
    import concourse.bacc as bacc
    from concourse.bass_utils import run_bass_kernel_spmd

    nc = bacc.Bacc("TRN2", target_bir_lowering=False, num_devices=1)
    arrays = {f"in_{k}": v for k, v in laid_out(inputs).items()}
    d = {k[3:]: nc.dram_tensor(k, v.shape, mybir.dt.from_np(v.dtype), kind="ExternalInput").ap()
         for k, v in arrays.items()}
    out = nc.dram_tensor("out", (N, D), F32, kind="ExternalOutput").ap()
    build(nc, d, out)
    r = run_bass_kernel_spmd(nc, [arrays], core_ids=[0])
    return r.results[0]["out"].reshape(B, S, D)
```

```python
from contextlib import ExitStack

import numpy as np
import concourse.bass as bass
from concourse import mybir
from concourse.alu_op_type import AluOpType as ALU

F32 = mybir.dt.float32
BF16 = mybir.dt.bfloat16
ACT = mybir.ActivationFunctionType
AX = mybir.AxisListType

P = 128
B, S, D = 2, 1024, 128
N = B * S
NT = N // P
H, DH = 16, 64
PAIRS = H // 2
LAYERS = 6
WIN = 32
FFN_IN = int(D * 4 * 2 / 3)
FFN_PARTS = [(i * P, min(P, FFN_IN - i * P)) for i in range(-(-FFN_IN // P))]
NF = len(FFN_PARTS)
CH = 512
NCH = N // CH
E, F = 16, 128
NE = E + 2
GROUPS, TOP_GROUPS, TOP_K, ROUTE_SCALE = 4, 2, 4, 2.5
LN_EPS = 1e-5
RMS_EPS = float(np.finfo(np.float32).eps)
NEG = -1e30
QK_SCALE = 8.0
SOFTCLAMP = 50.0
BANK = 512
START = 4


def spread(ap, axis, n):
    a = ap.unsqueeze(axis)
    shape = list(a.shape)
    shape[axis] = n
    return a.broadcast_to(shape)


class Chain:

    def __init__(self, engine, sem, start=0):
        self.engine, self.sem, self.start, self.count = engine, sem, start, 0

    def link(self, instruction):
        instruction.then_inc(self.sem, 1)
        self.count += 1
        self.engine.wait_ge(self.sem, self.start + self.count)


def start_semaphores(nc, m, sems):
    with nc.Block() as block:
        @block.gpsimd
        def _(pool):
            for i, sem in enumerate(sems):
                nc.gpsimd.memset(m.scratch[:, i:i + 1], 0.0).then_inc(sem, START)


class Memory:
    pass


def tensors(ctx, nc, prefix):
    def sb(name, shape, dt=F32):
        return ctx.enter_context(nc.sbuf_tensor(prefix + name, shape, dt))

    def ps(name, shape, dt=F32):
        return ctx.enter_context(nc.psum_tensor(prefix + name, shape, dt))

    def sem(name):
        return ctx.enter_context(nc.semaphore(prefix + name))

    return sb, ps, sem


def norm_statistics(nc, dve, link, x, stats, mv, count):
    for t in range(count):
        last = nc.vector.bn_stats(stats[:, t, :], x[:, t, :])
    link(last)
    for t in range(count):
        last = nc.vector.bn_aggr(mv[:, t, :], stats[:, t, :])
    link(last)


def load_and_norm(nc, m, d):
    with ExitStack() as ctx:
        sb, ps, sem = tensors(ctx, nc, "n0_")
        stats = sb("stats", [P, NT, 6])
        mv = sb("mv", [P, NT, 2])
        veps = sb("veps", [P, NT])
        rstd = sb("rstd", [P, NT])
        xn = sb("xn", [P, NT, D])
        causal = sb("causal", [P, P])
        band = sb("band", [P, NT, 2 * WIN])
        psT = ps("psT", [P, 4, BANK])
        x_in, const_in, pow_in, ready, dchain, rstd_ready, xn_ready, xnT_ps = map(sem, (
            "x_in", "const_in", "pow_in", "ready", "dchain", "rstd_ready", "xn_ready", "xnT_ps"))
        xT_ready, zeros = sem("xT_ready"), sem("zeros")
        block = ctx.enter_context(nc.Block())

        @block.sync
        def _(sp):
            sp.dma_start(m.x[:, :, :], d["x"].rearrange("(t p) d -> p t d", p=P)).then_inc(x_in, 16)
            sp.dma_start(m.ident[:, :], d["ident"]).then_inc(const_in, 16)
            sp.dma_start(causal[:, :], d["causal"]).then_inc(const_in, 16)
            sp.dma_start(band[:, :, :], d["band"]).then_inc(const_in, 16)
            sp.dma_start(m.keep[:, :], d["keep"].partition_broadcast(P)).then_inc(const_in, 16)
            sp.dma_start(m.rot_base[:, :, :, :], d["rot_base"]).then_inc(const_in, 16)
            sp.dma_start(m.rot_scale[:, :, :], d["rot_scale"][0].partition_broadcast(P)).then_inc(const_in, 16)
            sp.wait_ge(const_in, 6 * 16)
            sp.wait_ge(x_in, 16)

        @block.gpsimd
        def _(pool):
            nc.gpsimd.memset(m.minus_half[:, :], -0.5).then_inc(ready, 1)
            nc.gpsimd.memset(m.ones[:, :], 1.0)
            nc.gpsimd.memset(m.xa[:, 0:1], 0.0)
            nc.gpsimd.memset(m.xa[:, 1 + N:], 0.0)
            nc.gpsimd.memset(m.xb[:, 0:1], 0.0)
            nc.gpsimd.memset(m.branchT[:, :], 0.0).then_inc(zeros, 1)
            pool.wait_ge(const_in, 6 * 16)
            for b in range(B):
                nc.gpsimd.tensor_tensor(m.rot[:, b * 8:b * 8 + 8, :, :], m.rot_base[:, :, :, :],
                                        spread(m.rot_scale[:, :, :], 1, 8), ALU.mult).then_inc(zeros, 1)
            pool.wait_ge(dchain, 3)
            pool.wait_ge(ready, 1)
            nc.gpsimd.tensor_tensor(rstd[:, :], veps[:, :], m.minus_half[:, 0:NT], ALU.pow).then_inc(rstd_ready, 1)

        @block.vector
        def _(dve):
            chain = Chain(dve, dchain)
            dve.wait_ge(x_in, 16)
            norm_statistics(nc, dve, chain.link, m.x, stats, mv, NT)
            chain.link(nc.vector.tensor_scalar(veps[:, :], mv[:, :, 1], LN_EPS, None, ALU.add))
            dve.wait_ge(rstd_ready, 1)
            for t in range(NT):
                nc.vector.tensor_scalar(xn[:, t, :], m.x[:, t, :], mv[:, t, 0:1], rstd[:, t:t + 1],
                                        ALU.subtract, ALU.mult).then_inc(xn_ready, 1)

        @block.tensor
        def _(pe):
            pe.wait_ge(const_in, 6 * 16)
            for t in range(NT):
                pe.wait_ge(xn_ready, t + 1)
                nc.tensor.transpose(psT[:, t // 4, (t % 4) * P:(t % 4 + 1) * P], xn[:, t, :],
                                    m.ident[:, :]).then_inc(xnT_ps, 1)

        @block.scalar
        def _(act):
            act.wait_ge(const_in, 6 * 16)
            nc.scalar.activation(m.identb[:, :], m.ident[:, :], ACT.Copy).then_inc(xT_ready, 1)
            nc.scalar.activation(m.causal[:, :], causal[:, :], ACT.Copy).then_inc(xT_ready, 1)
            nc.scalar.activation(m.band[:, :, :], band[:, :, :], ACT.Copy).then_inc(xT_ready, 1)
            for c in range(NCH):
                act.wait_ge(xnT_ps, 4 * (c + 1))
                nc.scalar.activation(m.xa[:, 1 + c * CH:1 + (c + 1) * CH], psT[:, c, :], ACT.Copy)\
                    .then_inc(xT_ready, 1)
                nc.scalar.activation(m.xnT[:, c * CH:(c + 1) * CH], psT[:, c, :], ACT.Copy)\
                    .then_inc(xT_ready, 1)


def causal_attention(nc, m, d):
    TB = S // P
    STEPS = [(b, qi, e) for b in range(B) for qi in range(TB) for e in range(2)]
    NS = len(STEPS)
    PER_CHUNK = 8
    CHUNKS = NS // PER_CHUNK
    groups = []
    for s, (b, qi, e) in enumerate(STEPS):
        groups += [(s, k, min(4, qi + 1 - k)) for k in range(0, qi + 1, 4)]
    NG = len(groups)
    first_group = [next(r for r, g in enumerate(groups) if g[0] == s) for s in range(NS)] + [NG]

    with ExitStack() as ctx:
        sb, ps, sem = tensors(ctx, nc, "a0_")
        w = sb("w", [P, 3, P])
        wo = sb("wo", [P, D])
        QT = sb("QT", [P, N])
        KT = sb("KT", [P, N])
        V = sb("V", [P, NT, P])
        prob = sb("prob", [P, 4, S])
        probT = sb("probT", [P, 2, 2, TB, CH])
        OT = sb("OT", [P, CH])
        nmax = sb("nmax", [P, 4])
        rsum = sb("rsum", [P, 4])
        rinv = sb("rinv", [P, 4])
        psS = ps("psS", [P, 2, S])
        psT = ps("psT", [P, 2, BANK])
        psO = ps("psO", [P, BANK])
        psW = ps("psW", [P, BANK])
        names = ("w_in wo_in proj_ps q_ready k_ready v_ready s_ps max_done exp_done dchain norm_done t_ps "
                 "ev_act ev_dve pv_ps ot_ready wo_ps acc_done").split()
        (w_in, wo_in, proj_ps, q_ready, k_ready, v_ready, s_ps, max_done, exp_done, dchain, norm_done, t_ps,
         ev_act, ev_dve, pv_ps, ot_ready, wo_ps, acc_done) = sems = [sem(name) for name in names]
        start_semaphores(nc, m, sems)
        block = ctx.enter_context(nc.Block())

        def bank(n):
            return psS[:, (n % 4) // 2, ((n % 4) % 2) * BANK:((n % 4) % 2 + 1) * BANK]

        @block.sync
        def _(sp):
            with sp.Fori(0, PAIRS) as g:
                sp.wait_ge(proj_ps, START + g * 12)
                sp.dma_start(w[:, :, :], d["a_wqkv"][bass.ds(g, 1)].rearrange("g d x f -> (g d) x f")).then_inc(w_in, 16)
                sp.wait_ge(wo_ps, START + g * CHUNKS)
                sp.dma_start(wo[:, :], d["a_wo"][bass.ds(g, 1)].rearrange("g f d -> (g f) d")).then_inc(wo_in, 16)

        @block.tensor
        def _(pe):
            def scores(g, s):
                b, qi, e = STEPS[s]
                if s >= 2:
                    pe.wait_ge(exp_done, START + g * NS + s - 1)
                keys = (qi + 1) * P
                h = slice(64 * e, 64 * e + 64)
                for k in range(0, keys, BANK):
                    n = min(BANK, keys - k)
                    diagonal = k + n == keys
                    last = nc.tensor.matmul(psS[:, e, k:k + n], QT[h, b * S + qi * P:b * S + (qi + 1) * P],
                                            KT[h, b * S + k:b * S + k + n], start=True, stop=not diagonal)
                    if diagonal:
                        last = nc.tensor.matmul(psS[:, e, keys - P:keys], m.identb[:, :], m.causal[:, :],
                                                start=False, stop=True)
                last.then_inc(s_ps, 1)

            def transposes(g, s):
                pe.wait_ge(norm_done, START + g * NS + s + 1)
                for r in range(first_group[s], first_group[s + 1]):
                    _, k0, n = groups[r]
                    pe.wait_ge(ev_act if r % 2 == 0 else ev_dve, START + g * (NG // 2) + r // 2)
                    for j in range(n):
                        last = nc.tensor.transpose(psT[:, r % 2, j * P:(j + 1) * P],
                                                   prob[:, s % 4, (k0 + j) * P:(k0 + j + 1) * P], m.ident[:, :])
                    last.then_inc(t_ps, 1)

            def values(g, c):
                b, qc = c // 2, c % 2
                done = first_group[PER_CHUNK * (c + 1)]
                pe.wait_ge(ev_act, START + g * (NG // 2) + (done + 1) // 2)
                pe.wait_ge(ev_dve, START + g * (NG // 2) + done // 2)
                pe.wait_ge(ot_ready, START + g * CHUNKS + c)
                kts = 4 * (qc + 1)
                for kt in range(kts):
                    r0 = max(0, kt - 4 * qc) * P
                    for e in range(2):
                        last = nc.tensor.matmul(psO[64 * e:64 * e + 64, r0:CH], V[:, b * TB + kt, 64 * e:64 * e + 64],
                                                probT[:, c % 2, e, kt, r0:CH], start=kt == 0, stop=kt == kts - 1)
                last.then_inc(pv_ps, 1)

            def project(g, c):
                pe.wait_ge(ot_ready, START + g * CHUNKS + c + 1)
                pe.wait_ge(acc_done, START + g * CHUNKS + c)
                if c == 0:
                    pe.wait_ge(wo_in, START + (g + 1) * 16)
                nc.tensor.matmul(psW[:, :], wo[:, :], OT[:, :], start=True, stop=True).then_inc(wo_ps, 1)

            with pe.Fori(0, PAIRS) as g:
                pe.wait_ge(w_in, START + (g + 1) * 16)
                pe.wait_ge(exp_done, START + g * NS)
                for i in range(NCH):
                    for x in range(3):
                        n = 3 * i + x
                        if n >= 4:
                            who = (q_ready, k_ready, v_ready)[(n - 4) % 3]
                            pe.wait_ge(who, START + g * NCH + (n - 4) // 3 + 1)
                        if x < 2:
                            last = nc.tensor.matmul(bank(n), w[:, x, :], m.xnT[:, i * CH:(i + 1) * CH],
                                                    start=True, stop=True)
                        else:
                            for j in range(4):
                                last = nc.tensor.matmul(bank(n)[:, j * P:(j + 1) * P],
                                                        m.xnT[:, i * CH + j * P:i * CH + (j + 1) * P], w[:, 2, :],
                                                        start=True, stop=True)
                        last.then_inc(proj_ps, 1)
                for ready in (q_ready, k_ready, v_ready):
                    pe.wait_ge(ready, START + (g + 1) * NCH)
                scores(g, 0)
                scores(g, 1)
                for s in range(NS + 1):
                    if s + 2 < NS:
                        scores(g, s + 2)
                    if s >= 1:
                        transposes(g, s - 1)
                    if s % PER_CHUNK == 3 and s > PER_CHUNK:
                        values(g, s // PER_CHUNK - 1)
                    if s % PER_CHUNK == 5 and s > PER_CHUNK:
                        project(g, s // PER_CHUNK - 1)
                values(g, CHUNKS - 1)
                project(g, CHUNKS - 1)

        def copy_out(engine, g, r, copy, done):
            s, k0, n = groups[r]
            b, qi, e = STEPS[s]
            c = s // PER_CHUNK
            engine.wait_ge(t_ps, START + g * NG + r + 1)
            if c >= 2:
                engine.wait_ge(pv_ps, START + g * CHUNKS + c - 1)
            copy(probT[:, c % 2, e, k0:k0 + n, (qi % 4) * P:(qi % 4 + 1) * P],
                 psT[:, r % 2, 0:n * P].rearrange("p (k q) -> p k q", q=P)).then_inc(done, 1)

        @block.scalar
        def _(act):
            def copy(out, in_):
                return nc.scalar.activation(out, in_, ACT.Copy)

            def heads_out(g, c):
                act.wait_ge(pv_ps, START + g * CHUNKS + c + 1)
                act.wait_ge(wo_ps, START + g * CHUNKS + c)
                nc.scalar.activation(OT[:, :], psO[:, :], ACT.Copy).then_inc(ot_ready, 1)

            with act.Fori(0, PAIRS) as g:
                for i in range(NCH):
                    act.wait_ge(proj_ps, START + g * 12 + 3 * i + 1)
                    nc.scalar.activation(QT[:, i * CH:(i + 1) * CH], bank(3 * i), ACT.Copy, scale=DH ** -0.5)\
                        .then_inc(q_ready, 1)
                    act.wait_ge(proj_ps, START + g * 12 + 3 * i + 3)
                    nc.scalar.activation(V[:, 4 * i:4 * i + 4, :], bank(3 * i + 2).rearrange("p (t f) -> p t f", f=P),
                                         ACT.Copy).then_inc(v_ready, 1)
                for s in range(NS + 3):
                    if s % PER_CHUNK == 6 and s > PER_CHUNK:
                        heads_out(g, s // PER_CHUNK - 1)
                    if s >= 3:
                        for r in range(first_group[s - 3], first_group[s - 2]):
                            if r % 2 == 0:
                                copy_out(act, g, r, copy, ev_act)
                    if s < NS:
                        b, qi, e = STEPS[s]
                        keys = (qi + 1) * P
                        act.wait_ge(max_done, START + g * NS + s + 1)
                        nc.scalar.activation(prob[:, s % 4, 0:keys], psS[:, e, 0:keys], ACT.Exp,
                                             bias=nmax[:, s % 4:s % 4 + 1],
                                             accum_out=rsum[:, s % 4:s % 4 + 1]).then_inc(exp_done, 1)
                heads_out(g, CHUNKS - 1)

        @block.vector
        def _(dve):
            def add_out(g, c):
                b, qc = c // 2, c % 2
                dve.wait_ge(wo_ps, START + g * CHUNKS + c + 1)
                cols = slice(b * S + qc * CH, b * S + (qc + 1) * CH)
                nc.vector.tensor_tensor(m.branchT[:, cols], m.branchT[:, cols], psW[:, :], ALU.add)\
                    .then_inc(acc_done, 1)

            with dve.Fori(0, PAIRS) as g:
                for i in range(NCH):
                    dve.wait_ge(proj_ps, START + g * 12 + 3 * i + 2)
                    nc.vector.tensor_copy(KT[:, i * CH:(i + 1) * CH], bank(3 * i + 1)).then_inc(k_ready, 1)
                for s in range(NS + 3):
                    if s < NS:
                        b, qi, e = STEPS[s]
                        dve.wait_ge(s_ps, START + g * NS + s + 1)
                        nc.vector.tensor_reduce(nmax[:, s % 4:s % 4 + 1], psS[:, e, 0:(qi + 1) * P], AX.X, ALU.max,
                                                negate=True).then_inc(max_done, 1)
                    if s % PER_CHUNK == 0 and s > PER_CHUNK:
                        add_out(g, s // PER_CHUNK - 2)
                    if s >= 3:
                        for r in range(first_group[s - 3], first_group[s - 2]):
                            if r % 2 == 1:
                                copy_out(dve, g, r, nc.vector.tensor_copy, ev_dve)
                    if 1 <= s <= NS:
                        b, qi, e = STEPS[s - 1]
                        keys, q = (qi + 1) * P, (s - 1) % 4
                        dve.wait_ge(exp_done, START + g * NS + s)
                        nc.vector.reciprocal(rinv[:, q:q + 1], rsum[:, q:q + 1]).then_inc(dchain, 1)
                        dve.wait_ge(dchain, START + g * NS + s)
                        nc.vector.tensor_scalar(prob[:, q, 0:keys], prob[:, q, 0:keys], rinv[:, q:q + 1], None,
                                                ALU.mult).then_inc(norm_done, 1)
                add_out(g, CHUNKS - 1)


def windowed_layers(nc, m, d):
    with ExitStack() as ctx:
        sb, ps, sem = tensors(ctx, nc, "b_")
        k = Memory()
        k.w_qkv = sb("w_qkv", [P, 3 * H * DH])
        k.wo = sb("wo", [P, PAIRS, D])
        k.w1 = sb("w1", [P, 2 * FFN_IN])
        k.w2 = sb("w2", [P, NF, D])
        k.cols = sb("cols", [P, 3 + 2 * NF])
        k.KT = sb("KT", [P, 2, PAIRS, WIN + P])
        k.v = sb("v", [P, 2, 2, PAIRS * DH])
        k.attn_in = sem("attn_in")
        k.ffn_in = sem("ffn_in")
        attention = WindowAttention(ctx, nc, k)
        ffn = GatedFfn(ctx, nc, k)
        start_semaphores(nc, m, [k.attn_in, k.ffn_in] + attention.sems + ffn.sems)
        with nc.Block() as block:
            @block.sync
            def _(sp):
                sp.dma_start(k.w_qkv[:, :], d["b_wqkv"][0]).then_inc(k.attn_in, 16)
                sp.dma_start(k.wo[:, :, :], d["b_wo"][0]).then_inc(k.attn_in, 16)

            @block.vector
            def _(dve):
                nc.vector.memset(k.KT[:, :, :, :], 0.0).then_inc(attention.o_ps, 1)
                nc.vector.memset(k.v[:, :, :, :], 0.0).then_inc(attention.o_ps, 1)

        with nc.Fori(0, LAYERS) as layer:
            attention.emit(nc, m, d, k, layer)
            ffn.emit(nc, m, d, k, layer)
        with nc.Block() as block:
            @block.sync
            def _(sp):
                sp.wait_ge(k.attn_in, START + (LAYERS + 1) * 32)


class WindowAttention:
    NAMES = ("xs_ready v_ps k_ps q_ps sq_done rot_done ss_done khat_done v_ready win_even win_odd tr_ps tr_act s_ps "
             "sub_done exp_done sum_done o_ps norm_done res_done halo_done dchain pchain").split()
    FULL = ["p0", "p1", "k0", "k1", "q0", "q1", "o0", "o1", "w"]
    LAST = ["p0", "p1", "o0", "o1", "w"]

    def __init__(self, ctx, nc, k):
        sb, ps, sem = tensors(ctx, nc, "ba_")
        self.sems = [sem(name) for name in self.NAMES]
        (self.xs_ready, self.v_ps, self.k_ps, self.q_ps, self.sq_done, self.rot_done, self.ss_done, self.khat_done,
         self.v_ready, self.win_even, self.win_odd, self.tr_ps, self.tr_act, self.s_ps, self.sub_done, self.exp_done,
         self.sum_done, self.o_ps, self.norm_done, self.res_done, self.halo_done, self.dchain,
         self.pchain) = self.sems
        self.win_in = (self.win_even, self.win_odd)

    def emit(self, nc, m, d, k, layer):
        with ExitStack() as ctx:
            sb, ps, _ = tensors(ctx, nc, "bt_")
            W = H * DH
            xs = sb("xs", [P, 2, P])
            sq = sb("sq", [P, 2, W])
            t1 = sb("t1", [P, 2, W])
            t2 = sb("t2", [P, 2, W])
            ss = sb("ss", [P, 2, H])
            rn = sb("rn", [P, 2, H])
            hat = sb("hat", [P, 2, 2, W])
            QT = sb("QT", [P, PAIRS, P])
            win = sb("win", [P, 2, P // WIN, PAIRS * DH])
            sc = sb("sc", [P, W])
            prob = sb("prob", [P, PAIRS, 2, 2 * WIN])
            probT = sb("probT", [P, PAIRS, P])
            mx = sb("mx", [P, H])
            rs = sb("rs", [P, H])
            rr = sb("rr", [P, H])
            o = sb("o", [P, PAIRS, 2, DH])
            OT = sb("OT", [P, PAIRS, P])
            psA = ps("psA", [P, W])
            psB = ps("psB", [P, W])
            psC = ps("psC", [P, 2, BANK])
            psD = ps("psD", [P, W])
            s = self
            base = layer * NT
            Q, K = 0, 1
            NTURN = 4 + 9 * (NT - 1) + 5
            NACT = 4 + 8 * (NT - 1) + 4

            def turn(n, u, what, last):
                order = self.LAST if last else self.FULL
                i = order.index(what)
                number = layer * NTURN + 4 + 9 * n + i
                half = (u + i) % 2
                return number, half, i, order

            def act_count(n, i, order):
                return layer * NACT + 4 + 8 * n + i + 1

            def normed(engine, u, x):
                engine.tensor_tensor(hat[:, u, 1 - x, :].rearrange("p (hp e f) -> p e hp f", e=2, f=DH),
                                     t1[:, x, :].rearrange("p (e hp f) -> p e hp f", e=2, f=DH),
                                     spread(rn[:, x, :].rearrange("p (e hp) -> p e hp", e=2), 3, DH),
                                     ALU.mult).then_inc(s.khat_done, 1)

            block = ctx.enter_context(nc.Block())

            @block.sync
            def _(sp):
                sp.dma_start(k.w1[:, :], d["b_w1"][bass.ds(layer, 1)].rearrange("l d f -> (l d) f")).then_inc(k.ffn_in, 16)
                sp.dma_start(k.w2[:, :, :], d["b_w2"][bass.ds(layer, 1)].rearrange("l p c d -> (l p) c d")).then_inc(k.ffn_in, 16)
                sp.dma_start(k.cols[:, :], d["b_cols"][bass.ds(layer, 1)].rearrange("l p c -> (l p) c")).then_inc(k.ffn_in, 16)
                sp.dma_start(m.rot_scale[:, :, :], d["rot_scale"][bass.ds(layer + 1, 1)].rearrange("l a f -> (l a f)")
                             .partition_broadcast(P).rearrange("p (a f) -> p a f", f=DH)).then_inc(k.ffn_in, 16)

                def windows(n, u):
                    sp.wait_ge(s.v_ready, START + base + n + 1)
                    sp.wait_ge(s.o_ps, START + base + n + 1)
                    for e in range(2):
                        h = 64 * e
                        sp.dma_start(win[h:h + 32, u, 0, :], k.v[P - WIN:P, 1 - u, e, :]).then_inc(s.win_in[u], 16)
                        sp.dma_start(win[h + 32:h + 64, u, 0, :], k.v[0:WIN, u, e, :]).then_inc(s.win_in[u], 16)
                        for w in range(1, P // WIN):
                            sp.dma_start(win[h:h + 64, u, w, :], k.v[WIN * (w - 1):WIN * (w + 1), u, e, :])\
                                .then_inc(s.win_in[u], 16)

                for u in range(2):
                    windows(u, u)
                with sp.Fori(1, NT // 2) as tp:
                    for u in range(2):
                        windows(2 * tp + u, u)

            @block.tensor
            def _(pe):
                def project(n, u, what, first="v"):
                    ps_, third, done = {"v": (psA, 2, s.v_ps), "k": (psB, 1, s.k_ps), "q": (psA, 0, s.q_ps)}[what]
                    if what == first:
                        pe.wait_ge(s.xs_ready, START + layer * (NT + 1) + n + 1)
                        pe.wait_ge(s.sq_done, START + 2 * (base + n))
                        pe.wait_ge(s.rot_done, START + 2 * (base + n))
                    if what == "q":
                        pe.wait_ge(s.v_ready, START + base + n + 1)
                    for e in range(2):
                        last = nc.tensor.matmul(ps_[:, e * BANK:(e + 1) * BANK], xs[:, u, :],
                                                k.w_qkv[:, third * W + e * BANK:third * W + (e + 1) * BANK],
                                                start=True, stop=True)
                    last.then_inc(done, 1)

                def take_turn(n, u, what, last):
                    number, half, i, order = turn(n, u, what, last)
                    if i == 0:
                        pe.wait_ge(s.tr_act, START + act_count(n, -2, order) + 1)
                    elif i == 1:
                        pe.wait_ge(s.res_done, START + base + n)
                    else:
                        pe.wait_ge(s.tr_act, START + act_count(n, i - 2, order))
                    return psC[:, half, :]

                def transpose4(dst, src):
                    for j in range(4):
                        last = nc.tensor.transpose(dst[:, j * P:(j + 1) * P], src(j), m.ident[:, :])
                    last.then_inc(s.tr_ps, 1)

                def hat_turn(dst, u, x, g):
                    transpose4(dst, lambda j: hat[:, u, x, (4 * g + j) * P:(4 * g + j + 1) * P])

                def scores(n, u):
                    pe.wait_ge(s.tr_act, START + layer * NACT + (4 if isinstance(n, int) and n == 0 else 2 + 8 * n))
                    pe.wait_ge(s.halo_done, START + base + n)
                    pe.wait_ge(s.norm_done, START + base + n)
                    for e in range(2):
                        nc.tensor.matmul(psD[:, e * BANK:(e + 1) * BANK].rearrange("p (h j) -> p h j", j=2 * WIN),
                                         m.identb[:, :], band_of(n), start=True, stop=True)
                    for hp in range(PAIRS):
                        for e in range(2):
                            for w in range(P // WIN):
                                c = e * BANK + hp * 2 * WIN
                                last = nc.tensor.matmul(
                                    psD[WIN * w:WIN * (w + 1), c:c + 2 * WIN],
                                    QT[64 * e:64 * e + 64, hp, WIN * w:WIN * (w + 1)],
                                    k.KT[64 * e:64 * e + 64, u, hp, WIN * w:WIN * (w + 2)],
                                    start=False, stop=True, skip_group_check=True)
                    last.then_inc(s.s_ps, 1)

                def band_of(n):
                    b = m.band[:, bass.ds(n, 1), :] if not isinstance(n, int) else m.band[:, n:n + 1, :]
                    return b.broadcast_to([P, PAIRS, 2 * WIN])

                def values(n, u):
                    pe.wait_ge(s.win_in[u], START + (base + n - u) * 80 + 160)
                    pe.wait_ge(s.sub_done, START + base + n + 1)
                    nc.tensor.matmul(psD[:, 0:1], m.identb[:, :], m.identb[:, 0:1], start=True, stop=True)
                    for hp in range(PAIRS):
                        for e in range(2):
                            for w in range(P // WIN):
                                c = e * BANK + hp * DH
                                last = nc.tensor.matmul(
                                    psD[WIN * w:WIN * (w + 1), c:c + DH],
                                    probT[64 * e:64 * e + 64, hp, WIN * w:WIN * (w + 1)],
                                    win[64 * e:64 * e + 64, u, w, hp * DH:(hp + 1) * DH],
                                    start=True, stop=True)
                    last.then_inc(s.o_ps, 1)

                def iteration(n, u, projecting, last):
                    if projecting:
                        project(n + 2, u, "v")
                        project(n + 2, u, "k")
                    pe.wait_ge(s.exp_done, START + base + n + 1)
                    for g in range(2):
                        transpose4(take_turn(n, u, f"p{g}", last),
                                   lambda j: prob[:, 4 * g + j, :, :].rearrange("p e j -> p (e j)"))
                    if projecting:
                        project(n + 2, u, "q")
                    pe.wait_ge(s.tr_act, START + act_count(n, 1, None))
                    values(n, u)
                    if not last:
                        for what, x, count in (("k", K, 1), ("q", Q, 2)):
                            pe.wait_ge(s.khat_done, START + 2 * (base + n + 1) + count)
                            for g in range(2):
                                hat_turn(take_turn(n, u, f"{what}{g}", last), 1 - u, x, g)
                    pe.wait_ge(s.norm_done, START + base + n + 1)
                    for g in range(2):
                        transpose4(take_turn(n, u, f"o{g}", last),
                                   lambda j: o[:, 4 * g + j, :, :].rearrange("p e f -> p (e f)"))
                    if not last:
                        scores(n + 1, 1 - u)
                    dst = take_turn(n, u, "w", last)
                    pe.wait_ge(s.tr_act, START + act_count(n, 3 if last else 7, None))
                    for hp in range(PAIRS):
                        mm = nc.tensor.matmul(dst[:, 0:P], k.wo[:, hp, :], OT[:, hp, :],
                                              start=hp == 0, stop=hp == PAIRS - 1)
                    mm.then_inc(s.tr_ps, 1)

                pe.wait_ge(k.attn_in, START + (layer + 1) * 32)
                for n in range(2):
                    for what in "kvq":
                        project(n, n, what, first="k")
                for x, count in ((K, 1), (Q, 2)):
                    pe.wait_ge(s.khat_done, START + 2 * base + count)
                    for g in range(2):
                        if x == Q:
                            pe.wait_ge(s.tr_act, START + layer * NACT + g + 1)
                        hat_turn(psC[:, g, :], 0, x, g)
                scores(0, 0)
                with pe.Fori(0, NT // 2 - 1) as tp:
                    for u in range(2):
                        iteration(2 * tp + u, u, True, False)
                iteration(NT - 2, 0, False, False)
                iteration(NT - 1, 1, False, True)

            @block.scalar
            def _(act):
                def value_out(n, u):
                    act.wait_ge(s.v_ps, START + base + n + 1)
                    act.wait_ge(s.win_in[u], START + (base + n - u) * 80)
                    act.wait_ge(s.win_in[1 - u], START + (base + n + u) * 80)
                    nc.scalar.activation(k.v[:, u, :, :], psA[:, :].rearrange("p (e f) -> p e f", e=2), ACT.Copy)\
                        .then_inc(s.v_ready, 1)

                def square(n, what):
                    x = {"k": 0, "q": 1}[what]
                    act.wait_ge(s.k_ps if x == 0 else s.q_ps, START + base + n + 1)
                    if not isinstance(n, int):
                        act.wait_ge(s.ss_done, START + 2 * (base + n) + x - 1)
                    elif n == 1:
                        act.wait_ge(s.ss_done, START + 2 * base + x + 1)
                    nc.scalar.activation(sq[:, x, :], (psB if x == 0 else psA)[:, :], ACT.Square).then_inc(s.sq_done, 1)

                def copy_out(number, half, dst):
                    act.wait_ge(s.tr_ps, START + number + 1)
                    nc.scalar.activation(dst, psC[:, half, :].rearrange("p (h t) -> p h t", t=P), ACT.Copy)\
                        .then_inc(s.tr_act, 1)

                def turn_out(n, u, what, last, dst):
                    number, half, i, order = turn(n, u, what, last)
                    copy_out(number, half, dst)

                def exponential(n):
                    act.wait_ge(s.sub_done, START + base + n + 1)
                    act.wait_ge(s.sum_done, START + base + n)
                    nc.scalar.activation(prob[:, :, :, :].rearrange("p h e j -> p e h j"),
                                         sc[:, :].rearrange("p (e h j) -> p e h j", e=2, j=2 * WIN), ACT.Exp,
                                         scale=QK_SCALE)\
                        .then_inc(s.exp_done, 1)

                def iteration(n, u, projecting, last):
                    if projecting:
                        value_out(n + 2, u)
                        square(n + 2, "k")
                    for g in range(2):
                        turn_out(n, u, f"p{g}", last, probT[:, 4 * g:4 * g + 4, :])
                    if projecting:
                        square(n + 2, "q")
                    if not last:
                        for g in range(2):
                            turn_out(n, u, f"k{g}", last, k.KT[:, 1 - u, 4 * g:4 * g + 4, WIN:WIN + P])
                        for g in range(2):
                            turn_out(n, u, f"q{g}", last, QT[:, 4 * g:4 * g + 4, :])
                    for g in range(2):
                        turn_out(n, u, f"o{g}", last, OT[:, 4 * g:4 * g + 4, :])
                    if not last:
                        exponential(n + 1)

                for n in range(2):
                    square(n, "k")
                    value_out(n, n)
                    square(n, "q")
                for g in range(2):
                    copy_out(layer * NTURN + g, g, k.KT[:, 0, 4 * g:4 * g + 4, WIN:WIN + P])
                for g in range(2):
                    copy_out(layer * NTURN + 2 + g, g, QT[:, 4 * g:4 * g + 4, :])
                exponential(0)
                with act.Fori(0, NT // 2 - 1) as tp:
                    for u in range(2):
                        iteration(2 * tp + u, u, True, False)
                iteration(NT - 2, 0, False, False)
                iteration(NT - 1, 1, False, True)

            CPT = 4

            @block.vector
            def _(dve):
                def shift(n, u):
                    at = n * P
                    nc.vector.tensor_copy(xs[0:64, u, :], m.xa[0:64, bass.ds(at + 1, P)])
                    nc.vector.tensor_copy(xs[64:P, u, 1:P], m.xa[64:P, bass.ds(at + 1, P - 1)])
                    nc.vector.tensor_scalar(xs[64:P, u, 0:1], m.xa[64:P, bass.ds(at, 1)],
                                            m.keep[64:P, bass.ds(n, 1)], None, ALU.mult).then_inc(s.xs_ready, 1)

                def rotate(n, u, what):
                    x = {"k": 0, "q": 1}[what]
                    src = (psB if x == 0 else psA)[:, :].rearrange("p (h c f) -> p h c f", c=2, f=DH // 2)
                    dve.wait_ge(s.sq_done, START + 2 * (base + n) + x + 1)
                    dve.wait_ge(s.khat_done, START + 2 * base + (2 * (n - 1) + x + 1 if not isinstance(n, int) or n >= 1
                                                            else 0))
                    table = m.rot[:, bass.ds(n, 1), :, :].rearrange("p n a f -> p (n a) f")
                    a = 2 * (1 - x)
                    cos = spread(table[:, a, :], 1, H)
                    sin = spread(table[:, a + 1, :].rearrange("p (c f) -> p c f", c=2), 1, H)
                    nc.vector.tensor_tensor(t1[:, x, :].rearrange("p (h f) -> p h f", f=DH),
                                            src.rearrange("p h c f -> p h (c f)"), cos, ALU.mult)
                    nc.vector.tensor_tensor(t2[:, x, :].rearrange("p (h c f) -> p h c f", c=2, f=DH // 2),
                                            src[:, :, ::-1, :], sin, ALU.mult).then_inc(s.rot_done, 1)

                def norms(n, what, link):
                    x = {"k": 0, "q": 1}[what]
                    link(n, nc.vector.tensor_reduce(ss[:, x, :], sq[:, x, :].rearrange("p (h f) -> p h f", f=DH), AX.X, ALU.add))
                    nc.vector.tensor_scalar(ss[:, x, :], ss[:, x, :], 1e-24, None, ALU.max).then_inc(s.ss_done, 1)

                def halo(n, u):
                    dve.wait_ge(s.tr_act, START + layer * NACT + 4 + 8 * n - 12)
                    dve.wait_ge(s.s_ps, START + base + n - 1)
                    nc.vector.tensor_scalar(k.KT[:, u, :, 0:WIN], k.KT[:, 1 - u, :, P:P + WIN],
                                            m.keep[:, bass.ds(n, 1)], None, ALU.mult).then_inc(s.halo_done, 1)

                def subtract_maximum(n, link):
                    dve.wait_ge(s.s_ps, START + base + n + 1)
                    scores = psD[:, :].rearrange("p (h j) -> p h j", j=2 * WIN)
                    link(n, nc.vector.tensor_reduce(mx[:, :], scores, AX.X, ALU.max))
                    dve.wait_ge(s.exp_done, START + base + n)
                    nc.vector.tensor_tensor(sc[:, :].rearrange("p (h j) -> p h j", j=2 * WIN), scores,
                                            spread(mx[:, :], 2, 2 * WIN), ALU.subtract).then_inc(s.sub_done, 1)

                def iteration(n, u, projecting, last):
                    counts = [0]
                    before = 7 + CPT * n - (2 if last else 0)

                    def link(_, ins):
                        ins.then_inc(s.dchain, 1)
                        counts[0] += 1
                        dve.wait_ge(s.dchain, START + layer * (CPT * NT + 2) + before + counts[0])

                    dve.wait_ge(s.exp_done, START + base + n + 1)
                    link(n, nc.vector.tensor_reduce(rs[:, :].rearrange("p (e h) -> p h e", e=2), prob[:, :, :, :],
                                                    AX.X, ALU.add))
                    nc.vector.reciprocal(rr[:, :], rs[:, :]).then_inc(s.sum_done, 1)
                    if projecting:
                        rotate(n + 2, u, "k")
                        norms(n + 2, "k", link)
                        shift(n + 3, 1 - u)
                    dve.wait_ge(s.sum_done, START + base + n + 1)
                    dve.wait_ge(s.o_ps, START + base + n + 3)
                    nc.vector.tensor_tensor(o[:, :, :, :].rearrange("p h e f -> p e h f"),
                                            psD[:, :].rearrange("p (e h f) -> p e h f", e=2, f=DH),
                                            spread(rr[:, :].rearrange("p (e h) -> p e h", e=2), 3, DH),
                                            ALU.mult).then_inc(s.norm_done, 1)
                    if projecting:
                        rotate(n + 2, u, "q")
                        norms(n + 2, "q", link)
                    if not last:
                        halo(n + 2, u)
                        subtract_maximum(n + 1, link)
                    number, half, _, _ = turn(n, u, "w", last)
                    dve.wait_ge(s.tr_ps, START + number + 1)
                    cols = bass.ds(n * P + 1, P)
                    nc.vector.tensor_tensor(m.xb[:, cols], m.xa[:, cols], psC[:, half, 0:P], ALU.add)\
                        .then_inc(s.res_done, 1)

                done = [0]

                def link0(n, ins):
                    ins.then_inc(s.dchain, 1)
                    done[0] += 1
                    dve.wait_ge(s.dchain, START + layer * (CPT * NT + 2) + done[0])

                for n in range(2):
                    shift(n, n)
                for x, what in enumerate("kq"):
                    rotate(0, 0, what)
                    norms(0, what, link0)
                    link0(0, nc.vector.tensor_tensor(t1[:, x, :], t1[:, x, :], t2[:, x, :], ALU.add))
                for x in range(2):
                    dve.wait_ge(s.pchain, START + 2 * (2 * base + x) + 2)
                    normed(nc.vector, 0, x)
                shift(2, 0)
                for what in "kq":
                    rotate(1, 1, what)
                    norms(1, what, link0)
                dve.wait_ge(s.tr_act, START + layer * NACT + 2)
                nc.vector.tensor_scalar(k.KT[:, 1, :, 0:WIN], k.KT[:, 0, :, P:P + WIN], m.keep[:, 1:2], None,
                                        ALU.mult).then_inc(s.halo_done, 1)
                subtract_maximum(0, link0)
                with dve.Fori(0, NT // 2 - 1) as tp:
                    for u in range(2):
                        iteration(2 * tp + u, u, True, False)
                iteration(NT - 2, 0, False, False)
                iteration(NT - 1, 1, False, True)

            @block.gpsimd
            def _(pool):
                def finish(n, u, what):
                    x = {"k": 0, "q": 1}[what]
                    count = 2 * (base + n) + x
                    pool.wait_ge(s.ss_done, START + count + 1)
                    nc.gpsimd.tensor_tensor(rn[:, x, :], ss[:, x, :], m.minus_half[:, 0:H], ALU.pow).then_inc(s.pchain, 1)
                    pool.wait_ge(s.rot_done, START + count + 1)
                    nc.gpsimd.tensor_tensor(t1[:, x, :], t1[:, x, :], t2[:, x, :], ALU.add).then_inc(s.pchain, 1)
                    pool.wait_ge(s.pchain, START + 2 * count + 2)
                    if not isinstance(n, int):
                        pool.wait_ge(s.tr_ps, START + layer * NTURN + 4 + 9 * (n - 2))
                    normed(nc.gpsimd, u, x)

                for x in range(2):
                    pool.wait_ge(s.ss_done, START + 2 * base + x + 1)
                    nc.gpsimd.tensor_tensor(rn[:, x, :], ss[:, x, :], m.minus_half[:, 0:H], ALU.pow)\
                        .then_inc(s.pchain, 2)
                for what in "kq":
                    finish(1, 1, what)
                with pool.Fori(1, NT // 2) as tp:
                    for u in range(2):
                        for what in "kq":
                            finish(2 * tp + u, u, what)


class GatedFfn:
    NAMES = "xs_ready f_ps stat_done rstd_done xn_ready b_ps xnT_ready ga_ps gelu_done h_done y_ps y_done rot_done dchain".split()

    def __init__(self, ctx, nc, k):
        sb, ps, sem = tensors(ctx, nc, "bf_")
        self.sems = [sem(name) for name in self.NAMES]
        (self.xs_ready, self.f_ps, self.stat_done, self.rstd_done, self.xn_ready, self.b_ps, self.xnT_ready,
         self.ga_ps, self.gelu_done, self.h_done, self.y_ps, self.y_done, self.rot_done, self.dchain) = self.sems

    def emit(self, nc, m, d, k, layer):
        with ExitStack() as ctx:
            sb, ps, _ = tensors(ctx, nc, "bg_")
            xs = sb("xs", [P, 2, CH])
            stats = sb("stats", [P, 4, 6])
            mv = sb("mv", [P, 4, 2])
            veps = sb("veps", [P, 4])
            rstd = sb("rstd", [P, 4])
            xn = sb("xn", [P, 4, D])
            xnT = sb("xnT", [P, 2, CH])
            gel = sb("gel", [P, 2, CH])
            h = sb("h", [P, 2, NF, CH])
            psF = ps("psF", [P, BANK])
            psR = ps("psR", [P, BANK])
            psG = ps("psG", [P, 2, 2, BANK])
            psY = ps("psY", [P, 2, BANK])
            s = self
            T = CH // P
            c0 = layer * NCH
            g0 = layer * (NCH * NF)
            ln_g, ln_b, b2 = (k.cols[:, i:i + 1] for i in range(3))
            block = ctx.enter_context(nc.Block())

            @block.sync
            def _(sp):
                sp.dma_start(k.w_qkv[:, :], d["b_wqkv"][bass.ds(layer + 1, 1)].rearrange("l d f -> (l d) f"))\
                    .then_inc(k.attn_in, 16)
                sp.dma_start(k.wo[:, :, :], d["b_wo"][bass.ds(layer + 1, 1)].rearrange("l p h d -> (l p) h d"))\
                    .then_inc(k.attn_in, 16)
            @block.tensor
            def _(pe):
                def forward(c):
                    pe.wait_ge(s.xs_ready, START + c0 + c + 1)
                    pe.wait_ge(s.xn_ready, START + c0 + c)
                    for j in range(T):
                        last = nc.tensor.transpose(psF[:, j * P:(j + 1) * P], xs[:, c % 2, j * P:(j + 1) * P], m.ident[:, :])
                    last.then_inc(s.f_ps, 1)

                def back(c):
                    pe.wait_ge(s.xn_ready, START + c0 + c + 1)
                    pe.wait_ge(s.xnT_ready, START + c0 + c)
                    for j in range(T):
                        last = nc.tensor.transpose(psR[:, j * P:(j + 1) * P], xn[:, j, :], m.ident[:, :])
                    last.then_inc(s.b_ps, 1)

                pe.wait_ge(k.ffn_in, START + (layer + 1) * 64)
                def gate_up(c, i):
                    f0, width = FFN_PARTS[i]
                    n = c * NF + i
                    if n >= 2:
                        pe.wait_ge(s.h_done, START + g0 + n - 1)
                    for gate in range(2):
                        last = nc.tensor.matmul(psG[0:width, n % 2, gate, :],
                                                k.w1[:, gate * FFN_IN + f0:gate * FFN_IN + f0 + width],
                                                xnT[:, c % 2, :], start=True, stop=True)
                    last.then_inc(s.ga_ps, 1)

                def down(c):
                    pe.wait_ge(s.h_done, START + g0 + (c + 1) * NF)
                    if c >= 2:
                        pe.wait_ge(s.y_done, START + c0 + c - 1)
                    for i, (f0, width) in enumerate(FFN_PARTS):
                        last = nc.tensor.matmul(psY[:, c % 2, :], k.w2[0:width, i, :], h[0:width, c % 2, i, :],
                                                start=i == 0, stop=i == NF - 1)
                    last.then_inc(s.y_ps, 1)

                forward(0)
                back(0)
                forward(1)
                for c in range(NCH):
                    pe.wait_ge(s.xnT_ready, START + c0 + c + 1)
                    gate_up(c, 0)
                    if c + 1 < NCH:
                        back(c + 1)
                    if c + 2 < NCH:
                        forward(c + 2)
                    if c >= 1:
                        down(c - 1)
                    for i in range(1, NF):
                        gate_up(c, i)
                down(NCH - 1)

            @block.scalar
            def _(act):
                def norm_out(c):
                    act.wait_ge(s.b_ps, START + c0 + c + 1)
                    nc.scalar.activation(xnT[:, c % 2, :], psR[:, :], ACT.Identity, scale=ln_g, bias=ln_b)\
                        .then_inc(s.xnT_ready, 1)

                act.wait_ge(k.ffn_in, START + (layer + 1) * 64)
                norm_out(0)
                for c in range(NCH):
                    for i, (f0, width) in enumerate(FFN_PARTS):
                        n = c * NF + i
                        act.wait_ge(s.ga_ps, START + g0 + n + 1)
                        if n >= 2:
                            act.wait_ge(s.h_done, START + g0 + n - 1)
                        nc.scalar.activation(gel[0:width, n % 2, :], psG[0:width, n % 2, 1, :], ACT.Gelu,
                                             bias=k.cols[0:width, 3 + NF + i:4 + NF + i]).then_inc(s.gelu_done, 1)
                        if i == 0 and c + 1 < NCH:
                            norm_out(c + 1)

            @block.vector
            def _(dve):
                def shift(c):
                    first = c * CH + 1
                    if c * CH % S == 0:
                        nc.vector.memset(xs[64:P, c % 2, 0:1], 0.0)
                    skip = 1 if c * CH % S == 0 else 0
                    nc.vector.tensor_copy(xs[64:P, c % 2, skip:CH], m.xb[64:P, first - 1 + skip:first + CH - 1])
                    nc.vector.tensor_copy(xs[0:64, c % 2, :], m.xb[0:64, first:first + CH]).then_inc(s.xs_ready, 1)

                def statistics(c):
                    chain = Chain(dve, s.dchain, START + layer * (2 * NCH) + 2 * c)
                    dve.wait_ge(s.f_ps, START + c0 + c + 1)
                    psx = psF[:, :].rearrange("p (t f) -> p t f", f=D)
                    for t in range(T):
                        last = nc.vector.bn_stats(stats[:, t, :], psx[:, t, :])
                    chain.link(last)
                    nc.vector.memset(veps[:, :], LN_EPS)
                    for t in range(T):
                        last = nc.vector.bn_aggr(mv[:, t, :], stats[:, t, :])
                    chain.link(last)
                    nc.vector.tensor_tensor(veps[:, :], veps[:, :], mv[:, :, 1], ALU.add).then_inc(s.stat_done, 1)

                def normalise(c):
                    if c >= 1:
                        dve.wait_ge(s.b_ps, START + c0 + c)
                    dve.wait_ge(s.rstd_done, START + c0 + c + 1)
                    for t in range(T):
                        last = nc.vector.tensor_scalar(xn[:, t, :], psF[:, t * P:(t + 1) * P], mv[:, t, 0:1],
                                                       rstd[:, t:t + 1], ALU.subtract, ALU.mult)
                    last.then_inc(s.xn_ready, 1)

                def gated(c, i):
                    f0, width = FFN_PARTS[i]
                    n = c * NF + i
                    dve.wait_ge(s.gelu_done, START + g0 + n + 1)
                    if i == 0 and c >= 2:
                        dve.wait_ge(s.y_ps, START + c0 + c - 1)
                    nc.vector.scalar_tensor_tensor(out=h[0:width, c % 2, i, :], in0=psG[0:width, n % 2, 0, :],
                                                   scalar=k.cols[0:width, 3 + i:4 + i], in1=gel[0:width, n % 2, :],
                                                   op0=ALU.add, op1=ALU.mult).then_inc(s.h_done, 1)

                def add_out(c):
                    dve.wait_ge(s.y_ps, START + c0 + c + 1)
                    cols = slice(1 + c * CH, 1 + (c + 1) * CH)
                    nc.vector.scalar_tensor_tensor(out=m.xa[:, cols], in0=psY[:, c % 2, :], scalar=b2,
                                                   in1=m.xb[:, cols], op0=ALU.add, op1=ALU.add).then_inc(s.y_done, 1)

                shift(0)
                dve.wait_ge(k.ffn_in, START + (layer + 1) * 64)
                statistics(0)
                shift(1)
                normalise(0)
                statistics(1)
                shift(2)
                normalise(1)
                for c in range(NCH):
                    gated(c, 0)
                    if c + 2 < NCH:
                        statistics(c + 2)
                    gated(c, 1)
                    if c + 2 < NCH:
                        normalise(c + 2)
                    if c + 3 < NCH:
                        shift(c + 3)
                    if c >= 1:
                        add_out(c - 1)
                    gated(c, 2)
                add_out(NCH - 1)

            @block.gpsimd
            def _(pool):
                for c in range(NCH):
                    pool.wait_ge(s.stat_done, START + c0 + c + 1)
                    nc.gpsimd.tensor_tensor(rstd[:, :], veps[:, :], m.minus_half[:, 0:T], ALU.pow)\
                        .then_inc(s.rstd_done, 1)
                pool.wait_ge(k.ffn_in, START + (layer + 1) * 64)
                for b in range(B):
                    nc.gpsimd.tensor_tensor(m.rot[:, b * 8:b * 8 + 8, :, :], m.rot_base[:, :, :, :],
                                            spread(m.rot_scale[:, :, :], 1, 8), ALU.mult).then_inc(s.rot_done, 1)


def second_norm(nc, m, d):
    with ExitStack() as ctx:
        sb, ps, sem = tensors(ctx, nc, "n1_")
        stats = sb("stats", [P, NT, 6])
        mv = sb("mv", [P, NT, 2])
        eps_sum = sb("eps_sum", [P, NT])
        rstd = sb("rstd", [P, NT])
        ms = sb("ms", [P, NT])
        rrms = sb("rrms", [P, NT])
        xn = sb("xn", [P, NT, D])
        xr = sb("xr", [P, NT, D])
        router_w = sb("router_w", [D, E])
        bias = sb("bias", [P, E])
        norm_w = sb("norm_w", [D, 1])
        lower = sb("lower", [P, E, E])
        score = sb("score", [P, NT, E])
        s = sb("s", [P, NT, E])
        pair_max = sb("pair_max", [P, NT * GROUPS, 2])
        pair_min = sb("pair_min", [P, NT * GROUPS, 2])
        top = sb("top", [P, NT * GROUPS])
        second = sb("second", [P, NT * GROUPS])
        gscore = sb("gscore", [P, NT, GROUPS])
        above = sb("above", [P, NT * E * E])
        equal = sb("equal", [P, NT * E * E])
        rank = sb("rank", [P, NT * E])
        gsel = sb("gsel", [P, NT, GROUPS])
        gout = sb("gout", [P, NT, GROUPS])
        masked = sb("masked", [P, NT, E])
        wsum = sb("wsum", [P, NT])
        psX = ps("psX", [P, 4, BANK])
        psN = ps("psN", [P, 2, BANK])
        psL = ps("psL", [P, NT, E])
        names = "in_ dchain x_ps x_ready stat_done pow_done xn_ready n_ps n_ready logits_ps score_done".split()
        in_, dchain, x_ps, x_ready, stat_done, pow_done, xn_ready, n_ps, n_ready, logits_ps, score_done = map(sem, names)
        block = ctx.enter_context(nc.Block())
        T4 = CH // P

        @block.sync
        def _(sp):
            sp.dma_start(router_w[:, :], d["router_w"]).then_inc(in_, 16)
            sp.dma_start(bias[:, :], d["router_bias"].partition_broadcast(P)).then_inc(in_, 16)
            sp.dma_start(norm_w[:, :], d["c_norm_w"]).then_inc(in_, 16)
            sp.dma_start(lower[:, :, :].rearrange("p a b -> p (a b)"),
                         d["lower"].rearrange("a b -> (a b)").partition_broadcast(P)).then_inc(in_, 16)
            sp.wait_ge(in_, 64)

        @block.tensor
        def _(pe):
            pe.wait_ge(dchain, 1)
            for t in range(NT):
                nc.tensor.transpose(psX[:, t // 4, (t % 4) * P:(t % 4 + 1) * P],
                                    m.branchT[:, t * P:(t + 1) * P], m.ident[:, :]).then_inc(x_ps, 1)
            for i in range(2 * NCH):
                src = (xn, xr)[i // NCH]
                pe.wait_ge(xn_ready, i // NCH + 1)
                if i >= 2:
                    pe.wait_ge(n_ready, i - 1)
                for j in range(T4):
                    last = nc.tensor.transpose(psN[:, i % 2, j * P:(j + 1) * P], src[:, (i % NCH) * T4 + j, :],
                                               m.ident[:, :])
                last.then_inc(n_ps, 1)
            pe.wait_ge(n_ready, NCH)
            pe.wait_ge(in_, 64)
            for t in range(NT):
                last = nc.tensor.matmul(psL[:, t, :], m.xnT[:, t * P:(t + 1) * P], router_w[:, :], start=True, stop=True)
            last.then_inc(logits_ps, 1)

        @block.scalar
        def _(act):
            act.wait_ge(in_, 64)
            for i in range(2 * NCH):
                act.wait_ge(n_ps, i + 1)
                cols = slice((i % NCH) * CH, (i % NCH + 1) * CH)
                if i < NCH:
                    nc.scalar.activation(m.xnT[:, cols], psN[:, i % 2, :], ACT.Copy).then_inc(n_ready, 1)
                else:
                    nc.scalar.activation(m.xrT[:, cols], psN[:, i % 2, :], ACT.Copy, scale=norm_w[:, 0:1])\
                        .then_inc(n_ready, 1)
            act.wait_ge(logits_ps, 1)
            nc.scalar.activation(score[:, :, :], psL[:, :, :], ACT.Sigmoid).then_inc(score_done, 1)

        @block.gpsimd
        def _(pool):
            for i, out in enumerate((rstd, rrms)):
                pool.wait_ge(stat_done, i + 1)
                nc.gpsimd.tensor_tensor(out[:, :], eps_sum[:, :], m.minus_half[:, 0:NT], ALU.pow).then_inc(pow_done, 1)

        @block.vector
        def _(dve):
            chain = Chain(dve, dchain)
            v = nc.vector
            chain.link(v.tensor_tensor(m.branchT[:, :], m.branchT[:, :], m.xa[:, 1:1 + N], ALU.add))
            for c in range(NCH):
                dve.wait_ge(x_ps, T4 * (c + 1))
                tiles = slice(T4 * c, T4 * (c + 1))
                last = v.tensor_tensor(m.x[:, tiles, :], m.x[:, tiles, :],
                                       psX[:, c, :].rearrange("p (t f) -> p t f", f=D), ALU.add)
            chain.link(last)
            norm_statistics(nc, dve, chain.link, m.x, stats, mv, NT)
            v.tensor_scalar(eps_sum[:, :], mv[:, :, 1], LN_EPS, None, ALU.add).then_inc(stat_done, 1)
            dve.wait_ge(pow_done, 1)
            for t in range(NT):
                last = v.tensor_scalar(xn[:, t, :], m.x[:, t, :], mv[:, t, 0:1], rstd[:, t:t + 1],
                                       ALU.subtract, ALU.mult)
            last.then_inc(xn_ready, 1)
            dve.wait_ge(xn_ready, 1)
            chain.link(v.tensor_tensor(xr[:, :, :], xn[:, :, :], xn[:, :, :], ALU.mult))
            chain.link(v.tensor_reduce(ms[:, :], xr[:, :, :], AX.X, ALU.add))
            v.tensor_scalar(eps_sum[:, :], ms[:, :], 1.0 / D, RMS_EPS, ALU.mult, ALU.add).then_inc(stat_done, 1)
            dve.wait_ge(pow_done, 2)
            v.tensor_tensor(xr[:, :, :], xn[:, :, :], spread(rrms[:, :], 2, D), ALU.mult).then_inc(xn_ready, 1)

            def ranks(x, n):
                big = [P, NT, n, n]
                a = above[:, 0:NT * n * n].rearrange("p (t i j) -> p t i j", i=n, j=n)
                q = equal[:, 0:NT * n * n].rearrange("p (t i j) -> p t i j", i=n, j=n)
                mine, other = spread(x, 3, n), spread(x, 2, n)
                v.tensor_tensor(a, other, mine, ALU.is_gt)
                chain.link(v.tensor_tensor(q, other, mine, ALU.is_equal))
                chain.link(v.tensor_tensor(q, q, spread(lower[:, 0:n, 0:n], 1, NT), ALU.mult))
                chain.link(v.tensor_tensor(a, a, q, ALU.add))
                chain.link(v.tensor_reduce(rank[:, 0:NT * n].rearrange("p (t i) -> p t i", i=n), a, AX.X, ALU.add))

            dve.wait_ge(in_, 64)
            dve.wait_ge(score_done, 1)
            chain.link(v.tensor_tensor(s[:, :, :], score[:, :, :], spread(bias[:, :], 1, NT), ALU.add))
            by_pair = s[:, :, :].rearrange("p t (g c a) -> p (t g) c a", g=GROUPS, a=2)
            v.tensor_tensor(pair_max[:, :, :], by_pair[:, :, :, 0], by_pair[:, :, :, 1], ALU.max)
            chain.link(v.tensor_tensor(pair_min[:, :, :], by_pair[:, :, :, 0], by_pair[:, :, :, 1], ALU.min))
            v.tensor_tensor(top[:, :], pair_max[:, :, 0], pair_max[:, :, 1], ALU.max)
            v.tensor_tensor(second[:, :], pair_max[:, :, 0], pair_max[:, :, 1], ALU.min)
            chain.link(v.tensor_tensor(pair_min[:, :, 0], pair_min[:, :, 0], pair_min[:, :, 1], ALU.max))
            chain.link(v.tensor_tensor(second[:, :], second[:, :], pair_min[:, :, 0], ALU.max))
            chain.link(v.tensor_tensor(gscore[:, :, :].rearrange("p t g -> p (t g)"), top[:, :], second[:, :], ALU.add))
            ranks(gscore[:, :, :], GROUPS)
            rank_g = rank[:, 0:NT * GROUPS].rearrange("p (t i) -> p t i", i=GROUPS)
            chain.link(v.tensor_scalar(gsel[:, :, :], rank_g, float(TOP_GROUPS), None, ALU.is_lt))
            chain.link(v.tensor_scalar(gout[:, :, :], gsel[:, :, :], -1.0, None, ALU.add))
            by_group = masked[:, :, :].rearrange("p t (g c) -> p (t g) c", g=GROUPS)
            flat = gsel[:, :, :].rearrange("p t g -> p (t g)"), gout[:, :, :].rearrange("p t g -> p (t g)")
            chain.link(v.tensor_tensor(by_group, s[:, :, :].rearrange("p t (g c) -> p (t g) c", g=GROUPS),
                                       spread(flat[0], 2, E // GROUPS), ALU.mult))
            chain.link(v.tensor_tensor(by_group, by_group, spread(flat[1], 2, E // GROUPS), ALU.add))
            ranks(masked[:, :, :], E)
            chain.link(v.tensor_scalar(masked[:, :, :], rank[:, :].rearrange("p (t i) -> p t i", i=E), float(TOP_K),
                                       None, ALU.is_lt))
            chain.link(v.tensor_tensor(masked[:, :, :], masked[:, :, :], score[:, :, :], ALU.mult))
            chain.link(v.tensor_reduce(wsum[:, :], masked[:, :, :], AX.X, ALU.add))
            chain.link(v.tensor_scalar(wsum[:, :], wsum[:, :], 1e-20, None, ALU.add))
            chain.link(v.reciprocal(wsum[:, :], wsum[:, :]))
            chain.link(v.tensor_scalar(wsum[:, :], wsum[:, :], ROUTE_SCALE, None, ALU.mult))
            v.tensor_tensor(m.combine[:, 0:E, :].rearrange("p e t -> p t e"), masked[:, :, :],
                            spread(wsum[:, :], 2, E), ALU.mult)
            v.memset(m.combine[:, E:NE, :], 1.0)


def capped_attention(nc, m, d):
    TB = S // P
    NS = B * TB * 2
    NJ = NS // 2
    with ExitStack() as ctx:
        sb, ps, sem = tensors(ctx, nc, "c_")
        gamma = sb("gamma", [P, PAIRS + 1, 2])
        factor = sb("factor", [P, PAIRS + 1, 2])
        fac = sb("fac", [P, 2])
        w = sb("w", [P, 3 * P])
        wo = sb("wo", [P, D])
        raw = sb("raw", [P, NT, 3 * P])
        sq = sb("sq", [P, 4, 2 * P])
        ss = sb("ss", [P, NT, 4])
        rn = sb("rn", [P, NT, 4])
        QT = sb("QT", [P, N])
        KT = sb("KT", [P, N])
        th = sb("th", [P, 4, S])
        prob = sb("prob", [P, 4, S])
        acc = sb("acc", [P, 2, S])
        rec = sb("rec", [P, 2, BANK])
        OT = sb("OT", [P, S])
        psS = ps("psS", [P, 2, S])
        psO = ps("psO", [P, S])
        psL = ps("psL", [P, BANK])
        psW = ps("psW", [P, BANK])
        names = ("g_in w_in wo_in proj_ps raw_ready ss_done rn_done hat_done h_ps q_ready k_ready st_ps tanh_done "
                 "exp_done acc_done pv_ps sum_ps rec_done ot_ready wo_ps add_done dchain factor_done").split()
        (g_in, w_in, wo_in, proj_ps, raw_ready, ss_done, rn_done, hat_done, h_ps, q_ready, k_ready, st_ps, tanh_done,
         exp_done, acc_done, pv_ps, sum_ps, rec_done, ot_ready, wo_ps, add_done, dchain, factor_done) = sems = \
            [sem(name) for name in names]
        start_semaphores(nc, m, sems)
        block = ctx.enter_context(nc.Block())

        def prepared(g, b):
            return 2 * g + 1 + b, (1 - b) * TB

        EARLY = {2: [0, 1], 3: [4, 5]}
        LATE = {2: [2, 3], 3: [6, 7]}
        SHIFT = 2

        @block.sync
        def _(sp):
            sp.dma_start(gamma[:, :, :], d["c_gamma"].rearrange("a p x -> p a x")).then_inc(g_in, 16)
            sp.dma_start(w[:, :], d["c_wqkv"][0].rearrange("d x f -> d (x f)")).then_inc(w_in, 16)
            with sp.Fori(0, PAIRS) as g:
                sp.wait_ge(wo_ps, START + g * 2 * B)
                sp.dma_start(wo[:, :], d["c_wo"][bass.ds(g, 1)].rearrange("g f d -> (g f) d")).then_inc(wo_in, 16)
                sp.wait_ge(proj_ps, START + (g + 1) * NT)
                sp.dma_start(w[:, :], d["c_wqkv"][bass.ds(g + 1, 1)].rearrange("g d x f -> (g d) (x f)"))\
                    .then_inc(w_in, 16)
            sp.wait_ge(g_in, START + 16)
            sp.wait_ge(w_in, START + (PAIRS + 1) * 16)
            sp.wait_ge(wo_in, START + PAIRS * 16)

        @block.tensor
        def _(pe):
            def scores(g, s):
                b, kt, e = s % NS // (2 * TB), s // 2 % TB, s % 2
                if s % (2 * TB) == 0:
                    half = 2 * g + s // (2 * TB)
                    pe.wait_ge(q_ready, START + 2 * half + 2)
                    pe.wait_ge(k_ready, START + 2 * half + 1)
                pe.wait_ge(tanh_done, START + g * NS + s - 1)
                h = slice(64 * e, 64 * e + 64)
                for c in range(2):
                    last = nc.tensor.matmul(psS[:, e, c * BANK:(c + 1) * BANK],
                                            KT[h, b * S + kt * P:b * S + (kt + 1) * P],
                                            QT[h, b * S + c * BANK:b * S + (c + 1) * BANK], start=True, stop=True)
                last.then_inc(st_ps, 1)

            def values(g, j):
                b, kt = j // TB % B, j % TB
                pe.wait_ge(exp_done, START + g * NS + 2 * j + 2)
                if kt == 0:
                    pe.wait_ge(ot_ready, START + g * 2 * B + 2 * (j // TB))
                for c in range(2):
                    for e in range(2):
                        last = nc.tensor.matmul(psO[64 * e:64 * e + 64, c * BANK:(c + 1) * BANK],
                                                raw[:, b * TB + kt, 2 * P + 64 * e:2 * P + 64 * e + 64],
                                                prob[:, (2 * j + e) % 4, c * BANK:(c + 1) * BANK],
                                                start=kt == 0, stop=kt == TB - 1)
                last.then_inc(pv_ps, 1)

            def sums(g, b):
                half, _ = prepared(g, b)
                pe.wait_ge(k_ready, START + 2 * half + 2)
                pe.wait_ge(acc_done, START + g * NS + (b + 1) * 2 * TB)
                for c, out in enumerate((psL, psW)):
                    for e in range(2):
                        last = nc.tensor.matmul(out[64 * e:64 * e + 64, :], m.ones[:, 0:64],
                                                acc[:, e, c * BANK:(c + 1) * BANK], start=True, stop=True)
                    last.then_inc(sum_ps, 1)

            def project_out(g, b):
                if b == 0:
                    pe.wait_ge(wo_in, START + (g + 1) * 16)
                for c, out in enumerate((psL, psW)):
                    pe.wait_ge(ot_ready, START + g * 2 * B + 2 * b + c + 1)
                    for t in range(4):
                        last = nc.tensor.matmul(out[:, t * P:(t + 1) * P], OT[:, (4 * c + t) * P:(4 * c + t + 1) * P],
                                                wo[:, :], start=True, stop=True)
                    last.then_inc(wo_ps, 1)

            def project_in(g, b, t):
                half, first = prepared(g, b)
                if t == 0:
                    pe.wait_ge(k_ready, START + 2 * half)
                    pe.wait_ge(add_done, START + 2 * (half - 1))
                    if b == 1:
                        pe.wait_ge(w_in, START + (g + 2) * 16)
                if t >= 2:
                    pe.wait_ge(raw_ready, START + TB * half + t - 1)
                nc.tensor.matmul((psW, psL)[t % 2][:, 0:3 * P], m.xrT[:, (first + t) * P:(first + t + 1) * P], w[:, :],
                                 start=True, stop=True).then_inc(proj_ps, 1)

            def transposes(g, b, i, x):
                half, first = prepared(g, b)
                pe.wait_ge(hat_done, START + 2 * half + i + 1)
                if i == 0:
                    pe.wait_ge(raw_ready, START + TB * (half + 1))
                else:
                    pe.wait_ge((q_ready, k_ready)[x], START + 2 * half + 1)
                for t in range(4):
                    last = nc.tensor.transpose((psW, psL)[x][:, t * P:(t + 1) * P],
                                               raw[:, first + 4 * i + t, x * P:(x + 1) * P], m.ident[:, :])
                last.then_inc(h_ps, 1)

            for t in range(TB):
                project_in(-1, 1, t)
            for i in range(2):
                for x in range(2):
                    transposes(-1, 1, i, x)
            scores(0, 0)
            scores(0, 1)

            def key_tile(g, j, start):
                b, kt = j // TB, j % TB
                scores(g, 2 * j + 2)
                for t in EARLY.get(kt, []):
                    project_in(g, b, t)
                if kt == TB - 2:
                    transposes(g, b, 1, 0)
                if kt == 1 and not start:
                    project_out(g, b - 1)
                if kt >= 1:
                    values(g, j - 1)
                scores(g, 2 * j + 3)
                for t in LATE.get(kt, []):
                    project_in(g, b, t)
                if kt == TB - 4:
                    transposes(g, b, 0, 0)
                    transposes(g, b, 0, 1)
                if kt == TB - 2:
                    transposes(g, b, 1, 1)
                if kt == TB - 1:
                    sums(g, b)
                    values(g, j)

            for j in range(SHIFT):
                key_tile(0, j, True)
            with pe.Fori(0, PAIRS) as g:
                for j in range(SHIFT, NJ + SHIFT):
                    key_tile(g, j, False)
            for c in range(2):
                for e in range(2):
                    nc.tensor.matmul(psO[64 * e:64 * e + 64, c * BANK:(c + 1) * BANK], m.identb[:, 0:64],
                                     m.band[:, 0:BANK // (2 * WIN), :], start=False, stop=True)

        @block.scalar
        def _(act):
            def tanh(g, s):
                act.wait_ge(st_ps, START + g * NS + s + 1)
                act.wait_ge(exp_done, START + g * NS + s - 3)
                nc.scalar.activation(th[:, s % 4, :], psS[:, s % 2, :], ACT.Tanh, scale=1.0 / SOFTCLAMP)\
                    .then_inc(tanh_done, 1)

            def exponential(g, s):
                act.wait_ge(tanh_done, START + g * NS + s + 1)
                act.wait_ge(pv_ps, START + g * NJ + (s - 4) // 2 + 1)
                act.wait_ge(acc_done, START + g * NS + s - 3)
                nc.scalar.activation(prob[:, s % 4, :], th[:, s % 4, :], ACT.Exp,
                                     scale=SOFTCLAMP * DH ** -0.5).then_inc(exp_done, 1)

            def raw_out(g, b, t):
                half, first = prepared(g, b)
                act.wait_ge(proj_ps, START + TB * half + t + 1)
                nc.scalar.activation(raw[:, first + t, :], (psW, psL)[t % 2][:, 0:3 * P], ACT.Copy)\
                    .then_inc(raw_ready, 1)

            def q_out(g, b, i):
                half, first = prepared(g, b)
                if i == 0 and b == 1:
                    act.wait_ge(factor_done, START + g + 3)
                act.wait_ge(h_ps, START + 4 * half + (1, 3)[i])
                nc.scalar.activation(QT[:, (first + 4 * i) * P:(first + 4 * i + 4) * P], psW[:, :], ACT.Copy,
                                     scale=fac[:, 0:1]).then_inc(q_ready, 1)

            for t in range(TB):
                raw_out(-1, 1, t)
            q_out(-1, 1, 0)
            q_out(-1, 1, 1)
            tanh(0, 0)
            tanh(0, 1)
            exponential(0, 0)

            def key_tile(g, j):
                b, kt = j // TB, j % TB
                if kt == TB - 3:
                    q_out(g, b, 0)
                tanh(g, 2 * j + 2)
                exponential(g, 2 * j + 1)
                for t in EARLY.get(kt, []):
                    raw_out(g, b, t)
                if kt == TB - 2:
                    q_out(g, b, 1)
                tanh(g, 2 * j + 3)
                exponential(g, 2 * j + 2)
                for t in LATE.get(kt, []):
                    raw_out(g, b, t)

            for j in range(SHIFT):
                key_tile(0, j)
            with act.Fori(0, PAIRS) as g:
                for j in range(SHIFT, NJ + SHIFT):
                    key_tile(g, j)

        @block.gpsimd
        def _(pool):
            def norms(g, b, i):
                half, first = prepared(g, b)
                pool.wait_ge(ss_done, START + 2 * half + i + 1)
                tiles = slice(first + 4 * i, first + 4 * i + 4)
                nc.gpsimd.tensor_tensor(rn[:, tiles, :], ss[:, tiles, :],
                                        m.minus_half[:, 0:16].rearrange("p (t h) -> p t h", h=4), ALU.pow)\
                    .then_inc(rn_done, 1)

            for i in range(2):
                norms(-1, 1, i)
            with pool.Fori(0, PAIRS) as g:
                for b in range(B):
                    for i in range(2):
                        norms(g, b, i)

        @block.vector
        def _(dve):
            v = nc.vector

            def squares(g, b, i):
                half, first = prepared(g, b)
                chain = Chain(dve, dchain, START + 4 * half + 2 * i)
                tiles = slice(first + 4 * i, first + 4 * i + 4)
                dve.wait_ge(raw_ready, START + TB * half + 4 * i + 4)
                qk = raw[:, tiles, 0:2 * P]
                chain.link(v.tensor_tensor(sq[:, :, :], qk, qk, ALU.mult))
                chain.link(v.tensor_reduce(ss[:, tiles, :], sq[:, :, :].rearrange("p t (h f) -> p t h f", f=DH),
                                           AX.X, ALU.add))
                v.tensor_scalar(ss[:, tiles, :], ss[:, tiles, :], 1e-24, None, ALU.max).then_inc(ss_done, 1)

            def normed(g, b, i):
                half, first = prepared(g, b)
                tiles = slice(first + 4 * i, first + 4 * i + 4)
                dve.wait_ge(rn_done, START + 2 * half + i + 1)
                heads = raw[:, tiles, 0:2 * P].rearrange("p t (h f) -> p t h f", f=DH)
                v.tensor_tensor(heads, heads, spread(rn[:, tiles, :], 3, DH), ALU.mult).then_inc(hat_done, 1)

            def factors(g):
                dve.wait_ge(q_ready, START + 4 * (g + 1))
                v.tensor_copy(fac[:, :], factor[:, bass.ds(g + 1, 1), :].rearrange("p g x -> p (g x)"))\
                    .then_inc(factor_done, 1)

            def k_out(g, b, i):
                half, first = prepared(g, b)
                if i == 0 and b == 1:
                    dve.wait_ge(factor_done, START + g + 3)
                dve.wait_ge(h_ps, START + 4 * half + (2, 4)[i])
                v.tensor_scalar(KT[:, (first + 4 * i) * P:(first + 4 * i + 4) * P], psL[:, :], fac[:, 1:2], None,
                                ALU.mult).then_inc(k_ready, 1)

            def accumulate(g, s):
                kt, e = s // 2 % TB, s % 2
                dve.wait_ge(exp_done, START + g * NS + s + 1)
                if kt == 0:
                    dve.wait_ge(sum_ps, START + g * 2 * B + s // (2 * TB) * 2)
                    v.tensor_copy(acc[:, e, :], prob[:, s % 4, :]).then_inc(acc_done, 1)
                else:
                    dve.wait_ge(acc_done, START + g * NS + s - 1)
                    v.tensor_tensor(acc[:, e, :], acc[:, e, :], prob[:, s % 4, :], ALU.add).then_inc(acc_done, 1)

            def divide(g, b):
                first = START + g * 2 * B + 2 * b
                for c, sums in enumerate((psL, psW)):
                    dve.wait_ge(sum_ps, first + c + 1)
                    v.reciprocal(rec[:, c, :], sums[:, :]).then_inc(rec_done, 1)
                dve.wait_ge(wo_ps, first)
                dve.wait_ge(pv_ps, START + g * NJ + (b + 1) * TB)
                for c in range(2):
                    dve.wait_ge(rec_done, first + c + 1)
                    v.tensor_tensor(OT[:, c * BANK:(c + 1) * BANK], psO[:, c * BANK:(c + 1) * BANK],
                                    rec[:, c, :], ALU.mult).then_inc(ot_ready, 1)

            def add_out(g, b):
                for c, out in enumerate((psL, psW)):
                    dve.wait_ge(wo_ps, START + g * 2 * B + 2 * b + c + 1)
                    tiles = slice(b * TB + 4 * c, b * TB + 4 * c + 4)
                    v.tensor_tensor(m.x[:, tiles, :], m.x[:, tiles, :],
                                    out[:, :].rearrange("p (t f) -> p t f", f=D), ALU.add).then_inc(add_done, 1)

            dve.wait_ge(g_in, START + 16)
            v.tensor_scalar(factor[:, :, :], gamma[:, :, :], 1.0, DH ** 0.5, ALU.add, ALU.mult).then_inc(factor_done, 1)
            dve.wait_ge(factor_done, START + 1)
            v.tensor_copy(fac[:, :], factor[:, 0, :]).then_inc(factor_done, 1)
            for i in range(2):
                squares(-1, 1, i)
            for i in range(2):
                normed(-1, 1, i)
            for i in range(2):
                k_out(-1, 1, i)
            accumulate(0, 0)

            def key_tile(g, j, start):
                b, kt = j // TB, j % TB
                if kt == 3:
                    squares(g, b, 0)
                if kt == 4:
                    normed(g, b, 0)
                    squares(g, b, 1)
                if kt == 5:
                    normed(g, b, 1)
                    k_out(g, b, 0)
                if kt == 7:
                    k_out(g, b, 1)
                accumulate(g, 2 * j + 1)
                if kt == TB - 1:
                    divide(g, b)
                accumulate(g, 2 * j + 2)
                if kt == 1 and not start:
                    add_out(g, b - 1)
                if j == TB:
                    factors(g)

            for j in range(SHIFT):
                key_tile(0, j, True)
            with dve.Fori(0, PAIRS) as g:
                for j in range(SHIFT, NJ + SHIFT):
                    key_tile(g, j, False)


def experts(nc, m, d, out):
    with ExitStack() as ctx:
        sb, ps, sem = tensors(ctx, nc, "e_")
        w_gu = sb("w_gu", [D, 2, 2, F])
        w_down = sb("w_down", [F, 2, D])
        weight = sb("weight", [P, 2, NT])
        sg = sb("sg", [F, 2, CH])
        hT = sb("hT", [F, 2, CH])
        psG = ps("psG", [P, 2, BANK])
        psU = ps("psU", [P, 2, BANK])
        psY = ps("psY", [P, 2, BANK])
        names = "w_in_even w_in_odd gu_ps silu_done h_done y_ps y_done weight_done out_done".split()
        w_in_even, w_in_odd, gu_ps, silu_done, h_done, y_ps, y_done, weight_done, out_done = sems = [sem(name) for name in names]
        start_semaphores(nc, m, sems)
        w_in = (w_in_even, w_in_odd)
        block = ctx.enter_context(nc.Block())
        PER = 2 * NCH

        @block.sync
        def _(sp):
            def load(i, u):
                e = 2 * i + u
                sp.dma_start(w_gu[:, u, :, :], d["e_gate_up"][bass.ds(e, 1)].rearrange("e d x f -> (e d) x f"))\
                    .then_inc(w_in[u], 16)
                sp.dma_start(w_down[:, u, :], d["e_down"][bass.ds(e, 1)].rearrange("e f d -> (e f) d"))\
                    .then_inc(w_in[u], 16)
            load(0, 0)
            load(0, 1)
            with sp.Fori(1, NE // 2) as i:
                for u in range(2):
                    sp.wait_ge(y_ps, START + PER * i + NCH * (u - 1))
                    load(i, u)
            rows = out.rearrange("(t p) d -> p t d", p=P)
            for c in range(NCH):
                sp.wait_ge(y_done, START + (NE - 1) * NCH + c + 1)
                sp.dma_start(rows[:, 4 * c:4 * c + 4, :], m.x[:, 4 * c:4 * c + 4, :]).then_inc(out_done, 16)
            sp.wait_ge(out_done, START + NCH * 16)

        @block.tensor
        def _(pe):
            def gate_up(i, c):
                u = c // NCH
                if c % NCH == 0:
                    pe.wait_ge(w_in[u], START + (i + 1) * 32)
                if c >= 2:
                    pe.wait_ge(h_done, START + PER * i + c - 1)
                for x, dst in enumerate((psG, psU)):
                    last = nc.tensor.matmul(dst[:, c % 2, :], w_gu[:, u, x, :],
                                            m.xnT[:, (c % NCH) * CH:(c % NCH + 1) * CH], start=True, stop=True)
                last.then_inc(gu_ps, 1)

            def down(i, c):
                pe.wait_ge(h_done, START + PER * i + c + 1)
                pe.wait_ge(y_done, START + PER * i + max(0, c - 1))
                for t in range(4):
                    last = nc.tensor.matmul(psY[:, c % 2, t * P:(t + 1) * P], hT[:, c % 2, t * P:(t + 1) * P],
                                            w_down[:, c // NCH, :], start=True, stop=True)
                last.then_inc(y_ps, 1)

            with pe.Fori(0, NE // 2) as i:
                for c in range(PER):
                    gate_up(i, c)
                    if c >= 1:
                        down(i, c - 1)
                down(i, PER - 1)

        @block.scalar
        def _(act):
            with act.Fori(0, NE // 2) as i:
                for c in range(PER):
                    act.wait_ge(gu_ps, START + PER * i + c + 1)
                    nc.scalar.activation(sg[:, c % 2, :], psG[:, c % 2, :], ACT.Silu).then_inc(silu_done, 1)

        @block.vector
        def _(dve):
            v = nc.vector

            def add(i, c):
                dve.wait_ge(y_ps, START + PER * i + c + 1)
                for t in range(4):
                    tile = (c % NCH) * 4 + t
                    last = v.scalar_tensor_tensor(out=m.x[:, tile, :], in0=psY[:, c % 2, t * P:(t + 1) * P],
                                                  scalar=weight[:, c // NCH, tile:tile + 1], in1=m.x[:, tile, :],
                                                  op0=ALU.mult, op1=ALU.add)
                last.then_inc(y_done, 1)

            with dve.Fori(0, NE // 2) as i:
                dve.wait_ge(y_done, START + PER * i)
                for u in range(2):
                    v.tensor_copy(weight[:, u, :], m.combine[:, bass.ds(2 * i + u, 1), :].rearrange("p e t -> p (e t)"))\
                        .then_inc(weight_done, 1)
                dve.wait_ge(weight_done, START + 2 * i + 2)
                for c in range(PER):
                    dve.wait_ge(silu_done, START + PER * i + c + 1)
                    if c >= 2:
                        dve.wait_ge(y_ps, START + PER * i + c - 1)
                    v.tensor_tensor(hT[:, c % 2, :], psU[:, c % 2, :], sg[:, c % 2, :], ALU.mult).then_inc(h_done, 1)
                    if c >= 1:
                        add(i, c - 1)
                add(i, PER - 1)


def persistent(ctx, nc):
    sb, _, _ = tensors(ctx, nc, "")
    m = Memory()
    m.x = sb("x", [P, NT, D])
    m.xnT = sb("xnT", [P, N])
    m.xa = sb("xaT", [P, 1 + N + P])
    m.xb = sb("xbT", [P, 1 + N])
    m.branchT = sb("branchT", [P, N])
    m.ident = sb("ident", [P, P])
    m.identb = sb("identb", [P, P], BF16)
    m.causal = sb("causal", [P, P], BF16)
    m.band = sb("band", [P, NT, 2 * WIN], BF16)
    m.keep = sb("keep", [P, NT + 1])
    m.ones = sb("ones", [P, P])
    m.minus_half = sb("minus_half", [P, 4 * NT])
    m.rot_base = sb("rot_base", [P, S // P, 4, DH])
    m.rot_scale = sb("rot_scale", [P, 4, DH])
    m.rot = sb("rot", [P, NT, 4, DH])
    m.xrT = m.xb[:, 1:]
    m.scratch = sb("scratch", [P, 64])
    m.combine = sb("combine", [P, NE, NT])
    return m


def shape_constants():
    i, j = np.arange(P)[:, None], np.arange(P)[None, :]
    c = {"ident": np.eye(P, dtype=np.float32), 
         "causal": np.where(j > i, NEG, 0.0).astype(np.float32)}
    q, k = np.arange(P)[:, None] % WIN, np.arange(2 * WIN)[None, :]
    band = np.where((k >= q) & (k <= q + WIN), 0.0, NEG)
    band = np.repeat(band[:, None, :], NT, axis=1)
    for t in range(0, NT, S // P):
        band[0:WIN, t, 0:WIN] = NEG
    c["band"] = band.astype(np.float32)
    keep = np.ones((NT + 1,), np.float32)
    keep[::S // P] = 0.0
    c["keep"] = keep
    half = np.arange(0, DH, 2, dtype=np.float32)
    inv_freq = (1.0 / np.float32(10000.0) ** (half / np.float32(DH))).astype(np.float32)
    t = np.arange(S, dtype=np.float32)
    freqs = (t[:, None] * inv_freq[None, :]).astype(np.float32).astype(np.float64)
    base = ((half + np.float32(0.4 * DH)) / np.float32(1.4 * DH)).astype(np.float32)
    power = ((t - S // 2) / np.float32(WIN // 2)).astype(np.float32)
    scale = base[None, :].astype(np.float64) ** power[:, None]
    cos, sin = np.cos(freqs), np.sin(freqs)
    sign = np.array([-1.0, 1.0])[None, :, None]

    def both(a):
        return np.repeat(a[:, None, :], 2, axis=1)

    tabs = [both(cos * scale), both(sin * scale) * sign, both(cos / scale), both(sin / scale) * sign]
    tabs = np.stack([a.reshape(S, DH) for a in tabs], axis=1).astype(np.float32)
    c["rot_base"] = np.ascontiguousarray(tabs.reshape(S // P, P, 4, DH).transpose(1, 0, 2, 3))
    c["lower"] = (np.arange(E)[None, :] < np.arange(E)[:, None]).astype(np.float32)
    return c


def laid_out(i):
    f = {k: np.asarray(v) for k, v in i.items()}

    def pairs(w):
        return w.reshape(D, PAIRS, P).transpose(1, 0, 2)

    a = {"x": f["L0_attn_x"].reshape(N, D)}
    qkv = [f[f"L0_attn_w{n}"].reshape(PAIRS, P, D).transpose(0, 2, 1) for n in "qkv"]
    a["a_wqkv"] = np.stack(qkv, axis=2)
    a["a_wo"] = f["L0_attn_wo"].reshape(D, PAIRS, P).transpose(1, 2, 0)

    def again(w):
        return np.concatenate([w, w[:1]])

    def swapped(s):
        return np.concatenate([s[:, DH // 2:], s[:, :DH // 2]], axis=1)

    qs, ks = f["L0_ffn_q_scale"], f["L0_ffn_k_scale"]
    a["rot_scale"] = again(np.stack([qs, swapped(qs), ks, swapped(ks)], axis=1))
    w = f["L0_ffn_Wqkv"].reshape(LAYERS, D, 3, PAIRS, 2, DH).transpose(0, 1, 2, 4, 3, 5)
    a["b_wqkv"] = again(w.reshape(LAYERS, D, 3 * H * DH))
    a["b_wo"] = again(f["L0_ffn_Wo"].reshape(LAYERS, PAIRS, P, D).transpose(0, 2, 1, 3))
    a["b_w1"] = f["L0_ffn_W1"]
    pad = NF * P - FFN_IN
    a["b_w2"] = np.pad(f["L0_ffn_W2"], ((0, 0), (0, pad), (0, 0))).reshape(LAYERS, NF, P, D).transpose(0, 2, 1, 3)
    b1 = np.pad(f["L0_ffn_b1"].reshape(LAYERS, 2, FFN_IN), ((0, 0), (0, 0), (0, pad))).reshape(LAYERS, 2 * NF, P)
    a["b_cols"] = np.concatenate([f["L0_ffn_ln_g"][:, None], f["L0_ffn_ln_b"][:, None], f["L0_ffn_b2"][:, None], b1],
                                 axis=1).transpose(0, 2, 1)
    q, (k, v) = f["L1_attn_Wq"], np.split(f["L1_attn_Wkv"], 2, axis=1)
    a["c_wqkv"] = again(np.stack([pairs(q), pairs(k), pairs(v)], axis=2))
    a["c_wo"] = f["L1_attn_Wo"].reshape(PAIRS, P, D)
    a["c_norm_w"] = f["L1_attn_norm_w"].reshape(D, 1)
    a["c_gamma"] = again(np.stack([f["L1_attn_q_gamma"].reshape(PAIRS, P), f["L1_attn_k_gamma"].reshape(PAIRS, P)],
                                  axis=2))
    a["router_w"] = f["L1_ffn_router_w"].T
    a["router_bias"] = f["L1_ffn_bias"]

    def halves(w):
        return w.reshape(D, 2, F).transpose(1, 0, 2)

    a["e_gate_up"] = np.stack([np.concatenate([f["L1_ffn_gate_w"], halves(f["L1_ffn_sh_gate_w"])]),
                               np.concatenate([f["L1_ffn_up_w"], halves(f["L1_ffn_sh_up_w"])])], axis=2)
    a["e_down"] = np.concatenate([f["L1_ffn_down_w"], f["L1_ffn_sh_down_w"].reshape(2, F, D)])
    a.update(shape_constants())
    return {k: np.ascontiguousarray(v) for k, v in a.items()}


def build(nc, d, out):
    with ExitStack() as ctx:
        m = persistent(ctx, nc)
        load_and_norm(nc, m, d)
        causal_attention(nc, m, d)
        windowed_layers(nc, m, d)
        second_norm(nc, m, d)
        capped_attention(nc, m, d)
        experts(nc, m, d, out)


def kernel(**inputs):
    import concourse.bacc as bacc
    from concourse.bass_utils import run_bass_kernel_spmd

    nc = bacc.Bacc("TRN2", target_bir_lowering=False, num_devices=1)
    arrays = {f"in_{k}": v for k, v in laid_out(inputs).items()}
    d = {k[3:]: nc.dram_tensor(k, v.shape, mybir.dt.from_np(v.dtype), kind="ExternalInput").ap()
         for k, v in arrays.items()}
    out = nc.dram_tensor("out", (N, D), F32, kind="ExternalOutput").ap()
    build(nc, d, out)
    r = run_bass_kernel_spmd(nc, [arrays], core_ids=[0])
    return r.results[0]["out"].reshape(B, S, D)
```

```python
from contextlib import ExitStack

import numpy as np
import concourse.bass as bass
from concourse import mybir
from concourse.alu_op_type import AluOpType as ALU

F32 = mybir.dt.float32
F32R = mybir.dt.float32r
BF16 = mybir.dt.bfloat16
ACT = mybir.ActivationFunctionType
AX = mybir.AxisListType

P = 128
B, S, D = 2, 1024, 128
N = B * S
NT = N // P
H, DH = 16, 64
PAIRS = H // 2
LAYERS = 6
WIN = 32
FFN_IN = int(D * 4 * 2 / 3)
FFN_PARTS = [(i * P, min(P, FFN_IN - i * P)) for i in range(-(-FFN_IN // P))]
NF = len(FFN_PARTS)
CH = 512
NCH = N // CH
E, F = 16, 128
NE = E + 2
GROUPS, TOP_GROUPS, TOP_K, ROUTE_SCALE = 4, 2, 4, 2.5
LN_EPS = 1e-5
RMS_EPS = float(np.finfo(np.float32).eps)
NEG = -1e30
QK_SCALE = 8.0
SOFTCLAMP = 50.0
BANK = 512
START = 4


def spread(ap, axis, n):
    a = ap.unsqueeze(axis)
    shape = list(a.shape)
    shape[axis] = n
    return a.broadcast_to(shape)


class Chain:

    def __init__(self, engine, sem, start=0):
        self.engine, self.sem, self.start, self.count = engine, sem, start, 0

    def link(self, instruction):
        instruction.then_inc(self.sem, 1)
        self.count += 1
        self.engine.wait_ge(self.sem, self.start + self.count)


def start_semaphores(nc, stage, sems):
    with nc.sbuf_tensor(stage + "_scratch", [P, len(sems)], F32) as scratch, nc.Block() as block:
        @block.gpsimd
        def _(pool):
            for i, sem in enumerate(sems):
                nc.gpsimd.memset(scratch[:, i:i + 1], 0.0).then_inc(sem, START)


def split_product(nc, out, hi_lhs, lo_lhs, hi_rhs, lo_rhs):
    nc.tensor.matmul(out, hi_lhs, hi_rhs, start=True, stop=False)
    nc.tensor.matmul(out, lo_lhs, hi_rhs, start=False, stop=False)
    return nc.tensor.matmul(out, hi_lhs, lo_rhs, start=False, stop=True)


class Memory:
    pass


def tensors(ctx, nc, prefix):
    def sb(name, shape, dt=F32):
        return ctx.enter_context(nc.sbuf_tensor(prefix + name, shape, dt))

    def ps(name, shape, dt=F32):
        return ctx.enter_context(nc.psum_tensor(prefix + name, shape, dt))

    def sem(name):
        return ctx.enter_context(nc.semaphore(prefix + name))

    return sb, ps, sem


def norm_statistics(nc, dve, link, x, stats, mv, count):
    for t in range(count):
        last = nc.vector.bn_stats(stats[:, t, :], x[:, t, :])
    link(last)
    for t in range(count):
        last = nc.vector.bn_aggr(mv[:, t, :], stats[:, t, :])
    link(last)


def load_and_norm(nc, m, d):
    with ExitStack() as ctx:
        sb, ps, sem = tensors(ctx, nc, "n0_")
        stats = sb("stats", [P, NT, 6])
        mv = sb("mv", [P, NT, 2])
        veps = sb("veps", [P, NT])
        rstd = sb("rstd", [P, NT])
        xn = sb("xn", [P, NT, D])
        causal = sb("causal", [P, P])
        band = sb("band", [P, NT, 2 * WIN])
        psT = ps("psT", [P, 4, BANK])
        x_in, const_in, pow_in, ready, dchain, rstd_ready, xn_ready, xnT_ps = map(sem, (
            "x_in", "const_in", "pow_in", "ready", "dchain", "rstd_ready", "xn_ready", "xnT_ps"))
        xT_ready, zeros = sem("xT_ready"), sem("zeros")
        block = ctx.enter_context(nc.Block())

        @block.sync
        def _(sp):
            sp.dma_start(m.x[:, :, :], d["x"].rearrange("(t p) d -> p t d", p=P)).then_inc(x_in, 16)
            sp.dma_start(m.ident[:, :], d["ident"]).then_inc(const_in, 16)
            sp.dma_start(causal[:, :], d["causal"]).then_inc(const_in, 16)
            sp.dma_start(band[:, :, :], d["band"]).then_inc(const_in, 16)
            sp.dma_start(m.keep[:, :], d["keep"].partition_broadcast(P)).then_inc(const_in, 16)
            sp.dma_start(m.rot_base[:, :, :, :], d["rot_base"]).then_inc(const_in, 16)
            sp.dma_start(m.rot_scale[:, :, :], d["rot_scale"][0].partition_broadcast(P)).then_inc(const_in, 16)
            sp.wait_ge(const_in, 6 * 16)
            sp.wait_ge(x_in, 16)

        @block.gpsimd
        def _(pool):
            nc.gpsimd.memset(m.minus_half[:, :], -0.5).then_inc(ready, 1)
            nc.gpsimd.memset(m.ones[:, :], 1.0)
            nc.gpsimd.memset(m.xa[:, 0:1], 0.0)
            nc.gpsimd.memset(m.xa[:, 1 + N:], 0.0)
            nc.gpsimd.memset(m.xb[:, 0:1], 0.0)
            nc.gpsimd.memset(m.branchT[:, :], 0.0).then_inc(zeros, 1)
            pool.wait_ge(const_in, 6 * 16)
            for b in range(B):
                nc.gpsimd.tensor_tensor(m.rot[:, b * 8:b * 8 + 8, :, :], m.rot_base[:, :, :, :],
                                        spread(m.rot_scale[:, :, :], 1, 8), ALU.mult).then_inc(zeros, 1)
            pool.wait_ge(dchain, 3)
            pool.wait_ge(ready, 1)
            nc.gpsimd.tensor_tensor(rstd[:, :], veps[:, :], m.minus_half[:, 0:NT], ALU.pow).then_inc(rstd_ready, 1)

        @block.vector
        def _(dve):
            chain = Chain(dve, dchain)
            dve.wait_ge(x_in, 16)
            norm_statistics(nc, dve, chain.link, m.x, stats, mv, NT)
            chain.link(nc.vector.tensor_scalar(veps[:, :], mv[:, :, 1], LN_EPS, None, ALU.add))
            dve.wait_ge(rstd_ready, 1)
            for t in range(NT):
                nc.vector.tensor_scalar(xn[:, t, :], m.x[:, t, :], mv[:, t, 0:1], rstd[:, t:t + 1],
                                        ALU.subtract, ALU.mult).then_inc(xn_ready, 1)

        @block.tensor
        def _(pe):
            pe.wait_ge(const_in, 6 * 16)
            for t in range(NT):
                pe.wait_ge(xn_ready, t + 1)
                nc.tensor.transpose(psT[:, t // 4, (t % 4) * P:(t % 4 + 1) * P], xn[:, t, :],
                                    m.ident[:, :]).then_inc(xnT_ps, 1)

        @block.scalar
        def _(act):
            act.wait_ge(const_in, 6 * 16)
            nc.scalar.activation(m.identb[:, :], m.ident[:, :], ACT.Copy).then_inc(xT_ready, 1)
            nc.scalar.activation(m.causal[:, :], causal[:, :], ACT.Copy).then_inc(xT_ready, 1)
            nc.scalar.activation(m.band[:, :, :], band[:, :, :], ACT.Copy).then_inc(xT_ready, 1)
            for c in range(NCH):
                act.wait_ge(xnT_ps, 4 * (c + 1))
                nc.scalar.activation(m.xa[:, 1 + c * CH:1 + (c + 1) * CH], psT[:, c, :], ACT.Copy)\
                    .then_inc(xT_ready, 1)
                nc.scalar.activation(m.xnT[:, c * CH:(c + 1) * CH], psT[:, c, :], ACT.Copy)\
                    .then_inc(xT_ready, 1)


def causal_attention(nc, m, d):
    TB = S // P
    STEPS = [(b, qi, e) for b in range(B) for qi in range(TB) for e in range(2)]
    NS = len(STEPS)
    PER_CHUNK = 8
    CHUNKS = NS // PER_CHUNK
    groups = []
    for s, (b, qi, e) in enumerate(STEPS):
        groups += [(s, k, min(4, qi + 1 - k)) for k in range(0, qi + 1, 4)]
    NG = len(groups)
    first_group = [next(r for r, g in enumerate(groups) if g[0] == s) for s in range(NS)] + [NG]

    with ExitStack() as ctx:
        sb, ps, sem = tensors(ctx, nc, "a0_")
        w = sb("w", [P, 3, P])
        wo = sb("wo", [P, D])
        QT = sb("QT", [P, N])
        KT = sb("KT", [P, N])
        V = sb("V", [P, NT, P])
        prob = sb("prob", [P, 4, S])
        probT = sb("probT", [P, 2, 2, TB, CH])
        OT = sb("OT", [P, CH])
        nmax = sb("nmax", [P, 4])
        rsum = sb("rsum", [P, 4])
        rinv = sb("rinv", [P, 4])
        psS = ps("psS", [P, 2, S])
        psT = ps("psT", [P, 2, BANK])
        psO = ps("psO", [P, BANK])
        psW = ps("psW", [P, BANK])
        names = ("w_in wo_in proj_ps q_ready k_ready v_ready s_ps max_done exp_done dchain norm_done t_ps "
                 "ev_act ev_dve pv_ps ot_ready wo_ps acc_done").split()
        (w_in, wo_in, proj_ps, q_ready, k_ready, v_ready, s_ps, max_done, exp_done, dchain, norm_done, t_ps,
         ev_act, ev_dve, pv_ps, ot_ready, wo_ps, acc_done) = sems = [sem(name) for name in names]
        start_semaphores(nc, "a0", sems)
        block = ctx.enter_context(nc.Block())

        def bank(n):
            return psS[:, (n % 4) // 2, ((n % 4) % 2) * BANK:((n % 4) % 2 + 1) * BANK]

        @block.sync
        def _(sp):
            with sp.Fori(0, PAIRS) as g:
                sp.wait_ge(proj_ps, START + g * 12)
                sp.dma_start(w[:, :, :], d["a_wqkv"][bass.ds(g, 1)].rearrange("g d x f -> (g d) x f")).then_inc(w_in, 16)
                sp.wait_ge(wo_ps, START + g * CHUNKS)
                sp.dma_start(wo[:, :], d["a_wo"][bass.ds(g, 1)].rearrange("g f d -> (g f) d")).then_inc(wo_in, 16)

        @block.tensor
        def _(pe):
            def scores(g, s):
                b, qi, e = STEPS[s]
                if s >= 2:
                    pe.wait_ge(exp_done, START + g * NS + s - 1)
                keys = (qi + 1) * P
                h = slice(64 * e, 64 * e + 64)
                for k in range(0, keys, BANK):
                    n = min(BANK, keys - k)
                    diagonal = k + n == keys
                    last = nc.tensor.matmul(psS[:, e, k:k + n], QT[h, b * S + qi * P:b * S + (qi + 1) * P],
                                            KT[h, b * S + k:b * S + k + n], start=True, stop=not diagonal)
                    if diagonal:
                        last = nc.tensor.matmul(psS[:, e, keys - P:keys], m.identb[:, :], m.causal[:, :],
                                                start=False, stop=True)
                last.then_inc(s_ps, 1)

            def transposes(g, s):
                pe.wait_ge(norm_done, START + g * NS + s + 1)
                for r in range(first_group[s], first_group[s + 1]):
                    _, k0, n = groups[r]
                    pe.wait_ge(ev_act if r % 2 == 0 else ev_dve, START + g * (NG // 2) + r // 2)
                    for j in range(n):
                        last = nc.tensor.transpose(psT[:, r % 2, j * P:(j + 1) * P],
                                                   prob[:, s % 4, (k0 + j) * P:(k0 + j + 1) * P], m.ident[:, :])
                    last.then_inc(t_ps, 1)

            def values(g, c):
                b, qc = c // 2, c % 2
                done = first_group[PER_CHUNK * (c + 1)]
                pe.wait_ge(ev_act, START + g * (NG // 2) + (done + 1) // 2)
                pe.wait_ge(ev_dve, START + g * (NG // 2) + done // 2)
                pe.wait_ge(ot_ready, START + g * CHUNKS + c)
                kts = 4 * (qc + 1)
                for kt in range(kts):
                    r0 = max(0, kt - 4 * qc) * P
                    for e in range(2):
                        last = nc.tensor.matmul(psO[64 * e:64 * e + 64, r0:CH], V[:, b * TB + kt, 64 * e:64 * e + 64],
                                                probT[:, c % 2, e, kt, r0:CH], start=kt == 0, stop=kt == kts - 1)
                last.then_inc(pv_ps, 1)

            def project(g, c):
                pe.wait_ge(ot_ready, START + g * CHUNKS + c + 1)
                pe.wait_ge(acc_done, START + g * CHUNKS + c)
                if c == 0:
                    pe.wait_ge(wo_in, START + (g + 1) * 16)
                nc.tensor.matmul(psW[:, :], wo[:, :], OT[:, :], start=True, stop=True).then_inc(wo_ps, 1)

            with pe.Fori(0, PAIRS) as g:
                pe.wait_ge(w_in, START + (g + 1) * 16)
                pe.wait_ge(exp_done, START + g * NS)
                for i in range(NCH):
                    for x in range(3):
                        n = 3 * i + x
                        if n >= 4:
                            who = (q_ready, k_ready, v_ready)[(n - 4) % 3]
                            pe.wait_ge(who, START + g * NCH + (n - 4) // 3 + 1)
                        if x < 2:
                            last = nc.tensor.matmul(bank(n), w[:, x, :], m.xnT[:, i * CH:(i + 1) * CH],
                                                    start=True, stop=True)
                        else:
                            for j in range(4):
                                last = nc.tensor.matmul(bank(n)[:, j * P:(j + 1) * P],
                                                        m.xnT[:, i * CH + j * P:i * CH + (j + 1) * P], w[:, 2, :],
                                                        start=True, stop=True)
                        last.then_inc(proj_ps, 1)
                for ready in (q_ready, k_ready, v_ready):
                    pe.wait_ge(ready, START + (g + 1) * NCH)
                scores(g, 0)
                scores(g, 1)
                for s in range(NS + 1):
                    if s + 2 < NS:
                        scores(g, s + 2)
                    if s >= 1:
                        transposes(g, s - 1)
                    if s % PER_CHUNK == 3 and s > PER_CHUNK:
                        values(g, s // PER_CHUNK - 1)
                    if s % PER_CHUNK == 5 and s > PER_CHUNK:
                        project(g, s // PER_CHUNK - 1)
                values(g, CHUNKS - 1)
                project(g, CHUNKS - 1)

        def copy_out(engine, g, r, copy, done):
            s, k0, n = groups[r]
            b, qi, e = STEPS[s]
            c = s // PER_CHUNK
            engine.wait_ge(t_ps, START + g * NG + r + 1)
            if c >= 2:
                engine.wait_ge(pv_ps, START + g * CHUNKS + c - 1)
            copy(probT[:, c % 2, e, k0:k0 + n, (qi % 4) * P:(qi % 4 + 1) * P],
                 psT[:, r % 2, 0:n * P].rearrange("p (k q) -> p k q", q=P)).then_inc(done, 1)

        @block.scalar
        def _(act):
            def copy(out, in_):
                return nc.scalar.activation(out, in_, ACT.Copy)

            def heads_out(g, c):
                act.wait_ge(pv_ps, START + g * CHUNKS + c + 1)
                act.wait_ge(wo_ps, START + g * CHUNKS + c)
                nc.scalar.activation(OT[:, :], psO[:, :], ACT.Copy).then_inc(ot_ready, 1)

            with act.Fori(0, PAIRS) as g:
                for i in range(NCH):
                    act.wait_ge(proj_ps, START + g * 12 + 3 * i + 1)
                    nc.scalar.activation(QT[:, i * CH:(i + 1) * CH], bank(3 * i), ACT.Copy, scale=DH ** -0.5)\
                        .then_inc(q_ready, 1)
                    act.wait_ge(proj_ps, START + g * 12 + 3 * i + 3)
                    nc.scalar.activation(V[:, 4 * i:4 * i + 4, :], bank(3 * i + 2).rearrange("p (t f) -> p t f", f=P),
                                         ACT.Copy).then_inc(v_ready, 1)
                for s in range(NS + 3):
                    if s % PER_CHUNK == 6 and s > PER_CHUNK:
                        heads_out(g, s // PER_CHUNK - 1)
                    if s >= 3:
                        for r in range(first_group[s - 3], first_group[s - 2]):
                            if r % 2 == 0:
                                copy_out(act, g, r, copy, ev_act)
                    if s < NS:
                        b, qi, e = STEPS[s]
                        keys = (qi + 1) * P
                        act.wait_ge(max_done, START + g * NS + s + 1)
                        nc.scalar.activation(prob[:, s % 4, 0:keys], psS[:, e, 0:keys], ACT.Exp,
                                             bias=nmax[:, s % 4:s % 4 + 1],
                                             accum_out=rsum[:, s % 4:s % 4 + 1]).then_inc(exp_done, 1)
                heads_out(g, CHUNKS - 1)

        @block.vector
        def _(dve):
            def add_out(g, c):
                b, qc = c // 2, c % 2
                dve.wait_ge(wo_ps, START + g * CHUNKS + c + 1)
                cols = slice(b * S + qc * CH, b * S + (qc + 1) * CH)
                nc.vector.tensor_tensor(m.branchT[:, cols], m.branchT[:, cols], psW[:, :], ALU.add)\
                    .then_inc(acc_done, 1)

            with dve.Fori(0, PAIRS) as g:
                for i in range(NCH):
                    dve.wait_ge(proj_ps, START + g * 12 + 3 * i + 2)
                    nc.vector.tensor_copy(KT[:, i * CH:(i + 1) * CH], bank(3 * i + 1)).then_inc(k_ready, 1)
                for s in range(NS + 3):
                    if s < NS:
                        b, qi, e = STEPS[s]
                        dve.wait_ge(s_ps, START + g * NS + s + 1)
                        nc.vector.tensor_reduce(nmax[:, s % 4:s % 4 + 1], psS[:, e, 0:(qi + 1) * P], AX.X, ALU.max,
                                                negate=True).then_inc(max_done, 1)
                    if s % PER_CHUNK == 0 and s > PER_CHUNK:
                        add_out(g, s // PER_CHUNK - 2)
                    if s >= 3:
                        for r in range(first_group[s - 3], first_group[s - 2]):
                            if r % 2 == 1:
                                copy_out(dve, g, r, nc.vector.tensor_copy, ev_dve)
                    if 1 <= s <= NS:
                        b, qi, e = STEPS[s - 1]
                        keys, q = (qi + 1) * P, (s - 1) % 4
                        dve.wait_ge(exp_done, START + g * NS + s)
                        nc.vector.reciprocal(rinv[:, q:q + 1], rsum[:, q:q + 1]).then_inc(dchain, 1)
                        dve.wait_ge(dchain, START + g * NS + s)
                        nc.vector.tensor_scalar(prob[:, q, 0:keys], prob[:, q, 0:keys], rinv[:, q:q + 1], None,
                                                ALU.mult).then_inc(norm_done, 1)
                add_out(g, CHUNKS - 1)


def windowed_layers(nc, m, d):
    with ExitStack() as ctx:
        sb, ps, sem = tensors(ctx, nc, "b_")
        k = Memory()
        k.w_raw = sb("w_raw", [P, 3 * H * DH])
        k.w_hi = sb("w_hi", [P, 3 * H * DH], F32R)
        k.w_lo = sb("w_lo", [P, 3 * H * DH], F32R)
        k.w_split = sem("w_split")
        k.wo = sb("wo", [P, PAIRS, D])
        k.w1 = sb("w1", [P, 2 * FFN_IN])
        k.w2 = sb("w2", [P, NF, D])
        k.cols = sb("cols", [P, 3 + 2 * NF])
        k.KT = sb("KT", [P, 2, PAIRS, WIN + P])
        k.v = sb("v", [P, 2, 2, PAIRS * DH])
        k.attn_in = sem("attn_in")
        k.ffn_in = sem("ffn_in")
        attention = WindowAttention(ctx, nc, k)
        ffn = GatedFfn(ctx, nc, k)
        start_semaphores(nc, "b", [k.attn_in, k.ffn_in, k.w_split] + attention.sems + ffn.sems)
        with nc.Block() as block:
            @block.sync
            def _(sp):
                sp.dma_start(k.w_raw[:, :], d["b_wqkv"][0]).then_inc(k.attn_in, 16)
                sp.dma_start(k.wo[:, :, :], d["b_wo"][0]).then_inc(k.attn_in, 16)

            @block.scalar
            def _(act):
                split_hi(nc, act, k, 0)

            @block.gpsimd
            def _(pool):
                split_lo(nc, pool, k, 0)

            @block.vector
            def _(dve):
                nc.vector.memset(k.KT[:, :, :, :], 0.0).then_inc(attention.o_ps, 1)
                nc.vector.memset(k.v[:, :, :, :], 0.0).then_inc(attention.o_ps, 1)

        with nc.Fori(0, LAYERS) as layer:
            attention.emit(nc, m, d, k, layer)
            ffn.emit(nc, m, d, k, layer)
        with nc.Block() as block:
            @block.sync
            def _(sp):
                sp.wait_ge(k.attn_in, START + (LAYERS + 1) * 32)


def split_hi(nc, act, k, layer):
    act.wait_ge(k.attn_in, START + (layer + 1) * 32)
    for c in range(2):
        half = slice(c * (3 * H * DH // 2), (c + 1) * (3 * H * DH // 2))
        nc.scalar.activation(k.w_hi[:, half], k.w_raw[:, half], ACT.Copy).then_inc(k.w_split, 1)


def split_lo(nc, pool, k, layer):
    pool.wait_ge(k.w_split, START + 3 * layer + 2)
    nc.gpsimd.tensor_tensor(k.w_lo[:, :], k.w_raw[:, :], k.w_hi[:, :], ALU.subtract).then_inc(k.w_split, 1)


class WindowAttention:
    NAMES = ("xs_raw xs_upper xs_ready v_ps k_ps q_ps sq_done rot_done ss_done khat_done v_ready win_even win_odd tr_ps tr_act s_ps "
             "sub_done exp_done sum_done o_ps norm_done res_done halo_done dchain pchain").split()
    FULL = ["p0", "p1", "k0", "k1", "q0", "q1", "o0", "o1", "w"]
    LAST = ["p0", "p1", "o0", "o1", "w"]

    def __init__(self, ctx, nc, k):
        sb, ps, sem = tensors(ctx, nc, "ba_")
        self.sems = [sem(name) for name in self.NAMES]
        (self.xs_raw, self.xs_upper, self.xs_ready, self.v_ps, self.k_ps, self.q_ps, self.sq_done, self.rot_done, self.ss_done, self.khat_done,
         self.v_ready, self.win_even, self.win_odd, self.tr_ps, self.tr_act, self.s_ps, self.sub_done, self.exp_done,
         self.sum_done, self.o_ps, self.norm_done, self.res_done, self.halo_done, self.dchain,
         self.pchain) = self.sems
        self.win_in = (self.win_even, self.win_odd)

    def emit(self, nc, m, d, k, layer):
        with ExitStack() as ctx:
            sb, ps, _ = tensors(ctx, nc, "bt_")
            W = H * DH
            xs = sb("xs", [P, P])
            xs_hi = sb("xs_hi", [P, 2, P], F32R)
            xs_lo = sb("xs_lo", [P, 2, P], F32R)
            sq = sb("sq", [P, 2, W])
            t1 = sb("t1", [P, 2, W])
            t2 = sb("t2", [P, 2, W])
            ss = sb("ss", [P, 2, H])
            rn = sb("rn", [P, 2, H])
            hat = sb("hat", [P, 2, 2, W])
            QT = sb("QT", [P, PAIRS, P])
            win = sb("win", [P, 2, P // WIN, PAIRS * DH])
            sc = sb("sc", [P, W])
            prob = sb("prob", [P, PAIRS, 2, 2 * WIN])
            probT = sb("probT", [P, PAIRS, P])
            mx = sb("mx", [P, H])
            rs = sb("rs", [P, H])
            rr = sb("rr", [P, H])
            o = m.xnT[:, 0:W].rearrange("p (h e f) -> p h e f", e=2, f=DH)
            OT = m.xnT[:, W:2 * W].rearrange("p (h t) -> p h t", t=P)
            psA = ps("psA", [P, W])
            psB = ps("psB", [P, W])
            psC = ps("psC", [P, 2, BANK])
            psD = ps("psD", [P, W])
            s = self
            base = layer * NT
            Q, K = 0, 1
            NTURN = 4 + 9 * (NT - 1) + 5
            NACT = 4 + 8 * (NT - 1) + 4

            def turn(n, u, what, last):
                order = self.LAST if last else self.FULL
                i = order.index(what)
                number = layer * NTURN + 4 + 9 * n + i
                half = (u + i) % 2
                return number, half, i, order

            def act_count(n, i, order):
                return layer * NACT + 4 + 8 * n + i + 1

            def normed(engine, u, x):
                engine.tensor_tensor(hat[:, u, 1 - x, :].rearrange("p (hp e f) -> p e hp f", e=2, f=DH),
                                     t1[:, x, :].rearrange("p (e hp f) -> p e hp f", e=2, f=DH),
                                     spread(rn[:, x, :].rearrange("p (e hp) -> p e hp", e=2), 3, DH),
                                     ALU.mult).then_inc(s.khat_done, 1)

            block = ctx.enter_context(nc.Block())

            @block.sync
            def _(sp):
                sp.dma_start(k.w1[:, :], d["b_w1"][bass.ds(layer, 1)].rearrange("l d f -> (l d) f")).then_inc(k.ffn_in, 16)
                sp.dma_start(k.w2[:, :, :], d["b_w2"][bass.ds(layer, 1)].rearrange("l p c d -> (l p) c d")).then_inc(k.ffn_in, 16)
                sp.dma_start(k.cols[:, :], d["b_cols"][bass.ds(layer, 1)].rearrange("l p c -> (l p) c")).then_inc(k.ffn_in, 16)
                sp.dma_start(m.rot_scale[:, :, :], d["rot_scale"][bass.ds(layer + 1, 1)].rearrange("l a f -> (l a f)")
                             .partition_broadcast(P).rearrange("p (a f) -> p a f", f=DH)).then_inc(k.ffn_in, 16)

                def windows(n, u):
                    sp.wait_ge(s.v_ready, START + base + n + 1)
                    sp.wait_ge(s.o_ps, START + base + n + 1)
                    for e in range(2):
                        h = 64 * e
                        sp.dma_start(win[h:h + 32, u, 0, :], k.v[P - WIN:P, 1 - u, e, :]).then_inc(s.win_in[u], 16)
                        sp.dma_start(win[h + 32:h + 64, u, 0, :], k.v[0:WIN, u, e, :]).then_inc(s.win_in[u], 16)
                        for w in range(1, P // WIN):
                            sp.dma_start(win[h:h + 64, u, w, :], k.v[WIN * (w - 1):WIN * (w + 1), u, e, :])\
                                .then_inc(s.win_in[u], 16)

                for u in range(2):
                    windows(u, u)
                with sp.Fori(1, NT // 2) as tp:
                    for u in range(2):
                        windows(2 * tp + u, u)

            @block.tensor
            def _(pe):
                def project(n, u, what, first="v"):
                    ps_, third, done = {"v": (psA, 2, s.v_ps), "k": (psB, 1, s.k_ps), "q": (psA, 0, s.q_ps)}[what]
                    if what == first:
                        pe.wait_ge(s.xs_ready, START + layer * (NT + 1) + n + 1)
                        pe.wait_ge(s.sq_done, START + 2 * (base + n))
                        pe.wait_ge(s.rot_done, START + 2 * (base + n))
                    if what == "q":
                        pe.wait_ge(s.v_ready, START + base + n + 1)
                    for e in range(2):
                        cols = slice(third * W + e * BANK, third * W + (e + 1) * BANK)
                        last = split_product(nc, ps_[:, e * BANK:(e + 1) * BANK], xs_hi[:, u, :], xs_lo[:, u, :],
                                             k.w_hi[:, cols], k.w_lo[:, cols])
                    last.then_inc(done, 1)

                def take_turn(n, u, what, last):
                    number, half, i, order = turn(n, u, what, last)
                    if i == 0:
                        pe.wait_ge(s.tr_act, START + act_count(n, -2, order) + 1)
                    elif i == 1:
                        pe.wait_ge(s.res_done, START + base + n)
                    else:
                        pe.wait_ge(s.tr_act, START + act_count(n, i - 2, order))
                    return psC[:, half, :]

                def transpose4(dst, src):
                    for j in range(4):
                        last = nc.tensor.transpose(dst[:, j * P:(j + 1) * P], src(j), m.ident[:, :])
                    last.then_inc(s.tr_ps, 1)

                def hat_turn(dst, u, x, g):
                    transpose4(dst, lambda j: hat[:, u, x, (4 * g + j) * P:(4 * g + j + 1) * P])

                def scores(n, u):
                    pe.wait_ge(s.tr_act, START + layer * NACT + (4 if isinstance(n, int) and n == 0 else 2 + 8 * n))
                    pe.wait_ge(s.halo_done, START + base + n)
                    pe.wait_ge(s.norm_done, START + base + n)
                    for e in range(2):
                        nc.tensor.matmul(psD[:, e * BANK:(e + 1) * BANK].rearrange("p (h j) -> p h j", j=2 * WIN),
                                         m.identb[:, :], band_of(n), start=True, stop=True)
                    for hp in range(PAIRS):
                        for e in range(2):
                            for w in range(P // WIN):
                                c = e * BANK + hp * 2 * WIN
                                last = nc.tensor.matmul(
                                    psD[WIN * w:WIN * (w + 1), c:c + 2 * WIN],
                                    QT[64 * e:64 * e + 64, hp, WIN * w:WIN * (w + 1)],
                                    k.KT[64 * e:64 * e + 64, u, hp, WIN * w:WIN * (w + 2)],
                                    start=False, stop=True, skip_group_check=True)
                    last.then_inc(s.s_ps, 1)

                def band_of(n):
                    b = m.band[:, bass.ds(n, 1), :] if not isinstance(n, int) else m.band[:, n:n + 1, :]
                    return b.broadcast_to([P, PAIRS, 2 * WIN])

                def values(n, u):
                    pe.wait_ge(s.win_in[u], START + (base + n - u) * 80 + 160)
                    pe.wait_ge(s.sub_done, START + base + n + 1)
                    nc.tensor.matmul(psD[:, 0:1], m.identb[:, :], m.identb[:, 0:1], start=True, stop=True)
                    for hp in range(PAIRS):
                        for e in range(2):
                            for w in range(P // WIN):
                                c = e * BANK + hp * DH
                                last = nc.tensor.matmul(
                                    psD[WIN * w:WIN * (w + 1), c:c + DH],
                                    probT[64 * e:64 * e + 64, hp, WIN * w:WIN * (w + 1)],
                                    win[64 * e:64 * e + 64, u, w, hp * DH:(hp + 1) * DH],
                                    start=True, stop=True)
                    last.then_inc(s.o_ps, 1)

                def iteration(n, u, projecting, last):
                    if projecting:
                        project(n + 2, u, "v")
                        project(n + 2, u, "k")
                    pe.wait_ge(s.exp_done, START + base + n + 1)
                    for g in range(2):
                        transpose4(take_turn(n, u, f"p{g}", last),
                                   lambda j: prob[:, 4 * g + j, :, :].rearrange("p e j -> p (e j)"))
                    if projecting:
                        project(n + 2, u, "q")
                    pe.wait_ge(s.tr_act, START + act_count(n, 1, None))
                    values(n, u)
                    if not last:
                        for what, x, count in (("k", K, 1), ("q", Q, 2)):
                            pe.wait_ge(s.khat_done, START + 2 * (base + n + 1) + count)
                            for g in range(2):
                                hat_turn(take_turn(n, u, f"{what}{g}", last), 1 - u, x, g)
                    pe.wait_ge(s.norm_done, START + base + n + 1)
                    for g in range(2):
                        transpose4(take_turn(n, u, f"o{g}", last),
                                   lambda j: o[:, 4 * g + j, :, :].rearrange("p e f -> p (e f)"))
                    if not last:
                        scores(n + 1, 1 - u)
                    dst = take_turn(n, u, "w", last)
                    pe.wait_ge(s.tr_act, START + act_count(n, 3 if last else 7, None))
                    for hp in range(PAIRS):
                        mm = nc.tensor.matmul(dst[:, 0:P], k.wo[:, hp, :], OT[:, hp, :],
                                              start=hp == 0, stop=hp == PAIRS - 1)
                    mm.then_inc(s.tr_ps, 1)

                pe.wait_ge(k.attn_in, START + (layer + 1) * 32)
                for n in range(2):
                    for what in "kvq":
                        project(n, n, what, first="k")
                for x, count in ((K, 1), (Q, 2)):
                    pe.wait_ge(s.khat_done, START + 2 * base + count)
                    for g in range(2):
                        if x == Q:
                            pe.wait_ge(s.tr_act, START + layer * NACT + g + 1)
                        hat_turn(psC[:, g, :], 0, x, g)
                scores(0, 0)
                with pe.Fori(0, NT // 2 - 1) as tp:
                    for u in range(2):
                        iteration(2 * tp + u, u, True, False)
                iteration(NT - 2, 0, False, False)
                iteration(NT - 1, 1, False, True)

            @block.scalar
            def _(act):
                def value_out(n, u):
                    act.wait_ge(s.v_ps, START + base + n + 1)
                    act.wait_ge(s.win_in[u], START + (base + n - u) * 80)
                    act.wait_ge(s.win_in[1 - u], START + (base + n + u) * 80)
                    nc.scalar.activation(k.v[:, u, :, :], psA[:, :].rearrange("p (e f) -> p e f", e=2), ACT.Copy)\
                        .then_inc(s.v_ready, 1)

                def square(n, what):
                    x = {"k": 0, "q": 1}[what]
                    act.wait_ge(s.k_ps if x == 0 else s.q_ps, START + base + n + 1)
                    if not isinstance(n, int):
                        act.wait_ge(s.ss_done, START + 2 * (base + n) + x - 1)
                    elif n == 1:
                        act.wait_ge(s.ss_done, START + 2 * base + x + 1)
                    nc.scalar.activation(sq[:, x, :], (psB if x == 0 else psA)[:, :], ACT.Square).then_inc(s.sq_done, 1)

                def copy_out(number, half, dst):
                    act.wait_ge(s.tr_ps, START + number + 1)
                    nc.scalar.activation(dst, psC[:, half, :].rearrange("p (h t) -> p h t", t=P), ACT.Copy)\
                        .then_inc(s.tr_act, 1)

                def turn_out(n, u, what, last, dst):
                    number, half, i, order = turn(n, u, what, last)
                    copy_out(number, half, dst)

                def exponential(n):
                    act.wait_ge(s.sub_done, START + base + n + 1)
                    act.wait_ge(s.sum_done, START + base + n)
                    nc.scalar.activation(prob[:, :, :, :].rearrange("p h e j -> p e h j"),
                                         sc[:, :].rearrange("p (e h j) -> p e h j", e=2, j=2 * WIN), ACT.Exp,
                                         scale=QK_SCALE)\
                        .then_inc(s.exp_done, 1)

                def iteration(n, u, projecting, last):
                    if projecting:
                        value_out(n + 2, u)
                        square(n + 2, "k")
                    for g in range(2):
                        turn_out(n, u, f"p{g}", last, probT[:, 4 * g:4 * g + 4, :])
                    if projecting:
                        square(n + 2, "q")
                    if not last:
                        for g in range(2):
                            turn_out(n, u, f"k{g}", last, k.KT[:, 1 - u, 4 * g:4 * g + 4, WIN:WIN + P])
                        for g in range(2):
                            turn_out(n, u, f"q{g}", last, QT[:, 4 * g:4 * g + 4, :])
                    for g in range(2):
                        turn_out(n, u, f"o{g}", last, OT[:, 4 * g:4 * g + 4, :])
                    if not last:
                        exponential(n + 1)

                for n in range(2):
                    square(n, "k")
                    value_out(n, n)
                    square(n, "q")
                for g in range(2):
                    copy_out(layer * NTURN + g, g, k.KT[:, 0, 4 * g:4 * g + 4, WIN:WIN + P])
                for g in range(2):
                    copy_out(layer * NTURN + 2 + g, g, QT[:, 4 * g:4 * g + 4, :])
                exponential(0)
                with act.Fori(0, NT // 2 - 1) as tp:
                    for u in range(2):
                        iteration(2 * tp + u, u, True, False)
                iteration(NT - 2, 0, False, False)
                iteration(NT - 1, 1, False, True)

            CPT = 4

            @block.vector
            def _(dve):
                def shift(n, u):
                    at = n * P
                    count = START + layer * (NT + 1) + n
                    dve.wait_ge(s.xs_ready, count)
                    nc.vector.tensor_copy(xs[0:64, :], m.xa[0:64, bass.ds(at + 1, P)])
                    nc.vector.tensor_copy(xs[64:P, 1:P], m.xa[64:P, bass.ds(at + 1, P - 1)])
                    nc.vector.tensor_scalar(xs[64:P, 0:1], m.xa[64:P, bass.ds(at, 1)],
                                            m.keep[64:P, bass.ds(n, 1)], None, ALU.mult).then_inc(s.xs_raw, 1)
                    dve.wait_ge(s.xs_raw, count + 1)
                    nc.vector.tensor_copy(xs_hi[:, u, :], xs[:, :]).then_inc(s.xs_upper, 1)
                    dve.wait_ge(s.xs_upper, count + 1)
                    nc.vector.tensor_tensor(xs_lo[:, u, :], xs[:, :], xs_hi[:, u, :], ALU.subtract)\
                        .then_inc(s.xs_ready, 1)

                def rotate(n, u, what):
                    x = {"k": 0, "q": 1}[what]
                    src = (psB if x == 0 else psA)[:, :].rearrange("p (h c f) -> p h c f", c=2, f=DH // 2)
                    dve.wait_ge(s.sq_done, START + 2 * (base + n) + x + 1)
                    dve.wait_ge(s.khat_done, START + 2 * base + (2 * (n - 1) + x + 1 if not isinstance(n, int) or n >= 1
                                                            else 0))
                    table = m.rot[:, bass.ds(n, 1), :, :].rearrange("p n a f -> p (n a) f")
                    a = 2 * (1 - x)
                    cos = spread(table[:, a, :], 1, H)
                    sin = spread(table[:, a + 1, :].rearrange("p (c f) -> p c f", c=2), 1, H)
                    nc.vector.tensor_tensor(t1[:, x, :].rearrange("p (h f) -> p h f", f=DH),
                                            src.rearrange("p h c f -> p h (c f)"), cos, ALU.mult)
                    nc.vector.tensor_tensor(t2[:, x, :].rearrange("p (h c f) -> p h c f", c=2, f=DH // 2),
                                            src[:, :, ::-1, :], sin, ALU.mult).then_inc(s.rot_done, 1)

                def norms(n, what, link):
                    x = {"k": 0, "q": 1}[what]
                    link(n, nc.vector.tensor_reduce(ss[:, x, :], sq[:, x, :].rearrange("p (h f) -> p h f", f=DH), AX.X, ALU.add))
                    nc.vector.tensor_scalar(ss[:, x, :], ss[:, x, :], 1e-24, None, ALU.max).then_inc(s.ss_done, 1)

                def halo(n, u):
                    dve.wait_ge(s.tr_act, START + layer * NACT + 4 + 8 * n - 12)
                    dve.wait_ge(s.s_ps, START + base + n - 1)
                    nc.vector.tensor_scalar(k.KT[:, u, :, 0:WIN], k.KT[:, 1 - u, :, P:P + WIN],
                                            m.keep[:, bass.ds(n, 1)], None, ALU.mult).then_inc(s.halo_done, 1)

                def subtract_maximum(n, link):
                    dve.wait_ge(s.s_ps, START + base + n + 1)
                    scores = psD[:, :].rearrange("p (h j) -> p h j", j=2 * WIN)
                    link(n, nc.vector.tensor_reduce(mx[:, :], scores, AX.X, ALU.max))
                    dve.wait_ge(s.exp_done, START + base + n)
                    nc.vector.tensor_tensor(sc[:, :].rearrange("p (h j) -> p h j", j=2 * WIN), scores,
                                            spread(mx[:, :], 2, 2 * WIN), ALU.subtract).then_inc(s.sub_done, 1)

                def iteration(n, u, projecting, last):
                    counts = [0]
                    before = 7 + CPT * n - (2 if last else 0)

                    def link(_, ins):
                        ins.then_inc(s.dchain, 1)
                        counts[0] += 1
                        dve.wait_ge(s.dchain, START + layer * (CPT * NT + 2) + before + counts[0])

                    dve.wait_ge(s.exp_done, START + base + n + 1)
                    link(n, nc.vector.tensor_reduce(rs[:, :].rearrange("p (e h) -> p h e", e=2), prob[:, :, :, :],
                                                    AX.X, ALU.add))
                    nc.vector.reciprocal(rr[:, :], rs[:, :]).then_inc(s.sum_done, 1)
                    if projecting:
                        rotate(n + 2, u, "k")
                        norms(n + 2, "k", link)
                    dve.wait_ge(s.sum_done, START + base + n + 1)
                    dve.wait_ge(s.o_ps, START + base + n + 3)
                    nc.vector.tensor_tensor(o[:, :, :, :].rearrange("p h e f -> p e h f"),
                                            psD[:, :].rearrange("p (e h f) -> p e h f", e=2, f=DH),
                                            spread(rr[:, :].rearrange("p (e h) -> p e h", e=2), 3, DH),
                                            ALU.mult).then_inc(s.norm_done, 1)
                    if projecting:
                        shift(n + 3, 1 - u)
                        rotate(n + 2, u, "q")
                        norms(n + 2, "q", link)
                    if not last:
                        halo(n + 2, u)
                        subtract_maximum(n + 1, link)
                    number, half, _, _ = turn(n, u, "w", last)
                    dve.wait_ge(s.tr_ps, START + number + 1)
                    cols = bass.ds(n * P + 1, P)
                    nc.vector.tensor_tensor(m.xb[:, cols], m.xa[:, cols], psC[:, half, 0:P], ALU.add)\
                        .then_inc(s.res_done, 1)

                done = [0]

                def link0(n, ins):
                    ins.then_inc(s.dchain, 1)
                    done[0] += 1
                    dve.wait_ge(s.dchain, START + layer * (CPT * NT + 2) + done[0])

                for n in range(2):
                    shift(n, n)
                for x, what in enumerate("kq"):
                    rotate(0, 0, what)
                    norms(0, what, link0)
                    link0(0, nc.vector.tensor_tensor(t1[:, x, :], t1[:, x, :], t2[:, x, :], ALU.add))
                for x in range(2):
                    dve.wait_ge(s.pchain, START + 2 * (2 * base + x) + 2)
                    normed(nc.vector, 0, x)
                shift(2, 0)
                for what in "kq":
                    rotate(1, 1, what)
                    norms(1, what, link0)
                dve.wait_ge(s.tr_act, START + layer * NACT + 2)
                nc.vector.tensor_scalar(k.KT[:, 1, :, 0:WIN], k.KT[:, 0, :, P:P + WIN], m.keep[:, 1:2], None,
                                        ALU.mult).then_inc(s.halo_done, 1)
                subtract_maximum(0, link0)
                with dve.Fori(0, NT // 2 - 1) as tp:
                    for u in range(2):
                        iteration(2 * tp + u, u, True, False)
                iteration(NT - 2, 0, False, False)
                iteration(NT - 1, 1, False, True)

            @block.gpsimd
            def _(pool):
                def finish(n, u, what):
                    x = {"k": 0, "q": 1}[what]
                    count = 2 * (base + n) + x
                    pool.wait_ge(s.ss_done, START + count + 1)
                    nc.gpsimd.tensor_tensor(rn[:, x, :], ss[:, x, :], m.minus_half[:, 0:H], ALU.pow).then_inc(s.pchain, 1)
                    pool.wait_ge(s.rot_done, START + count + 1)
                    nc.gpsimd.tensor_tensor(t1[:, x, :], t1[:, x, :], t2[:, x, :], ALU.add).then_inc(s.pchain, 1)
                    pool.wait_ge(s.pchain, START + 2 * count + 2)
                    if not isinstance(n, int):
                        pool.wait_ge(s.tr_ps, START + layer * NTURN + 4 + 9 * (n - 2))
                    normed(nc.gpsimd, u, x)

                for x in range(2):
                    pool.wait_ge(s.ss_done, START + 2 * base + x + 1)
                    nc.gpsimd.tensor_tensor(rn[:, x, :], ss[:, x, :], m.minus_half[:, 0:H], ALU.pow)\
                        .then_inc(s.pchain, 2)
                for what in "kq":
                    finish(1, 1, what)
                with pool.Fori(1, NT // 2) as tp:
                    for u in range(2):
                        for what in "kq":
                            finish(2 * tp + u, u, what)


class GatedFfn:
    NAMES = "xs_ready f_ps stat_done rstd_done xn_ready b_ps xnT_ready ga_ps gelu_done h_done y_ps y_done rot_done dchain".split()

    def __init__(self, ctx, nc, k):
        sb, ps, sem = tensors(ctx, nc, "bf_")
        self.sems = [sem(name) for name in self.NAMES]
        (self.xs_ready, self.f_ps, self.stat_done, self.rstd_done, self.xn_ready, self.b_ps, self.xnT_ready,
         self.ga_ps, self.gelu_done, self.h_done, self.y_ps, self.y_done, self.rot_done, self.dchain) = self.sems

    def emit(self, nc, m, d, k, layer):
        with ExitStack() as ctx:
            sb, ps, _ = tensors(ctx, nc, "bg_")
            xs = sb("xs", [P, 2, CH])
            stats = sb("stats", [P, 4, 6])
            mv = sb("mv", [P, 4, 2])
            veps = sb("veps", [P, 4])
            rstd = sb("rstd", [P, 4])
            xn = sb("xn", [P, 4, D])
            xnT = sb("xnT", [P, 2, CH])
            gel = sb("gel", [P, 2, CH])
            h = sb("h", [P, 2, NF, CH])
            psF = ps("psF", [P, BANK])
            psR = ps("psR", [P, BANK])
            psG = ps("psG", [P, 2, 2, BANK])
            psY = ps("psY", [P, 2, BANK])
            s = self
            T = CH // P
            c0 = layer * NCH
            g0 = layer * (NCH * NF)
            ln_g, ln_b, b2 = (k.cols[:, i:i + 1] for i in range(3))
            block = ctx.enter_context(nc.Block())

            @block.sync
            def _(sp):
                sp.dma_start(k.w_raw[:, :], d["b_wqkv"][bass.ds(layer + 1, 1)].rearrange("l d f -> (l d) f"))\
                    .then_inc(k.attn_in, 16)
                sp.dma_start(k.wo[:, :, :], d["b_wo"][bass.ds(layer + 1, 1)].rearrange("l p h d -> (l p) h d"))\
                    .then_inc(k.attn_in, 16)
            @block.tensor
            def _(pe):
                def forward(c):
                    pe.wait_ge(s.xs_ready, START + c0 + c + 1)
                    pe.wait_ge(s.xn_ready, START + c0 + c)
                    for j in range(T):
                        last = nc.tensor.transpose(psF[:, j * P:(j + 1) * P], xs[:, c % 2, j * P:(j + 1) * P], m.ident[:, :])
                    last.then_inc(s.f_ps, 1)

                def back(c):
                    pe.wait_ge(s.xn_ready, START + c0 + c + 1)
                    pe.wait_ge(s.xnT_ready, START + c0 + c)
                    for j in range(T):
                        last = nc.tensor.transpose(psR[:, j * P:(j + 1) * P], xn[:, j, :], m.ident[:, :])
                    last.then_inc(s.b_ps, 1)

                pe.wait_ge(k.ffn_in, START + (layer + 1) * 64)
                def gate_up(c, i):
                    f0, width = FFN_PARTS[i]
                    n = c * NF + i
                    if n >= 2:
                        pe.wait_ge(s.h_done, START + g0 + n - 1)
                    for gate in range(2):
                        last = nc.tensor.matmul(psG[0:width, n % 2, gate, :],
                                                k.w1[:, gate * FFN_IN + f0:gate * FFN_IN + f0 + width],
                                                xnT[:, c % 2, :], start=True, stop=True)
                    last.then_inc(s.ga_ps, 1)

                def down(c):
                    pe.wait_ge(s.h_done, START + g0 + (c + 1) * NF)
                    if c >= 2:
                        pe.wait_ge(s.y_done, START + c0 + c - 1)
                    for i, (f0, width) in enumerate(FFN_PARTS):
                        last = nc.tensor.matmul(psY[:, c % 2, :], k.w2[0:width, i, :], h[0:width, c % 2, i, :],
                                                start=i == 0, stop=i == NF - 1)
                    last.then_inc(s.y_ps, 1)

                forward(0)
                back(0)
                forward(1)
                for c in range(NCH):
                    pe.wait_ge(s.xnT_ready, START + c0 + c + 1)
                    gate_up(c, 0)
                    if c + 1 < NCH:
                        back(c + 1)
                    if c + 2 < NCH:
                        forward(c + 2)
                    gate_up(c, 1)
                    if c >= 1:
                        down(c - 1)
                    for i in range(2, NF):
                        gate_up(c, i)
                down(NCH - 1)

            @block.scalar
            def _(act):
                def norm_out(c):
                    act.wait_ge(s.b_ps, START + c0 + c + 1)
                    nc.scalar.activation(xnT[:, c % 2, :], psR[:, :], ACT.Identity, scale=ln_g, bias=ln_b)\
                        .then_inc(s.xnT_ready, 1)

                act.wait_ge(k.ffn_in, START + (layer + 1) * 64)
                norm_out(0)
                for c in range(NCH):
                    for i, (f0, width) in enumerate(FFN_PARTS):
                        n = c * NF + i
                        act.wait_ge(s.ga_ps, START + g0 + n + 1)
                        if n >= 2:
                            act.wait_ge(s.h_done, START + g0 + n - 1)
                        nc.scalar.activation(gel[0:width, n % 2, :], psG[0:width, n % 2, 1, :], ACT.Gelu,
                                             bias=k.cols[0:width, 3 + NF + i:4 + NF + i]).then_inc(s.gelu_done, 1)
                        if i == 0 and c + 1 < NCH:
                            norm_out(c + 1)
                    if c == 1:
                        split_hi(nc, act, k, layer + 1)

            @block.vector
            def _(dve):
                def shift(c):
                    first = c * CH + 1
                    if c * CH % S == 0:
                        nc.vector.memset(xs[64:P, c % 2, 0:1], 0.0)
                    skip = 1 if c * CH % S == 0 else 0
                    nc.vector.tensor_copy(xs[64:P, c % 2, skip:CH], m.xb[64:P, first - 1 + skip:first + CH - 1])
                    nc.vector.tensor_copy(xs[0:64, c % 2, :], m.xb[0:64, first:first + CH]).then_inc(s.xs_ready, 1)

                def statistics(c):
                    chain = Chain(dve, s.dchain, START + layer * (2 * NCH) + 2 * c)
                    dve.wait_ge(s.f_ps, START + c0 + c + 1)
                    psx = psF[:, :].rearrange("p (t f) -> p t f", f=D)
                    for t in range(T):
                        last = nc.vector.bn_stats(stats[:, t, :], psx[:, t, :])
                    chain.link(last)
                    nc.vector.memset(veps[:, :], LN_EPS)
                    for t in range(T):
                        last = nc.vector.bn_aggr(mv[:, t, :], stats[:, t, :])
                    chain.link(last)
                    nc.vector.tensor_tensor(veps[:, :], veps[:, :], mv[:, :, 1], ALU.add).then_inc(s.stat_done, 1)

                def normalise(c):
                    if c >= 1:
                        dve.wait_ge(s.b_ps, START + c0 + c)
                    dve.wait_ge(s.rstd_done, START + c0 + c + 1)
                    for t in range(T):
                        last = nc.vector.tensor_scalar(xn[:, t, :], psF[:, t * P:(t + 1) * P], mv[:, t, 0:1],
                                                       rstd[:, t:t + 1], ALU.subtract, ALU.mult)
                    last.then_inc(s.xn_ready, 1)

                def gated(c, i):
                    f0, width = FFN_PARTS[i]
                    n = c * NF + i
                    dve.wait_ge(s.gelu_done, START + g0 + n + 1)
                    if i == 0 and c >= 2:
                        dve.wait_ge(s.y_ps, START + c0 + c - 1)
                    nc.vector.scalar_tensor_tensor(out=h[0:width, c % 2, i, :], in0=psG[0:width, n % 2, 0, :],
                                                   scalar=k.cols[0:width, 3 + i:4 + i], in1=gel[0:width, n % 2, :],
                                                   op0=ALU.add, op1=ALU.mult).then_inc(s.h_done, 1)

                def add_out(c):
                    dve.wait_ge(s.y_ps, START + c0 + c + 1)
                    cols = slice(1 + c * CH, 1 + (c + 1) * CH)
                    nc.vector.scalar_tensor_tensor(out=m.xa[:, cols], in0=psY[:, c % 2, :], scalar=b2,
                                                   in1=m.xb[:, cols], op0=ALU.add, op1=ALU.add).then_inc(s.y_done, 1)

                shift(0)
                dve.wait_ge(k.ffn_in, START + (layer + 1) * 64)
                statistics(0)
                shift(1)
                normalise(0)
                statistics(1)
                shift(2)
                normalise(1)
                for c in range(NCH):
                    gated(c, 0)
                    if c + 2 < NCH:
                        statistics(c + 2)
                    gated(c, 1)
                    if c + 2 < NCH:
                        normalise(c + 2)
                    if c + 3 < NCH:
                        shift(c + 3)
                    if c >= 1:
                        add_out(c - 1)
                    gated(c, 2)
                add_out(NCH - 1)

            @block.gpsimd
            def _(pool):
                for c in range(NCH):
                    pool.wait_ge(s.stat_done, START + c0 + c + 1)
                    nc.gpsimd.tensor_tensor(rstd[:, :], veps[:, :], m.minus_half[:, 0:T], ALU.pow)\
                        .then_inc(s.rstd_done, 1)
                pool.wait_ge(k.ffn_in, START + (layer + 1) * 64)
                for b in range(B):
                    nc.gpsimd.tensor_tensor(m.rot[:, b * 8:b * 8 + 8, :, :], m.rot_base[:, :, :, :],
                                            spread(m.rot_scale[:, :, :], 1, 8), ALU.mult).then_inc(s.rot_done, 1)
                split_lo(nc, pool, k, layer + 1)


def second_norm(nc, m, d):
    with ExitStack() as ctx:
        sb, ps, sem = tensors(ctx, nc, "n1_")
        stats = sb("stats", [P, NT, 6])
        mv = sb("mv", [P, NT, 2])
        eps_sum = sb("eps_sum", [P, NT])
        rstd = sb("rstd", [P, NT])
        ms = sb("ms", [P, NT])
        rrms = sb("rrms", [P, NT])
        xn = sb("xn", [P, NT, D])
        xr = sb("xr", [P, NT, D])
        router_w = sb("router_w", [D, E])
        bias = sb("bias", [P, E])
        norm_w = sb("norm_w", [D, 1])
        score = sb("score", [P, NT, E])
        s = sb("s", [P, NT, E])
        pair_max = sb("pair_max", [P, NT * GROUPS, 2])
        pair_min = sb("pair_min", [P, NT * GROUPS, 2])
        top = sb("top", [P, NT * GROUPS])
        second = sb("second", [P, NT * GROUPS])
        gscore = sb("gscore", [P, NT, GROUPS])
        above = sb("above", [P, NT * E * E])
        rank = sb("rank", [P, NT * E])
        gsel = sb("gsel", [P, NT, GROUPS])
        gout = sb("gout", [P, NT, GROUPS])
        masked = sb("masked", [P, NT, E])
        wsum = sb("wsum", [P, NT])
        psX = ps("psX", [P, 4, BANK])
        psN = ps("psN", [P, 2, BANK])
        psL = ps("psL", [P, NT, E])
        names = "in_ dchain x_ps x_ready stat_done pow_done xn_ready n_ps n_ready logits_ps score_done".split()
        in_, dchain, x_ps, x_ready, stat_done, pow_done, xn_ready, n_ps, n_ready, logits_ps, score_done = map(sem, names)
        block = ctx.enter_context(nc.Block())
        T4 = CH // P

        @block.sync
        def _(sp):
            sp.dma_start(router_w[:, :], d["router_w"]).then_inc(in_, 16)
            sp.dma_start(bias[:, :], d["router_bias"].partition_broadcast(P)).then_inc(in_, 16)
            sp.dma_start(norm_w[:, :], d["c_norm_w"]).then_inc(in_, 16)
            sp.wait_ge(in_, 48)

        @block.tensor
        def _(pe):
            pe.wait_ge(dchain, 1)
            for t in range(NT):
                nc.tensor.transpose(psX[:, t // 4, (t % 4) * P:(t % 4 + 1) * P],
                                    m.branchT[:, t * P:(t + 1) * P], m.ident[:, :]).then_inc(x_ps, 1)
            for i in range(2 * NCH):
                src = (xn, xr)[i // NCH]
                pe.wait_ge(xn_ready, i // NCH + 1)
                if i >= 2:
                    pe.wait_ge(n_ready, i - 1)
                for j in range(T4):
                    last = nc.tensor.transpose(psN[:, i % 2, j * P:(j + 1) * P], src[:, (i % NCH) * T4 + j, :],
                                               m.ident[:, :])
                last.then_inc(n_ps, 1)
            pe.wait_ge(n_ready, NCH)
            pe.wait_ge(in_, 48)
            for t in range(NT):
                last = nc.tensor.matmul(psL[:, t, :], m.xnT[:, t * P:(t + 1) * P], router_w[:, :], start=True, stop=True)
            last.then_inc(logits_ps, 1)

        @block.scalar
        def _(act):
            act.wait_ge(in_, 48)
            for i in range(2 * NCH):
                act.wait_ge(n_ps, i + 1)
                cols = slice((i % NCH) * CH, (i % NCH + 1) * CH)
                if i < NCH:
                    nc.scalar.activation(m.xnT[:, cols], psN[:, i % 2, :], ACT.Copy).then_inc(n_ready, 1)
                else:
                    nc.scalar.activation(m.xrT[:, cols], psN[:, i % 2, :], ACT.Copy, scale=norm_w[:, 0:1])\
                        .then_inc(n_ready, 1)
            act.wait_ge(logits_ps, 1)
            nc.scalar.activation(score[:, :, :], psL[:, :, :], ACT.Sigmoid).then_inc(score_done, 1)

        @block.gpsimd
        def _(pool):
            for i, out in enumerate((rstd, rrms)):
                pool.wait_ge(stat_done, i + 1)
                nc.gpsimd.tensor_tensor(out[:, :], eps_sum[:, :], m.minus_half[:, 0:NT], ALU.pow).then_inc(pow_done, 1)

        @block.vector
        def _(dve):
            chain = Chain(dve, dchain)
            v = nc.vector
            chain.link(v.tensor_tensor(m.branchT[:, :], m.branchT[:, :], m.xa[:, 1:1 + N], ALU.add))
            for c in range(NCH):
                dve.wait_ge(x_ps, T4 * (c + 1))
                tiles = slice(T4 * c, T4 * (c + 1))
                last = v.tensor_tensor(m.x[:, tiles, :], m.x[:, tiles, :],
                                       psX[:, c, :].rearrange("p (t f) -> p t f", f=D), ALU.add)
            chain.link(last)
            norm_statistics(nc, dve, chain.link, m.x, stats, mv, NT)
            v.tensor_scalar(eps_sum[:, :], mv[:, :, 1], LN_EPS, None, ALU.add).then_inc(stat_done, 1)
            dve.wait_ge(pow_done, 1)
            for t in range(NT):
                last = v.tensor_scalar(xn[:, t, :], m.x[:, t, :], mv[:, t, 0:1], rstd[:, t:t + 1],
                                       ALU.subtract, ALU.mult)
            last.then_inc(xn_ready, 1)
            dve.wait_ge(xn_ready, 1)
            chain.link(v.tensor_tensor(xr[:, :, :], xn[:, :, :], xn[:, :, :], ALU.mult))
            chain.link(v.tensor_reduce(ms[:, :], xr[:, :, :], AX.X, ALU.add))
            v.tensor_scalar(eps_sum[:, :], ms[:, :], 1.0 / D, RMS_EPS, ALU.mult, ALU.add).then_inc(stat_done, 1)
            dve.wait_ge(pow_done, 2)
            v.tensor_tensor(xr[:, :, :], xn[:, :, :], spread(rrms[:, :], 2, D), ALU.mult).then_inc(xn_ready, 1)

            def ranks(x, n):
                beats = above[:, 0:NT * n * n].rearrange("p (t i j) -> p t i j", i=n, j=n)
                for i in range(n):
                    if i > 0:
                        v.tensor_tensor(beats[:, :, i, 0:i], x[:, :, 0:i], x[:, :, i:i + 1].broadcast_to([P, NT, i]),
                                        ALU.is_ge)
                    last = v.tensor_tensor(beats[:, :, i, i:n], x[:, :, i:n],
                                           x[:, :, i:i + 1].broadcast_to([P, NT, n - i]), ALU.is_gt)
                chain.link(last)
                chain.link(v.tensor_reduce(rank[:, 0:NT * n].rearrange("p (t i) -> p t i", i=n), beats, AX.X, ALU.add))

            dve.wait_ge(in_, 48)
            dve.wait_ge(score_done, 1)
            chain.link(v.tensor_tensor(s[:, :, :], score[:, :, :], spread(bias[:, :], 1, NT), ALU.add))
            by_pair = s[:, :, :].rearrange("p t (g c a) -> p (t g) c a", g=GROUPS, a=2)
            v.tensor_tensor(pair_max[:, :, :], by_pair[:, :, :, 0], by_pair[:, :, :, 1], ALU.max)
            chain.link(v.tensor_tensor(pair_min[:, :, :], by_pair[:, :, :, 0], by_pair[:, :, :, 1], ALU.min))
            v.tensor_tensor(top[:, :], pair_max[:, :, 0], pair_max[:, :, 1], ALU.max)
            v.tensor_tensor(second[:, :], pair_max[:, :, 0], pair_max[:, :, 1], ALU.min)
            chain.link(v.tensor_tensor(pair_min[:, :, 0], pair_min[:, :, 0], pair_min[:, :, 1], ALU.max))
            chain.link(v.tensor_tensor(second[:, :], second[:, :], pair_min[:, :, 0], ALU.max))
            chain.link(v.tensor_tensor(gscore[:, :, :].rearrange("p t g -> p (t g)"), top[:, :], second[:, :], ALU.add))
            ranks(gscore[:, :, :], GROUPS)
            rank_g = rank[:, 0:NT * GROUPS].rearrange("p (t i) -> p t i", i=GROUPS)
            chain.link(v.tensor_scalar(gsel[:, :, :], rank_g, float(TOP_GROUPS), None, ALU.is_lt))
            chain.link(v.tensor_scalar(gout[:, :, :], gsel[:, :, :], -1.0, None, ALU.add))
            by_group = masked[:, :, :].rearrange("p t (g c) -> p (t g) c", g=GROUPS)
            flat = gsel[:, :, :].rearrange("p t g -> p (t g)"), gout[:, :, :].rearrange("p t g -> p (t g)")
            chain.link(v.tensor_tensor(by_group, s[:, :, :].rearrange("p t (g c) -> p (t g) c", g=GROUPS),
                                       spread(flat[0], 2, E // GROUPS), ALU.mult))
            chain.link(v.tensor_tensor(by_group, by_group, spread(flat[1], 2, E // GROUPS), ALU.add))
            ranks(masked[:, :, :], E)
            chain.link(v.tensor_scalar(masked[:, :, :], rank[:, :].rearrange("p (t i) -> p t i", i=E), float(TOP_K),
                                       None, ALU.is_lt))
            chain.link(v.tensor_tensor(masked[:, :, :], masked[:, :, :], score[:, :, :], ALU.mult))
            chain.link(v.tensor_reduce(wsum[:, :], masked[:, :, :], AX.X, ALU.add))
            chain.link(v.tensor_scalar(wsum[:, :], wsum[:, :], 1e-20, None, ALU.add))
            chain.link(v.reciprocal(wsum[:, :], wsum[:, :]))
            chain.link(v.tensor_scalar(wsum[:, :], wsum[:, :], ROUTE_SCALE, None, ALU.mult))
            v.tensor_tensor(m.combine[:, 0:E, :].rearrange("p e t -> p t e"), masked[:, :, :],
                            spread(wsum[:, :], 2, E), ALU.mult)
            v.memset(m.combine[:, E:NE, :], 1.0)


def capped_attention(nc, m, d):
    TB = S // P
    NS = B * TB * 2
    NJ = NS // 2
    with ExitStack() as ctx:
        sb, ps, sem = tensors(ctx, nc, "c_")
        gamma = sb("gamma", [P, PAIRS + 1, 4])
        factor = sb("factor", [P, PAIRS + 1, 4])
        fac = sb("fac", [P, 4])
        w = sb("w", [P, 3 * P])
        wo = sb("wo", [P, D])
        raw = sb("raw", [P, NT, 3 * P])
        sq = sb("sq", [P, 4, 2 * P])
        hat = sb("hat", [P, 4, 4, 2, DH])
        ss = sb("ss", [P, NT, 4])
        rn = sb("rn", [P, NT, 4])
        Q = sb("Q", [P, 2, N], F32R)
        K_hi = sb("K_hi", [P, 2, N], F32R)
        K_lo = sb("K_lo", [P, 2, N], F32R)
        th = sb("th", [P, 4, S])
        prob = sb("prob", [P, 4, S])
        tables = m.rot[:, :, :, :].rearrange("p n a f -> p (n a f)")
        acc = [a.rearrange("p (e q) -> p e q", e=2) for a in (tables[:, 0:2 * S], m.branchT[:, :])]
        rec = tables[:, 2 * S:3 * S].rearrange("p (c q) -> p c q", c=2)
        OT = tables[:, 3 * S:4 * S]
        psS = ps("psS", [P, 2, S])
        psO = ps("psO", [P, S])
        psL = ps("psL", [P, BANK])
        psW = ps("psW", [P, BANK])
        names = ("g_in w_in wo_in proj_ps raw_ready ss_done rn_done hat_done h_ps hi_done lo_done st_ps tanh_done "
                 "exp_done acc_done pv_ps sum_ps rec_done ot_ready wo_ps add_done dchain factor_done").split()
        (g_in, w_in, wo_in, proj_ps, raw_ready, ss_done, rn_done, hat_done, h_ps, hi_done, lo_done, st_ps, tanh_done,
         exp_done, acc_done, pv_ps, sum_ps, rec_done, ot_ready, wo_ps, add_done, dchain, factor_done) = sems = \
            [sem(name) for name in names]
        start_semaphores(nc, "c", sems)
        block = ctx.enter_context(nc.Block())

        def prepared(g, b):
            return 2 * g + 1 + b, (1 - b) * TB

        EARLY = {2: [0, 1], 3: [4, 5]}
        LATE = {2: [2, 3], 3: [6, 7]}
        TURNS = [(0, 0), (0, 1), (1, 0), (1, 1)]
        SHIFT = 2

        @block.sync
        def _(sp):
            sp.dma_start(gamma[:, :, :], d["c_gamma"].rearrange("a p x -> p a x")).then_inc(g_in, 16)
            sp.dma_start(w[:, :], d["c_wqkv"][0].rearrange("d x f -> d (x f)")).then_inc(w_in, 16)
            with sp.Fori(0, PAIRS) as g:
                sp.wait_ge(wo_ps, START + g * 2 * B)
                sp.dma_start(wo[:, :], d["c_wo"][bass.ds(g, 1)].rearrange("g f d -> (g f) d")).then_inc(wo_in, 16)
                sp.wait_ge(proj_ps, START + (g + 1) * NT)
                sp.dma_start(w[:, :], d["c_wqkv"][bass.ds(g + 1, 1)].rearrange("g d x f -> (g d) (x f)"))\
                    .then_inc(w_in, 16)
            sp.wait_ge(g_in, START + 16)
            sp.wait_ge(w_in, START + (PAIRS + 1) * 16)
            sp.wait_ge(wo_in, START + PAIRS * 16)

        @block.tensor
        def _(pe):
            def scores(g, s):
                b, kt, e = s % NS // (2 * TB), s // 2 % TB, s % 2
                if s % (2 * TB) == 0:
                    half = 2 * g + s // (2 * TB)
                    pe.wait_ge(lo_done, START + 8 * half + 6)
                pe.wait_ge(tanh_done, START + g * NS + s - 1)
                keys = slice(b * S + kt * P, b * S + (kt + 1) * P)
                for K in (K_hi, K_lo):
                    for c in range(2):
                        last = nc.tensor.matmul(psS[:, e, c * BANK:(c + 1) * BANK], K[:, e, keys],
                                                Q[:, e, b * S + c * BANK:b * S + (c + 1) * BANK],
                                                start=K is K_hi, stop=K is K_lo)
                last.then_inc(st_ps, 1)

            def values(g, j):
                b, kt = j // TB % B, j % TB
                pe.wait_ge(exp_done, START + g * NS + 2 * j + 2)
                if kt == 0:
                    pe.wait_ge(ot_ready, START + g * 2 * B + 2 * (j // TB))
                for c in range(2):
                    for e in range(2):
                        last = nc.tensor.matmul(psO[64 * e:64 * e + 64, c * BANK:(c + 1) * BANK],
                                                raw[:, b * TB + kt, 2 * P + 64 * e:2 * P + 64 * e + 64],
                                                prob[:, (2 * j + e) % 4, c * BANK:(c + 1) * BANK],
                                                start=kt == 0, stop=kt == TB - 1)
                last.then_inc(pv_ps, 1)

            def sums(g, b):
                half, _ = prepared(g, b)
                pe.wait_ge(lo_done, START + 8 * half + 8)
                pe.wait_ge(acc_done, START + g * NS + (b + 1) * 2 * TB)
                for c, out in enumerate((psL, psW)):
                    for e in range(2):
                        last = nc.tensor.matmul(out[64 * e:64 * e + 64, :], m.ones[:, 0:64],
                                                acc[b][:, e, c * BANK:(c + 1) * BANK], start=True, stop=True)
                    last.then_inc(sum_ps, 1)

            def project_out(g, b):
                if b == 0:
                    pe.wait_ge(wo_in, START + (g + 1) * 16)
                for c, out in enumerate((psL, psW)):
                    pe.wait_ge(ot_ready, START + g * 2 * B + 2 * b + c + 1)
                    for t in range(4):
                        last = nc.tensor.matmul(out[:, t * P:(t + 1) * P], OT[:, (4 * c + t) * P:(4 * c + t + 1) * P],
                                                wo[:, :], start=True, stop=True)
                    last.then_inc(wo_ps, 1)

            def project_in(g, b, t):
                half, first = prepared(g, b)
                if t == 0:
                    pe.wait_ge(lo_done, START + 8 * half)
                    pe.wait_ge(add_done, START + 2 * (half - 1))
                    if b == 1:
                        pe.wait_ge(w_in, START + (g + 2) * 16)
                if t >= 2:
                    pe.wait_ge(raw_ready, START + TB * half + t - 1)
                nc.tensor.matmul((psW, psL)[t % 2][:, 0:3 * P], m.xrT[:, (first + t) * P:(first + t + 1) * P], w[:, :],
                                 start=True, stop=True).then_inc(proj_ps, 1)

            def transposes(g, b, n):
                half, first = prepared(g, b)
                i, x = TURNS[n]
                pe.wait_ge(hat_done, START + 4 * half + 2 * i + 2)
                if n == 0:
                    pe.wait_ge(raw_ready, START + TB * (half + 1))
                for e, out in enumerate((psW, psL)):
                    if n >= 1:
                        pe.wait_ge(lo_done, START + 8 * half + 2 * n - 1 + e)
                    for t in range(4):
                        head = hat[:, t, 2 * x + e, :, :].rearrange("p c f -> p (c f)")
                        last = nc.tensor.transpose(out[:, t * P:(t + 1) * P], head, m.ident[:, :])
                    last.then_inc(h_ps, 1)

            for t in range(TB):
                project_in(-1, 1, t)
            for n in range(4):
                transposes(-1, 1, n)
            scores(0, 0)
            scores(0, 1)

            def key_tile(g, j, start):
                b, kt = j // TB, j % TB
                scores(g, 2 * j + 2)
                for t in EARLY.get(kt, []):
                    project_in(g, b, t)
                if kt in (5, 6):
                    transposes(g, b, 2 * kt - 10)
                if kt == 0 and j > 0:
                    sums(g, b - 1)
                if kt != 1 and j > 0:
                    values(g, j - 1)
                scores(g, 2 * j + 3)
                if kt == 1:
                    values(g, j - 1)
                    if not start:
                        project_out(g, b - 1)
                for t in LATE.get(kt, []):
                    project_in(g, b, t)
                if kt in (5, 6):
                    transposes(g, b, 2 * kt - 9)

            for j in range(SHIFT):
                key_tile(0, j, True)
            with pe.Fori(0, PAIRS) as g:
                for j in range(SHIFT, NJ + SHIFT):
                    key_tile(g, j, False)
            for c in range(2):
                for e in range(2):
                    nc.tensor.matmul(psO[64 * e:64 * e + 64, c * BANK:(c + 1) * BANK], m.identb[:, 0:64],
                                     m.band[:, 0:BANK // (2 * WIN), :], start=False, stop=True)

        @block.scalar
        def _(act):
            def tanh(g, s):
                act.wait_ge(st_ps, START + g * NS + s + 1)
                act.wait_ge(exp_done, START + g * NS + s - 3)
                nc.scalar.activation(th[:, s % 4, :], psS[:, s % 2, :], ACT.Tanh, scale=1.0 / SOFTCLAMP)\
                    .then_inc(tanh_done, 1)

            def exponential(g, s):
                act.wait_ge(tanh_done, START + g * NS + s + 1)
                act.wait_ge(pv_ps, START + g * NJ + (s - 4) // 2 + 1)
                act.wait_ge(acc_done, START + g * NS + s - 3)
                nc.scalar.activation(prob[:, s % 4, :], th[:, s % 4, :], ACT.Exp,
                                     scale=SOFTCLAMP * DH ** -0.5).then_inc(exp_done, 1)

            def raw_out(g, b, t):
                half, first = prepared(g, b)
                act.wait_ge(proj_ps, START + TB * half + t + 1)
                nc.scalar.activation(raw[:, first + t, :], (psW, psL)[t % 2][:, 0:3 * P], ACT.Copy)\
                    .then_inc(raw_ready, 1)

            def split_hi(g, b, n):
                half, first = prepared(g, b)
                i, x = TURNS[n]
                if n == 0 and b == 1:
                    act.wait_ge(factor_done, START + g + 3)
                tokens = slice((first + 4 * i) * P, (first + 4 * i + 4) * P)
                for e in range(2):
                    act.wait_ge(h_ps, START + 8 * half + 2 * n + e + 1)
                    nc.scalar.activation((Q, K_hi)[x][:, e, tokens], (psW, psL)[e][:, :], ACT.Copy,
                                         scale=fac[:, 2 * x + e:2 * x + e + 1]).then_inc(hi_done, 1)

            for t in range(TB):
                raw_out(-1, 1, t)
            for n in range(4):
                split_hi(-1, 1, n)
            tanh(0, 0)
            tanh(0, 1)
            exponential(0, 0)

            def key_tile(g, j):
                b, kt = j // TB, j % TB
                if kt in (6, 7):
                    split_hi(g, b, 2 * kt - 11)
                tanh(g, 2 * j + 2)
                exponential(g, 2 * j + 1)
                for t in EARLY.get(kt, []):
                    raw_out(g, b, t)
                if kt in (5, 6):
                    split_hi(g, b, 2 * kt - 10)
                tanh(g, 2 * j + 3)
                exponential(g, 2 * j + 2)
                for t in LATE.get(kt, []):
                    raw_out(g, b, t)

            for j in range(SHIFT):
                key_tile(0, j)
            with act.Fori(0, PAIRS) as g:
                for j in range(SHIFT, NJ + SHIFT):
                    key_tile(g, j)

        @block.gpsimd
        def _(pool):
            def norms(g, b, i):
                half, first = prepared(g, b)
                pool.wait_ge(ss_done, START + 2 * half + i + 1)
                tiles = slice(first + 4 * i, first + 4 * i + 4)
                nc.gpsimd.tensor_tensor(rn[:, tiles, :], ss[:, tiles, :],
                                        m.minus_half[:, 0:16].rearrange("p (t h) -> p t h", h=4), ALU.pow)\
                    .then_inc(rn_done, 1)
                pool.wait_ge(rn_done, START + 2 * half + i + 1)
                pool.wait_ge(h_ps, START + 8 * half + 4 * i)
                for c in range(2):
                    nc.gpsimd.tensor_tensor(hat[:, :, :, c, :],
                                            raw[:, tiles, 0:2 * P].rearrange("p t (h f) -> p t h f", f=DH),
                                            spread(rn[:, tiles, :], 3, DH), ALU.mult).then_inc(hat_done, 1)

            for i in range(2):
                norms(-1, 1, i)
            with pool.Fori(0, PAIRS) as g:
                for b in range(B):
                    for i in range(2):
                        norms(g, b, i)

        @block.vector
        def _(dve):
            v = nc.vector

            def squares(g, b, i):
                half, first = prepared(g, b)
                chain = Chain(dve, dchain, START + 4 * half + 2 * i)
                tiles = slice(first + 4 * i, first + 4 * i + 4)
                dve.wait_ge(raw_ready, START + TB * half + 4 * i + 4)
                qk = raw[:, tiles, 0:2 * P]
                chain.link(v.tensor_tensor(sq[:, :, :], qk, qk, ALU.mult))
                chain.link(v.tensor_reduce(ss[:, tiles, :], sq[:, :, :].rearrange("p t (h f) -> p t h f", f=DH),
                                           AX.X, ALU.add))
                v.tensor_scalar(ss[:, tiles, :], ss[:, tiles, :], 1e-24, None, ALU.max).then_inc(ss_done, 1)

            def factors(g):
                dve.wait_ge(hi_done, START + 16 * (g + 1))
                v.tensor_copy(fac[:, :], factor[:, bass.ds(g + 1, 1), :].rearrange("p g x -> p (g x)"))\
                    .then_inc(factor_done, 1)

            def split_lo(g, b, n):
                half, first = prepared(g, b)
                i, x = TURNS[n]
                tokens = slice((first + 4 * i) * P, (first + 4 * i + 4) * P)
                for e in range(2):
                    rows = slice(64 if x == 0 else 0, P)
                    dve.wait_ge(hi_done, START + 8 * half + 2 * n + e + 1)
                    v.scalar_tensor_tensor(out=(Q, K_lo)[x][rows, e, tokens], in0=(psW, psL)[e][rows, :],
                                           scalar=fac[rows, 2 * x + e:2 * x + e + 1],
                                           in1=(Q, K_hi)[x][rows, e, tokens], op0=ALU.mult, op1=ALU.subtract)\
                        .then_inc(lo_done, 1)

            def accumulate(g, s):
                kt, e = s // 2 % TB, s % 2
                dve.wait_ge(exp_done, START + g * NS + s + 1)
                a = acc[s // (2 * TB) % B]
                if kt == 0:
                    dve.wait_ge(sum_ps, START + g * 2 * B + s // (2 * TB) * 2 - 2)
                    v.tensor_copy(a[:, e, :], prob[:, s % 4, :]).then_inc(acc_done, 1)
                else:
                    dve.wait_ge(acc_done, START + g * NS + s - 1)
                    v.tensor_tensor(a[:, e, :], a[:, e, :], prob[:, s % 4, :], ALU.add).then_inc(acc_done, 1)

            def reciprocals(g, b):
                for c, sums in enumerate((psL, psW)):
                    dve.wait_ge(sum_ps, START + g * 2 * B + 2 * b + c + 1)
                    v.reciprocal(rec[:, c, :], sums[:, :]).then_inc(rec_done, 1)

            def divide(g, b):
                first = START + g * 2 * B + 2 * b
                dve.wait_ge(wo_ps, first)
                dve.wait_ge(pv_ps, START + g * NJ + (b + 1) * TB)
                for c in range(2):
                    dve.wait_ge(rec_done, first + c + 1)
                    v.tensor_tensor(OT[:, c * BANK:(c + 1) * BANK], psO[:, c * BANK:(c + 1) * BANK],
                                    rec[:, c, :], ALU.mult).then_inc(ot_ready, 1)

            def add_out(g, b):
                for c, out in enumerate((psL, psW)):
                    dve.wait_ge(wo_ps, START + g * 2 * B + 2 * b + c + 1)
                    tiles = slice(b * TB + 4 * c, b * TB + 4 * c + 4)
                    v.tensor_tensor(m.x[:, tiles, :], m.x[:, tiles, :],
                                    out[:, :].rearrange("p (t f) -> p t f", f=D), ALU.add).then_inc(add_done, 1)

            dve.wait_ge(g_in, START + 16)
            v.tensor_scalar(factor[:, :, :], gamma[:, :, :], 1.0, DH ** 0.5, ALU.add, ALU.mult).then_inc(factor_done, 1)
            dve.wait_ge(factor_done, START + 1)
            v.tensor_copy(fac[:, :], factor[:, 0, :]).then_inc(factor_done, 1)
            for i in range(2):
                squares(-1, 1, i)
            for n in range(4):
                split_lo(-1, 1, n)
            accumulate(0, 0)

            def key_tile(g, j, start):
                b, kt = j // TB, j % TB
                if kt == 3:
                    squares(g, b, 0)
                if kt == 4:
                    squares(g, b, 1)
                if kt in (6, 7):
                    split_lo(g, b, 2 * kt - 11)
                if kt == 0 and j > 0:
                    reciprocals(g, b - 1)
                accumulate(g, 2 * j + 1)
                if kt in (5, 6):
                    split_lo(g, b, 2 * kt - 10)
                if kt == 0 and j > 0:
                    divide(g, b - 1)
                accumulate(g, 2 * j + 2)
                if kt == 1 and not start:
                    add_out(g, b - 1)
                if j == TB:
                    factors(g)

            for j in range(SHIFT):
                key_tile(0, j, True)
            with dve.Fori(0, PAIRS) as g:
                for j in range(SHIFT, NJ + SHIFT):
                    key_tile(g, j, False)


def experts(nc, m, d, out):
    with ExitStack() as ctx:
        sb, ps, sem = tensors(ctx, nc, "e_")
        x_hi = sb("x_hi", [D, N], F32R)
        x_lo = sb("x_lo", [D, N], F32R)
        w_gu = sb("w_gu", [D, 2, 2, F])
        w_hi = sb("w_hi", [D, 2, 2, F], F32R)
        w_lo = sb("w_lo", [D, 2, 2, F], F32R)
        w_down = sb("w_down", [F, 2, D])
        weight = sb("weight", [P, 2, NT])
        sg = sb("sg", [F, 2, CH])
        hT = sb("hT", [F, 2, CH])
        psG = ps("psG", [P, 2, BANK])
        psU = ps("psU", [P, 2, BANK])
        psY = ps("psY", [P, 2, BANK])
        names = "w_in_even w_in_odd x_upper x_split w_upper w_split gu_ps silu_done h_done y_ps y_done weight_done out_done".split()
        (w_in_even, w_in_odd, x_upper, x_split, w_upper, w_split, gu_ps, silu_done, h_done, y_ps, y_done, weight_done,
         out_done) = sems = [sem(name) for name in names]
        start_semaphores(nc, "e", sems)
        w_in = (w_in_even, w_in_odd)
        block = ctx.enter_context(nc.Block())
        PER = 2 * NCH

        @block.sync
        def _(sp):
            def load(i, u):
                e = 2 * i + u
                sp.dma_start(w_gu[:, u, :, :], d["e_gate_up"][bass.ds(e, 1)].rearrange("e d x f -> (e d) x f"))\
                    .then_inc(w_in[u], 16)
                sp.dma_start(w_down[:, u, :], d["e_down"][bass.ds(e, 1)].rearrange("e f d -> (e f) d"))\
                    .then_inc(w_in[u], 16)
            load(0, 0)
            load(0, 1)
            with sp.Fori(1, NE // 2) as i:
                for u in range(2):
                    sp.wait_ge(y_ps, START + PER * i + NCH * (u - 1))
                    load(i, u)
            rows = out.rearrange("(t p) d -> p t d", p=P)
            for c in range(NCH):
                sp.wait_ge(y_done, START + (NE - 1) * NCH + c + 1)
                sp.dma_start(rows[:, 4 * c:4 * c + 4, :], m.x[:, 4 * c:4 * c + 4, :]).then_inc(out_done, 16)
            sp.wait_ge(out_done, START + NCH * 16)

        @block.tensor
        def _(pe):
            def gate_up(i, c):
                u = c // NCH
                if c % NCH == 0:
                    pe.wait_ge(w_in[u], START + (i + 1) * 32)
                    pe.wait_ge(w_split, START + 2 * i + u + 1)
                pe.wait_ge(x_split, START + c % NCH + 1)
                if c >= 2:
                    pe.wait_ge(h_done, START + PER * i + c - 1)
                for x, dst in enumerate((psG, psU)):
                    tokens = slice((c % NCH) * CH, (c % NCH + 1) * CH)
                    last = split_product(nc, dst[:, c % 2, :], w_hi[:, u, x, :], w_lo[:, u, x, :],
                                         x_hi[:, tokens], x_lo[:, tokens])
                last.then_inc(gu_ps, 1)

            def down(i, c):
                pe.wait_ge(h_done, START + PER * i + c + 1)
                pe.wait_ge(y_done, START + PER * i + max(0, c - 1))
                for t in range(4):
                    last = nc.tensor.matmul(psY[:, c % 2, t * P:(t + 1) * P], hT[:, c % 2, t * P:(t + 1) * P],
                                            w_down[:, c // NCH, :], start=True, stop=True)
                last.then_inc(y_ps, 1)

            with pe.Fori(0, NE // 2) as i:
                for c in range(PER):
                    gate_up(i, c)
                    if c >= 1:
                        down(i, c - 1)
                down(i, PER - 1)

        @block.scalar
        def _(act):
            def upper_weights(e, u):
                act.wait_ge(w_in[u], START + (e - u) * 16 + 32)
                if not (isinstance(e, int) and e == 0):
                    act.wait_ge(gu_ps, START + NCH * (e - 1))
                nc.scalar.activation(w_hi[:, u, :, :], w_gu[:, u, :, :], ACT.Copy).then_inc(w_upper, 1)

            def two_experts(i, last):
                for c in range(PER):
                    act.wait_ge(gu_ps, START + PER * i + c + 1)
                    nc.scalar.activation(sg[:, c % 2, :], psG[:, c % 2, :], ACT.Silu).then_inc(silu_done, 1)
                    if c == 1:
                        upper_weights(2 * i + 1, 1)
                    if c == NCH + 1 and not last:
                        upper_weights(2 * i + 2, 0)

            upper_weights(0, 0)
            for c in range(NCH):
                tokens = slice(c * CH, (c + 1) * CH)
                nc.scalar.activation(x_hi[:, tokens], m.xnT[:, tokens], ACT.Copy).then_inc(x_upper, 1)
            with act.Fori(0, NE // 2 - 1) as i:
                two_experts(i, False)
            two_experts(NE // 2 - 1, True)

        @block.gpsimd
        def _(pool):
            def lower_weights(e, u):
                pool.wait_ge(w_upper, START + e + 1)
                nc.gpsimd.tensor_tensor(w_lo[:, u, :, :], w_gu[:, u, :, :], w_hi[:, u, :, :], ALU.subtract)\
                    .then_inc(w_split, 1)

            with pool.Fori(0, NE // 2) as i:
                for u in range(2):
                    lower_weights(2 * i + u, u)

        @block.vector
        def _(dve):
            v = nc.vector

            def add(i, c):
                dve.wait_ge(y_ps, START + PER * i + c + 1)
                for t in range(4):
                    tile = (c % NCH) * 4 + t
                    last = v.scalar_tensor_tensor(out=m.x[:, tile, :], in0=psY[:, c % 2, t * P:(t + 1) * P],
                                                  scalar=weight[:, c // NCH, tile:tile + 1], in1=m.x[:, tile, :],
                                                  op0=ALU.mult, op1=ALU.add)
                last.then_inc(y_done, 1)

            for c in range(NCH):
                tokens = slice(c * CH, (c + 1) * CH)
                dve.wait_ge(x_upper, START + c + 1)
                v.tensor_tensor(x_lo[:, tokens], m.xnT[:, tokens], x_hi[:, tokens], ALU.subtract).then_inc(x_split, 1)
            with dve.Fori(0, NE // 2) as i:
                dve.wait_ge(y_done, START + PER * i)
                for u in range(2):
                    v.tensor_copy(weight[:, u, :], m.combine[:, bass.ds(2 * i + u, 1), :].rearrange("p e t -> p (e t)"))\
                        .then_inc(weight_done, 1)
                dve.wait_ge(weight_done, START + 2 * i + 2)
                for c in range(PER):
                    dve.wait_ge(silu_done, START + PER * i + c + 1)
                    if c >= 2:
                        dve.wait_ge(y_ps, START + PER * i + c - 1)
                    v.tensor_tensor(hT[:, c % 2, :], psU[:, c % 2, :], sg[:, c % 2, :], ALU.mult).then_inc(h_done, 1)
                    if c >= 1:
                        add(i, c - 1)
                add(i, PER - 1)


def persistent(ctx, nc):
    sb, _, _ = tensors(ctx, nc, "")
    m = Memory()
    m.x = sb("x", [P, NT, D])
    m.xnT = sb("xnT", [P, N])
    m.xa = sb("xaT", [P, 1 + N + P])
    m.xb = sb("xbT", [P, 1 + N])
    m.branchT = sb("branchT", [P, N])
    m.ident = sb("ident", [P, P])
    m.identb = sb("identb", [P, P], BF16)
    m.causal = sb("causal", [P, P], BF16)
    m.band = sb("band", [P, NT, 2 * WIN], BF16)
    m.keep = sb("keep", [P, NT + 1])
    m.ones = sb("ones", [P, P])
    m.minus_half = sb("minus_half", [P, 4 * NT])
    m.rot_base = sb("rot_base", [P, S // P, 4, DH])
    m.rot_scale = sb("rot_scale", [P, 4, DH])
    m.rot = sb("rot", [P, NT, 4, DH])
    m.xrT = m.xb[:, 1:]
    m.combine = sb("combine", [P, NE, NT])
    return m


def shape_constants():
    i, j = np.arange(P)[:, None], np.arange(P)[None, :]
    c = {"ident": np.eye(P, dtype=np.float32), 
         "causal": np.where(j > i, NEG, 0.0).astype(np.float32)}
    q, k = np.arange(P)[:, None] % WIN, np.arange(2 * WIN)[None, :]
    band = np.where((k >= q) & (k <= q + WIN), 0.0, NEG)
    band = np.repeat(band[:, None, :], NT, axis=1)
    for t in range(0, NT, S // P):
        band[0:WIN, t, 0:WIN] = NEG
    c["band"] = band.astype(np.float32)
    keep = np.ones((NT + 1,), np.float32)
    keep[::S // P] = 0.0
    c["keep"] = keep
    half = np.arange(0, DH, 2, dtype=np.float32)
    inv_freq = (1.0 / np.float32(10000.0) ** (half / np.float32(DH))).astype(np.float32)
    t = np.arange(S, dtype=np.float32)
    freqs = (t[:, None] * inv_freq[None, :]).astype(np.float32).astype(np.float64)
    base = ((half + np.float32(0.4 * DH)) / np.float32(1.4 * DH)).astype(np.float32)
    power = ((t - S // 2) / np.float32(WIN // 2)).astype(np.float32)
    scale = base[None, :].astype(np.float64) ** power[:, None]
    cos, sin = np.cos(freqs), np.sin(freqs)
    sign = np.array([-1.0, 1.0])[None, :, None]

    def both(a):
        return np.repeat(a[:, None, :], 2, axis=1)

    tabs = [both(cos * scale), both(sin * scale) * sign, both(cos / scale), both(sin / scale) * sign]
    tabs = np.stack([a.reshape(S, DH) for a in tabs], axis=1).astype(np.float32)
    c["rot_base"] = np.ascontiguousarray(tabs.reshape(S // P, P, 4, DH).transpose(1, 0, 2, 3))
    return c


def laid_out(i):
    f = {k: np.asarray(v) for k, v in i.items()}

    def pairs(w):
        return w.reshape(D, PAIRS, P).transpose(1, 0, 2)

    a = {"x": f["L0_attn_x"].reshape(N, D)}
    qkv = [f[f"L0_attn_w{n}"].reshape(PAIRS, P, D).transpose(0, 2, 1) for n in "qkv"]
    a["a_wqkv"] = np.stack(qkv, axis=2)
    a["a_wo"] = f["L0_attn_wo"].reshape(D, PAIRS, P).transpose(1, 2, 0)

    def again(w):
        return np.concatenate([w, w[:1]])

    def swapped(s):
        return np.concatenate([s[:, DH // 2:], s[:, :DH // 2]], axis=1)

    qs, ks = f["L0_ffn_q_scale"], f["L0_ffn_k_scale"]
    a["rot_scale"] = again(np.stack([qs, swapped(qs), ks, swapped(ks)], axis=1))
    w = f["L0_ffn_Wqkv"].reshape(LAYERS, D, 3, PAIRS, 2, DH).transpose(0, 1, 2, 4, 3, 5)
    a["b_wqkv"] = again(w.reshape(LAYERS, D, 3 * H * DH))
    a["b_wo"] = again(f["L0_ffn_Wo"].reshape(LAYERS, PAIRS, P, D).transpose(0, 2, 1, 3))
    a["b_w1"] = f["L0_ffn_W1"]
    pad = NF * P - FFN_IN
    a["b_w2"] = np.pad(f["L0_ffn_W2"], ((0, 0), (0, pad), (0, 0))).reshape(LAYERS, NF, P, D).transpose(0, 2, 1, 3)
    b1 = np.pad(f["L0_ffn_b1"].reshape(LAYERS, 2, FFN_IN), ((0, 0), (0, 0), (0, pad))).reshape(LAYERS, 2 * NF, P)
    a["b_cols"] = np.concatenate([f["L0_ffn_ln_g"][:, None], f["L0_ffn_ln_b"][:, None], f["L0_ffn_b2"][:, None], b1],
                                 axis=1).transpose(0, 2, 1)
    q, (k, v) = f["L1_attn_Wq"], np.split(f["L1_attn_Wkv"], 2, axis=1)
    a["c_wqkv"] = again(np.stack([pairs(q), pairs(k), pairs(v)], axis=2))
    a["c_wo"] = f["L1_attn_Wo"].reshape(PAIRS, P, D)
    a["c_norm_w"] = f["L1_attn_norm_w"].reshape(D, 1)
    gamma = np.stack([f["L1_attn_q_gamma"].reshape(PAIRS, 2, DH), f["L1_attn_k_gamma"].reshape(PAIRS, 2, DH)], axis=1)
    a["c_gamma"] = again(np.tile(gamma.reshape(PAIRS, 4, DH).transpose(0, 2, 1), (1, 2, 1)))
    a["router_w"] = f["L1_ffn_router_w"].T
    a["router_bias"] = f["L1_ffn_bias"]

    def halves(w):
        return w.reshape(D, 2, F).transpose(1, 0, 2)

    a["e_gate_up"] = np.stack([np.concatenate([f["L1_ffn_gate_w"], halves(f["L1_ffn_sh_gate_w"])]),
                               np.concatenate([f["L1_ffn_up_w"], halves(f["L1_ffn_sh_up_w"])])], axis=2)
    a["e_down"] = np.concatenate([f["L1_ffn_down_w"], f["L1_ffn_sh_down_w"].reshape(2, F, D)])
    a.update(shape_constants())
    return {k: np.ascontiguousarray(v) for k, v in a.items()}


def build(nc, d, out):
    with ExitStack() as ctx:
        m = persistent(ctx, nc)
        load_and_norm(nc, m, d)
        causal_attention(nc, m, d)
        windowed_layers(nc, m, d)
        second_norm(nc, m, d)
        capped_attention(nc, m, d)
        experts(nc, m, d, out)


def kernel(**inputs):
    import concourse.bacc as bacc
    from concourse.bass_utils import run_bass_kernel_spmd

    nc = bacc.Bacc("TRN2", target_bir_lowering=False, num_devices=1)
    arrays = {f"in_{k}": v for k, v in laid_out(inputs).items()}
    d = {k[3:]: nc.dram_tensor(k, v.shape, mybir.dt.from_np(v.dtype), kind="ExternalInput").ap()
         for k, v in arrays.items()}
    out = nc.dram_tensor("out", (N, D), F32, kind="ExternalOutput").ap()
    build(nc, d, out)
    r = run_bass_kernel_spmd(nc, [arrays], core_ids=[0])
    return r.results[0]["out"].reshape(B, S, D)
```
